# Optimizing a Trainium2 kernel written in Bass

```python
import numpy as np
import jax
import jax.numpy as jnp

def _softmax(x, axis=-1):
    return jax.nn.softmax(x, axis=axis)

def _gelu(x):
    return jax.nn.gelu(x, approximate=True)

def _silu(x):
    return jax.nn.silu(x)

def _sigmoid(x):
    return jax.nn.sigmoid(x)

def _layernorm(x, axis=-1, eps=1e-05):
    m = jnp.mean(x, axis=axis, keepdims=True)
    v = jnp.var(x, axis=axis, keepdims=True)
    return (x - m) / jnp.sqrt(v + eps)

def _scatter_add(tgt, idx, src, axis=0):
    return tgt.at[idx].add(src)

def _segment_sum(src, seg, n):
    return jax.ops.segment_sum(src, seg, n)
kernel_name = 'mk_decoder_postln_d1_seqx_r8_a6f1b9'

def setup_inputs(seed: int=0):
    np.random.seed(seed)
    _w = jnp.asarray

    def _rec_inputs():
        import jax
        import jax.numpy as jnp
        _rk = jax.random.key(seed)
        x = -0.0002928 + 1 * jax.random.normal(jax.random.fold_in(_rk, 1), (4, 256, 512), jnp.float32)
        _lenS = 256 - jax.random.randint(jax.random.fold_in(_rk, 7), (4,), 0, max(1, 256 // 4) + 1, jnp.int32)
        _lenS2 = 64 - jax.random.randint(jax.random.fold_in(_rk, 8), (4,), 0, max(1, 64 // 4) + 1, jnp.int32)
        _ctx_4096P = jax.random.normal(jax.random.fold_in(_rk, 11), (4, 16, 512), jnp.float32)
        _ctx_4096c = jax.random.dirichlet(jax.random.fold_in(_rk, 511), 0.3 * jnp.ones((16,), jnp.float32), (4, 64))
        _ctx_4096t = jnp.einsum('bsk,bkd->bsd', _ctx_4096c, _ctx_4096P)
        _ctx_4096t = _ctx_4096t * jax.lax.rsqrt(jnp.mean(jnp.square(_ctx_4096t)) + 1e-12) * 0.953939
        ctx_4096 = -2.8382e-05 + 0.999851 * (_ctx_4096t + 0.3 * jax.random.normal(jax.random.fold_in(_rk, 611), (4, 64, 512), jnp.float32))
        _validS = jnp.arange(256)[None, :] < _lenS[:, None]
        _validS2 = jnp.arange(64)[None, :] < _lenS2[:, None]
        _causal = jnp.tril(jnp.ones((256, 256), dtype=bool))
        mask_1x1xSxS2_ff0 = jnp.where(jnp.ones((1, 1, 256, 64), dtype=bool), 0.0, -1000000000.0).astype(jnp.float32)
        return (x, ctx_4096, mask_1x1xSxS2_ff0)
    x, ctx_4096, mask_1x1xSxS2_ff0 = _rec_inputs()

    def _L0_attn_setup():
        import jax, jax.numpy as jnp
        import numpy as np
        B, S, E, H = (2, 256, 512, 32)
        D = E // H
        ROPE_BASE = 10000.0
        MASK_VAL = -66504.0

        def _rope(x, cos, sin):
            x1, x2 = jnp.split(x, 2, axis=-1)
            return jnp.concatenate([x1 * cos - x2 * sin, x2 * cos + x1 * sin], axis=-1)
        key = jax.random.key(seed)
        k1, k2, k3, k4, k5 = jax.random.split(key, 5)
        return {'hidden_states': jax.random.normal(k1, (B, S, E), dtype=jnp.float32), 'qkv_w': jax.random.normal(k2, (E, 3 * E), dtype=jnp.float32) * 0.02, 'qkv_b': jax.random.normal(k3, (3 * E,), dtype=jnp.float32) * 0.02, 'out_w': jax.random.normal(k4, (E, E), dtype=jnp.float32) * 0.02, 'out_b': jax.random.normal(k5, (E,), dtype=jnp.float32) * 0.02}
    _L0_attn_all = _L0_attn_setup()
    _L0_attn_in = {k: v for k, v in _L0_attn_all.items() if k in ('qkv_w', 'qkv_b', 'out_w', 'out_b')}
    del _L0_attn_all

    def _L0_xattn_setup():
        import jax, jax.numpy as jnp
        import numpy as np
        NUM_HEADS = 32
        NUM_KV_HEADS = 8
        HEAD_DIM = 128
        HIDDEN = 512
        EPS = 1e-05

        def rmsnorm(x, w, eps=EPS):
            xf = x.astype(jnp.float32)
            var = jnp.mean(xf * xf, axis=-1, keepdims=True)
            return w * (xf * jax.lax.rsqrt(var + eps)).astype(x.dtype)
        key = jax.random.key(seed)
        ks = jax.random.split(key, 10)
        B, Q, KV = (1, 128, 6404)
        s = 1.0 / np.sqrt(HIDDEN)
        return {'hidden_states': jax.random.normal(ks[0], (B, Q, HIDDEN), jnp.float32), 'cross_attention_states': jax.random.normal(ks[1], (B, KV, HIDDEN), jnp.float32), 'attention_mask': jnp.zeros((B, 1, Q, KV), jnp.float32), 'q_proj_w': jax.random.normal(ks[2], (NUM_HEADS * HEAD_DIM, HIDDEN), jnp.float32) * s, 'k_proj_w': jax.random.normal(ks[3], (NUM_KV_HEADS * HEAD_DIM, HIDDEN), jnp.float32) * s, 'v_proj_w': jax.random.normal(ks[4], (NUM_KV_HEADS * HEAD_DIM, HIDDEN), jnp.float32) * s, 'o_proj_w': jax.random.normal(ks[5], (HIDDEN, NUM_HEADS * HEAD_DIM), jnp.float32) * s, 'q_norm_w': jnp.ones((HEAD_DIM,), jnp.float32), 'k_norm_w': jnp.ones((HEAD_DIM,), jnp.float32)}
    _L0_xattn_all = _L0_xattn_setup()
    _L0_xattn_in = {k: v for k, v in _L0_xattn_all.items() if k in ('q_proj_w', 'k_proj_w', 'v_proj_w', 'o_proj_w', 'q_norm_w', 'k_norm_w')}
    del _L0_xattn_all

    def _L0_ffn_setup():
        import jax, jax.numpy as jnp
        import numpy as np
        B, S, D_IN, D_OUT = (2, 256, 512, 512)
        E, K, R = (8, 2, 16)
        SCALING = 32.0 / 16.0
        key = jax.random.key(seed)
        ks = jax.random.split(key, 6)
        x = jax.random.normal(ks[0], (B, S, D_IN), dtype=jnp.float32)
        gate_w = jax.random.normal(ks[1], (E, D_IN), dtype=jnp.float32) * 0.02
        base_w = jax.random.normal(ks[2], (D_OUT, D_IN), dtype=jnp.float32) * 0.02
        base_b = jax.random.normal(ks[3], (D_OUT,), dtype=jnp.float32) * 0.02
        lora_A = jax.random.normal(ks[4], (E, R, D_IN), dtype=jnp.float32) * 0.02
        lora_B = jax.random.normal(ks[5], (E, D_OUT, R), dtype=jnp.float32) * 0.02
        return {'x': x, 'gate_w': gate_w, 'base_w': base_w, 'base_b': base_b, 'lora_A': lora_A, 'lora_B': lora_B}
    _L0_ffn_all = _L0_ffn_setup()
    _L0_ffn_in = {k: v for k, v in _L0_ffn_all.items() if k in ('gate_w', 'base_w', 'base_b', 'lora_A', 'lora_B')}
    del _L0_ffn_all
    return {'x': x, 'ctx_4096': ctx_4096, 'mask_1x1xSxS2_ff0': mask_1x1xSxS2_ff0, 'L0_attn_qkv_w': _L0_attn_in['qkv_w'], 'L0_attn_qkv_b': _L0_attn_in['qkv_b'], 'L0_attn_out_w': _L0_attn_in['out_w'], 'L0_attn_out_b': _L0_attn_in['out_b'], 'L0_xattn_q_proj_w': _L0_xattn_in['q_proj_w'], 'L0_xattn_k_proj_w': _L0_xattn_in['k_proj_w'], 'L0_xattn_v_proj_w': _L0_xattn_in['v_proj_w'], 'L0_xattn_o_proj_w': _L0_xattn_in['o_proj_w'], 'L0_xattn_q_norm_w': _L0_xattn_in['q_norm_w'], 'L0_xattn_k_norm_w': _L0_xattn_in['k_norm_w'], 'L0_ffn_gate_w': _L0_ffn_in['gate_w'], 'L0_ffn_base_w': _L0_ffn_in['base_w'], 'L0_ffn_base_b': _L0_ffn_in['base_b'], 'L0_ffn_lora_A': _L0_ffn_in['lora_A'], 'L0_ffn_lora_B': _L0_ffn_in['lora_B']}

def reference(x, ctx_4096, mask_1x1xSxS2_ff0, L0_attn_qkv_w, L0_attn_qkv_b, L0_attn_out_w, L0_attn_out_b, L0_xattn_q_proj_w, L0_xattn_k_proj_w, L0_xattn_v_proj_w, L0_xattn_o_proj_w, L0_xattn_q_norm_w, L0_xattn_k_norm_w, L0_ffn_gate_w, L0_ffn_base_w, L0_ffn_base_b, L0_ffn_lora_A, L0_ffn_lora_B):
    import jax
    import jax.numpy as jnp

    def _L0_attn_ref(hidden_states, qkv_w, qkv_b, out_w, out_b):
        import jax, jax.numpy as jnp
        import numpy as np
        B, S, E, H = (2, 256, 512, 32)
        D = E // H
        ROPE_BASE = 10000.0
        MASK_VAL = -66504.0

        def _rope(x, cos, sin):
            x1, x2 = jnp.split(x, 2, axis=-1)
            return jnp.concatenate([x1 * cos - x2 * sin, x2 * cos + x1 * sin], axis=-1)
        b, s, e = hidden_states.shape
        qkv = hidden_states @ qkv_w + qkv_b
        q, k, v = jnp.split(qkv, 3, axis=-1)
        q = q.reshape(b, s, H, D)
        k = k.reshape(b, s, H, D)
        v = v.reshape(b, s, H, D)
        half = D // 2
        inv_freq = 1.0 / ROPE_BASE ** (jnp.arange(0, half, dtype=jnp.float32) / half)
        ang = jnp.arange(s, dtype=jnp.float32)[:, None] * inv_freq[None, :]
        cos = jnp.cos(ang)[None, :, None, :]
        sin = jnp.sin(ang)[None, :, None, :]
        q = _rope(q, cos, sin)
        k = _rope(k, cos, sin)
        scale = 1.0 / jnp.sqrt(jnp.asarray(D, dtype=hidden_states.dtype))
        scores = jnp.einsum('bqhd,bkhd->bhqk', q, k) * scale
        causal = jnp.tril(jnp.ones((s, s), dtype=scores.dtype))
        scores = scores + (1.0 - causal) * MASK_VAL
        probs = jax.nn.softmax(scores, axis=-1)
        ctx = jnp.einsum('bhqk,bkhd->bqhd', probs, v).reshape(b, s, e)
        return ctx @ out_w + out_b

    def _L0_xattn_ref(hidden_states, cross_attention_states, attention_mask, q_proj_w, k_proj_w, v_proj_w, o_proj_w, q_norm_w, k_norm_w):
        import jax, jax.numpy as jnp
        import numpy as np
        NUM_HEADS = 32
        NUM_KV_HEADS = 8
        HEAD_DIM = 128
        HIDDEN = 512
        EPS = 1e-05

        def rmsnorm(x, w, eps=EPS):
            xf = x.astype(jnp.float32)
            var = jnp.mean(xf * xf, axis=-1, keepdims=True)
            return w * (xf * jax.lax.rsqrt(var + eps)).astype(x.dtype)
        B, Q, _ = hidden_states.shape
        KV = cross_attention_states.shape[1]
        n_rep = NUM_HEADS // NUM_KV_HEADS
        q = (hidden_states @ q_proj_w.T).reshape(B, Q, NUM_HEADS, HEAD_DIM).transpose(0, 2, 1, 3)
        k = (cross_attention_states @ k_proj_w.T).reshape(B, KV, NUM_KV_HEADS, HEAD_DIM).transpose(0, 2, 1, 3)
        v = (cross_attention_states @ v_proj_w.T).reshape(B, KV, NUM_KV_HEADS, HEAD_DIM).transpose(0, 2, 1, 3)
        q = rmsnorm(q, q_norm_w)
        k = jnp.repeat(k, n_rep, axis=1)
        v = jnp.repeat(v, n_rep, axis=1)
        k = rmsnorm(k, k_norm_w)
        scale = 1.0 / np.sqrt(HEAD_DIM)
        scores = jnp.einsum('bhqd,bhkd->bhqk', q, k) * scale + attention_mask
        attn = jax.nn.softmax(scores.astype(jnp.float32), axis=-1).astype(q.dtype)
        out = jnp.einsum('bhqk,bhkd->bhqd', attn, v)
        out = out.transpose(0, 2, 1, 3).reshape(B, Q, NUM_HEADS * HEAD_DIM)
        return out @ o_proj_w.T

    def _L0_ffn_ref(x, gate_w, base_w, base_b, lora_A, lora_B):
        import jax, jax.numpy as jnp
        import numpy as np
        B, S, D_IN, D_OUT = (2, 256, 512, 512)
        E, K, R = (8, 2, 16)
        SCALING = 32.0 / 16.0
        gate_logits = jnp.einsum('bsd,ed->bse', x, gate_w)
        weights, selected = jax.lax.top_k(gate_logits, K)
        weights = jax.nn.softmax(weights.astype(jnp.float32), axis=2).astype(x.dtype)
        result = jnp.einsum('bsd,od->bso', x, base_w) + base_b
        w_full = jnp.sum(jax.nn.one_hot(selected, E, dtype=x.dtype) * weights[..., None], axis=2)
        low = jnp.einsum('bsd,erd->ebsr', x, lora_A)
        lora_out = jnp.einsum('ebsr,eor,bse->bso', low, lora_B, w_full)
        result = result + SCALING * lora_out
        return result
    x = _layernorm(x + _L0_attn_ref(x, L0_attn_qkv_w, L0_attn_qkv_b, L0_attn_out_w, L0_attn_out_b), axis=-1)
    x = _layernorm(x + _L0_xattn_ref(x, ctx_4096, mask_1x1xSxS2_ff0, L0_xattn_q_proj_w, L0_xattn_k_proj_w, L0_xattn_v_proj_w, L0_xattn_o_proj_w, L0_xattn_q_norm_w, L0_xattn_k_norm_w), axis=-1)
    x = _layernorm(x + _L0_ffn_ref(x, L0_ffn_gate_w, L0_ffn_base_w, L0_ffn_base_b, L0_ffn_lora_A, L0_ffn_lora_B), axis=-1)
    return x

_drawn_inputs = setup_inputs


def setup_inputs(seed=0):
    import zlib

    import numpy as np

    out = dict(_drawn_inputs(seed))
    spreads = {'L0_xattn_q_norm_w': (1.0, 0.2), 'L0_xattn_k_norm_w': (1.0, 0.2)}
    factors = {'L0_attn_qkv_w': 2.771,
     'L0_attn_qkv_b': 8.0,
     'L0_attn_out_w': 2.671,
     'L0_attn_out_b': 4.289,
     'L0_ffn_base_b': 3.326}
    for name, (base, spread) in spreads.items():
        noise = np.random.default_rng([zlib.crc32(name.encode()), seed]).standard_normal(out[name].shape)
        drawn = base * np.exp(spread * noise) if base else spread * noise
        out[name] = jnp.asarray(drawn.astype(out[name].dtype))
    for name, factor in factors.items():
        out[name] = (out[name] * factor).astype(out[name].dtype)
    return out
```

```python
from contextlib import ExitStack

import concourse.bass as bass
from concourse import mybir

ALU = mybir.AluOpType
ACT = mybir.ActivationFunctionType
AX = mybir.AxisListType
F32 = mybir.dt.float32
F32R = mybir.dt.float32r
BF16 = mybir.dt.bfloat16

P = 128
B, SEQ, E = 4, 256, 512
NT = B * SEQ // P
KC = E // P
H, D = 32, 16
HQ = H // 4
NI = B * HQ
XH, XG, XD, XS = 32, 8, 128, 64
XR = XH // XG
NE, R = 8, 16
EPS = 1e-5
MASK_VAL = -66504.0
MASK_A, MASK_B = -1632.0, 163.0
KB = 1024
PASSES = ((0, 0), (0, 1), (1, 0))
assert MASK_A * MASK_B == 4 * MASK_VAL


def decoder_layer(nc, xT, x, ctxT, mask, wqkv, qkvb, wout, outb, wqT, wkT, wvT, woT, qn, kn,
                  gateT, baseT, baseb, loraAT, loraB, rope, ident, causal, order, out):
    with ExitStack() as ctx:
        base_at = 16512

        def at(name, kb, shape, dt):
            return nc.alloc_sbuf_tensor_at(name, shape, dt, offset=base_at + int(kb * KB))

        def sem(name):
            return ctx.enter_context(nc.semaphore(name))

        ps = ctx.enter_context(nc.psum_tensor("ps", [P, 8, 512], F32))

        KTx = at("KTx", 0, [P, XG, B * XS], F32)
        VTx = at("VTx", 8, [P, XG, B * XS], F32)
        c0 = 16
        identf = at("identf", c0, [P, P], F32)
        maskx = at("maskx", c0 + 0.5, [P, 2, XS], F32)
        outbs = at("outbs", c0 + 1, [P, E], F32)
        basebs = at("basebs", c0 + 3, [P, E], F32)
        causb = at("causb", c0 + 5, [P, 2, SEQ], BF16)
        diagb = at("diagb", c0 + 6, [P, P], BF16)
        ropes = at("ropes", c0 + 6.25, [P, 2, 2, D], F32)
        ones = at("ones", c0 + 6.5, [P, 1], F32)
        mhalf = at("mhalf", c0 + 6.5625, [P, 8], F32)
        wqn = at("wqn", c0 + 6.625, [P, 1], F32)
        wkn = at("wkn", c0 + 6.6875, [P, 1], F32)
        wqk = at("wqk", c0 + 6.75, [P, 1], F32)
        orders = at("orders", c0 + 6.8125, [P, NE], F32)
        small = at("small", c0 + 7, [P, 256], F32)
        junk = at("junk", 207, [P, P], F32)
        kvraw = at("kvraw", 142, [P, 4, KC, 512], F32)
        kvs = at("kvs", 174, [P, 2, 2, KC, 512], F32R)
        ctxs = at("ctxs", 110, [P, 2, KC, B * XS], F32R)
        ctxraw = at("ctxraw", 124, [P, KC, B * XS], F32)
        knat = at("knat", 128, [P, 2, 512], F32)
        wraw = at("wraw", 72, [P, 3, KC, 512], F32)
        ws = at("ws", 24, [P, 2, 3, KC, 512], F32R)
        xraw = at("xraw", 120, [P, 2, KC, P], F32)
        xs = at("xs", 132, [P, 2, 2, KC, P], F32R)
        qraw = at("qraw", 96, [P, 2, 512], F32)
        qrot = at("qrot", 100, [P, 2, 512], F32)
        qkvbs = at("qkvbs", 104, [P, 3, 512], F32)
        causf = at("causf", 118, [P, 2, SEQ], F32)
        qk = at("qk", 142, [P, NI, 2, 2, 64], F32)
        vx = at("vx", 174, [P, NI, 2, 4, D], F32)
        att = at("att", 191, [P, NI, 2, 64], F32)
        sb = at("sb", 104, [P, 2, 2, 4, SEQ], F32)
        pts = at("pts", 120, [P, 2, 512], F32)
        pack = at("pack", 124, [P, 2, 2, 4, 64], F32)
        qkt = at("qkt", 128, [P, 2, 2, SEQ], F32R)
        vst = at("vst", 136, [P, 2, 2, 4, 2 * D], F32)
        ot = at("ot", 138, [P, SEQ], F32)
        woraw = at("woraw", 72, [P, KC, 512], F32)
        wos = at("wos", 88, [P, 2, KC, 512], F32R)
        aT = at("aT", 80, [P, 2, 2, KC, P], F32R)
        attc = at("attc", 104, [P, 2, E], F32)
        x1c = at("x1c", 108, [P, 2, E], F32)
        ro = at("ro", 112, [P, 2, E], F32)
        xres = at("xres", 132, [P, 2, E], F32)
        yacc = at("yacc", 24, [P, NT, E], F32)
        x1T = at("x1T", 40, [P, 2, KC, B * SEQ], F32R)
        wqs = at("wqs", 72, [P, XR, 2, KC, P], F32R)
        wxs = at("wxs", 88, [P, XR, 2, E], F32R)
        vws = at("vws", 104, [P, 2, 2, 2, E], F32R)
        pT = at("pT", 120, [P, 2, 2, 8, P], F32R)
        vpad = at("vpad", 136, [P, 2, B, 3 * XS], F32R)
        qT = at("qT", 142, [P, 2, B * SEQ], F32)
        sq = at("sq", 150, [P, 2, B * SEQ], F32)
        wqraw = at("wqraw", 158, [P, XR, KC, P], F32)
        wxraw = at("wxraw", 166, [P, XR, E], F32)
        prob = at("prob", 174, [P, 2, 8, 2, XS], F32)
        lbs = at("lbs", 182, [P, E], F32)
        baseraw = at("baseraw", 191, [P, KC, E], F32)
        garaw = at("garaw", 199, [P, KC, NE + P], F32)
        gas = at("gas", 202, [P, 2, KC, NE + P], F32R)
        bases = at("bases", 72, [P, 2, KC, E], F32R)
        x2c = at("x2c", 142, [P, 2, E], F32)
        x2T = at("x2T", 146, [P, 2, 2, KC, P], F32R)
        x2b = at("x2b", 154, [P, 2, E], F32)
        lowm = at("lowm", 158, [P, 2, P], F32)
        lowT = at("lowT", 159, [P, 2, P], F32)
        fo = at("fo", 160, [P, 2, E], F32)
        fout = at("fout", 164, [P, 2, E], F32)
        gl = at("gl", 168, [P, NT, NE + P], F32)
        route = at("route", 173, [P, 8, NT, NE], F32)
        wts = at("wts", 175, [P, 8, NT], F32)

        d_const, d_ctx, d_wo, d_f = map(sem, ("d_const", "d_ctx", "d_wo", "d_f"))
        d_out = [sem(f"d_out{n}") for n in range(2)]
        d_kv = [sem(f"d_kv{n}") for n in range(4)]
        d_w = [sem(f"d_w{n}") for n in range(3)]
        d_x = [sem(f"d_x{n}") for n in range(2)]
        d_xres = [sem(f"d_xres{n}") for n in range(2)]
        d_wq = [sem(f"d_wq{n}") for n in range(XR)]
        d_wx = [sem(f"d_wx{n}") for n in range(XR)]
        consts_ready, dve_consts = sem("consts_ready"), sem("dve_consts")
        ctx_hi, ctx_lo, kv_hi, kv_lo = map(sem, ("ctx_hi", "ctx_lo", "kv_hi", "kv_lo"))
        k_mm, k_sq, k_ms, k_r, k_nat, k_tr, k_done = map(
            sem, ("k_mm", "k_sq", "k_ms", "k_r", "k_nat", "k_tr", "k_done"))
        v_mm, v_done = sem("v_mm"), sem("v_done")
        w_hi, w_lo, x_hi, x_lo = map(sem, ("w_hi", "w_lo", "x_hi", "x_lo"))
        qkv_mm, qkv_free, rope_step, rope_done = map(sem, ("qkv_mm", "qkv_free", "rope_step", "rope_done"))
        pack_hi, packed, tr_q, tr_k, qt_ready, kt_ready = map(
            sem, ("pack_hi", "packed", "tr_q", "tr_k", "qt_ready", "kt_ready"))
        s_mm, s_max, s_free, s_exp = map(sem, ("s_mm", "s_max", "s_free", "s_exp"))
        v_ready, pt_mm, pt_sb, pts_free, ot_sb, ob_mm, o_rec, o_norm = map(
            sem, ("v_ready", "pt_mm", "pt_sb", "pts_free", "ot_sb", "ob_mm", "o_rec", "o_norm"))
        wo_hi, wo_lo, a_copy, a_tr, a_hi, a_lo, o_mm, o_res, o_sum = map(
            sem, ("wo_hi", "wo_lo", "a_copy", "a_tr", "a_hi", "a_lo", "o_mm", "o_res", "o_sum"))
        o_stat, o_ve, o_rstd, x1_done, x1_tr, x1_hi, x1_free, y_init = map(
            sem, ("o_stat", "o_ve", "o_rstd", "x1_done", "x1_tr", "x1_hi", "x1_free", "y_init"))
        wq_hi, wq_lo, wx_hi, wx_lo = map(sem, ("wq_hi", "wq_lo", "wx_hi", "wx_lo"))
        q_mm, q_free, n_mm, sx_mm = map(sem, ("q_mm", "q_free", "n_mm", "sx_mm"))
        n_sb, n_r, p_scaled, p_masked, p_max, p_sub, p_exp, p_sum, p_rec, p_norm = map(
            sem, ("n_sb", "n_r", "p_scaled", "p_masked", "p_max", "p_sub", "p_exp", "p_sum", "p_rec", "p_norm"))
        xt_mm, xt_hi, xt_lo, z_zero, z_hi, z_lo = map(
            sem, ("xt_mm", "xt_hi", "xt_lo", "z_zero", "z_hi", "z_lo"))
        vw_mm, vw_hi, vw_free, y_mm, y_add = map(sem, ("vw_mm", "vw_hi", "vw_free", "y_mm", "y_add"))
        b_hi, b_lo, f_stat, f_ve, f_rstd, f_x2, f_tr, f_hi, f_lo, f_bias = map(
            sem, ("b_hi", "b_lo", "f_stat", "f_ve", "f_rstd", "f_x2", "f_tr", "f_hi", "f_lo", "f_bias"))
        f_mm, g_mm, g_sb, z_sum, r_step, r_exp = map(sem, ("f_mm", "g_mm", "g_sb", "z_sum", "r_step", "r_exp"))
        l_low, l_tr, l_sb, l_mm, h_sum, h_stat, h_ve, h_rstd, h_out = map(
            sem, ("l_low", "l_tr", "l_sb", "l_mm", "h_sum", "h_stat", "h_ve", "h_rstd", "h_out"))
        dve_passed, pool_passed = sem("dve_passed"), sem("pool_passed")
        NCONST = 10

        def over(ap, n):
            return ap.unsqueeze(len(ap.shape)).broadcast_to([*ap.shape, n])

        def heads(ap, n):
            return ap.rearrange("p (a b) -> p a b", a=n)

        def pt_bank(j):
            return (6, 0)[j % 2]

        block = ctx.enter_context(nc.Block())

        @block.sync
        def _(sp):
            sp.dma_start(ctxraw[:], ctxT).then_inc(d_ctx, 16)
            for n in range(4):
                sp.dma_start(kvraw[:, n], (wkT, wvT)[n // 2][n % 2]).then_inc(d_kv[n], 16)
                if n == 0:
                    for dst, src in ((identf[:], ident), (maskx[:], mask.rearrange("(c p) k -> p c k", p=P)),
                                     (outbs[:], outb.partition_broadcast(P)),
                                     (basebs[:], baseb.partition_broadcast(P)),
                                     (qkvbs[:].rearrange("p a b -> p (a b)"), qkvb.partition_broadcast(P)),
                                     (ropes[:], rope), (wqn[:], qn), (wkn[:], kn),
                                     (orders[:], order.partition_broadcast(P)), (causf[:], causal)):
                        sp.dma_start(dst, src).then_inc(d_const, 16)
            for n in range(3):
                sp.dma_start(wraw[:, n], wqkv.rearrange("(k p) n -> p k n", p=P)[:, :, n * 512:(n + 1) * 512]
                             ).then_inc(d_w[n], 16)
                if n == 0:
                    for s in range(2):
                        sp.dma_start(xraw[:, s], xT[s]).then_inc(d_x[s], 16)
            with sp.Fori(1, NT // 2) as u:
                for s in range(2):
                    sp.wait_ge(x_lo, 2 * u + s - 1)
                    sp.wait_ge(x_hi, 2 * u + s - 1)
                    sp.dma_start(xraw[:, s], xT[2 * u + s]).then_inc(d_x[s], 16)
            sp.wait_ge(w_lo, 3)
            sp.wait_ge(w_hi, 3)
            sp.dma_start(woraw[:], wout.rearrange("(k p) n -> p k n", p=P)).then_inc(d_wo, 16)
            sp.wait_ge(qkv_mm, 3 * NT)
            for s in range(2):
                sp.dma_start(xres[:, s], x[s]).then_inc(d_xres[s], 16)
            sp.wait_ge(packed, 2 * NI)
            for j in range(XR):
                sp.dma_start(wqraw[:, j], wqT[j]).then_inc(d_wq[j], 16)
            for j in range(XR):
                sp.dma_start(wxraw[:, j], woT[j]).then_inc(d_wx[j], 16)
            with sp.Fori(1, NT // 2) as u:
                for s in range(2):
                    sp.wait_ge(o_sum, 2 * u + s - 1)
                    sp.dma_start(xres[:, s], x[2 * u + s]).then_inc(d_xres[s], 16)
            sp.wait_ge(a_copy, NT)
            sp.dma_start(baseraw[:], baseT).then_inc(d_f, 16)
            sp.dma_start(garaw[:, :, 0:NE], gateT).then_inc(d_f, 16)
            sp.dma_start(garaw[:, :, NE:], loraAT).then_inc(d_f, 16)
            sp.dma_start(lbs[:], loraB).then_inc(d_f, 16)
            with sp.Fori(1, XG) as g:
                for j in range(XR):
                    sp.wait_ge(wq_lo, XR * g + j - (XR - 1))
                    sp.wait_ge(wq_hi, XR * g + j - (XR - 1))
                    sp.dma_start(wqraw[:, j], wqT[XR * g + j]).then_inc(d_wq[j], 16)
                for j in range(XR):
                    sp.wait_ge(wx_lo, XR * g + j - (XR - 1))
                    sp.wait_ge(wx_hi, XR * g + j - (XR - 1))
                    sp.dma_start(wxraw[:, j], woT[XR * g + j]).then_inc(d_wx[j], 16)
            with sp.Fori(0, NT // 2) as u:
                for s in range(2):
                    sp.wait_ge(h_out, 2 * u + s + 1)
                    sp.dma_start(out[2 * u + s], fout[:, s]).then_inc(d_out[s], 16)
            for s in range(2):
                sp.wait_ge(d_out[s], 16 * NT // 2)

        @block.gpsimd
        def _(pool):
            def minus(hi, lo, raw):
                return nc.gpsimd.tensor_tensor(lo, raw, hi.bitcast(F32), ALU.subtract)

            nc.gpsimd.memset(ones[:], 1.0).then_inc(consts_ready, 1)
            nc.gpsimd.memset(mhalf[:], -0.5).then_inc(consts_ready, 1)
            pool.wait_ge(consts_ready, 2)
            pool.wait_ge(d_ctx, 16)
            pool.wait_ge(ctx_hi, 1)
            minus(ctxs[:, 0], ctxs[:, 1], ctxraw[:]).then_inc(ctx_lo, 1)
            for n in range(4):
                pool.wait_ge(d_kv[n], 16)
                pool.wait_ge(kv_hi, n + 1)
                minus(kvs[:, n % 2, 0], kvs[:, n % 2, 1], kvraw[:, n]).then_inc(kv_lo, 1)
                if n == 3:
                    for u in range(4):
                        pool.wait_ge(k_ms, u + 1)
                        nc.gpsimd.tensor_tensor(small[:, 32 + 4 * u:36 + 4 * u], small[:, 16 + 4 * u:20 + 4 * u],
                                                mhalf[:, 0:4], ALU.pow).then_inc(k_r, 1)
            for n in range(3):
                pool.wait_ge(d_w[n], 16)
                pool.wait_ge(w_hi, n + 1)
                minus(ws[:, 0, n], ws[:, 1, n], wraw[:, n]).then_inc(w_lo, 1)
                if n == 0:
                    for s in range(2):
                        pool.wait_ge(d_x[s], 16)
                        pool.wait_ge(x_hi, s + 1)
                        minus(xs[:, s, 0], xs[:, s, 1], xraw[:, s]).then_inc(x_lo, 1)
            with pool.Fori(1, NT // 2) as u:
                for s in range(2):
                    pool.wait_ge(d_x[s], 16 * u + 16)
                    pool.wait_ge(x_hi, 2 * u + s + 1)
                    minus(xs[:, s, 0], xs[:, s, 1], xraw[:, s]).then_inc(x_lo, 1)

            pool.wait_ge(rope_done, 2 * NT + 1)
            nc.gpsimd.memset(pack[:], 0.0).then_inc(pack_hi, 1)
            nc.gpsimd.memset(vst[:], 1.0).then_inc(v_ready, 1)
            pool.wait_ge(pack_hi, 1)
            pool.wait_ge(v_ready, 1)

            def pack_qk(i):
                pool.wait_ge(tr_k, i + 1)
                for a in range(2):
                    nat = qk[:, i, :, a, :].rearrange("p c (j d) -> p c j d", j=4)
                    hi = pack[:, a, :, :, 0:D]
                    hi2 = pack[:, a, :, :, (1 + a) * D:(2 + a) * D]
                    lo = pack[:, a, :, :, (2 - a) * D:(3 - a) * D]
                    nc.gpsimd.tensor_copy(hi.bitcast(F32R), nat).then_inc(pack_hi, 1)
                    nc.gpsimd.tensor_copy(hi2.bitcast(F32R), nat).then_inc(pack_hi, 1)
                    pool.wait_ge(pack_hi, 4 * i + 2 * a + 3)
                    pool.sem_inc(pool_passed, 1)
                    nc.gpsimd.tensor_tensor(lo, nat, hi, ALU.subtract).then_inc(packed, 1)

            def v_copy(i, par):
                nc.gpsimd.tensor_copy(vst[:, par, :, :, 0:D], vx[:, i]).then_inc(v_ready, 1)

            pack_qk(0)
            pack_qk(1)
            v_copy(0, 0)
            with pool.Fori(1, NI // 2) as u:
                for par in range(2):
                    i = 2 * u + par
                    pack_qk(i)
                    pool.wait_ge(pts_free, 4 * i - 6)
                    v_copy(i - 1, 1 - par)
            pool.wait_ge(pts_free, 4 * NI - 6)
            v_copy(NI - 1, 1)

            pool.wait_ge(wo_hi, 1)
            minus(wos[:, 0], wos[:, 1], woraw[:]).then_inc(wo_lo, 1)
            with pool.Fori(0, NT // 2) as u:
                for s in range(2):
                    pool.wait_ge(d_xres[s], 16 * u + 16)
                    nc.gpsimd.tensor_tensor(xres[:, s], xres[:, s], outbs[:], ALU.add).then_inc(o_res, 1)
                    pool.wait_ge(o_ve, 2 * u + s + 1)
                    nc.gpsimd.tensor_tensor(small[:, 64 + s:65 + s], small[:, 62 + s:63 + s], mhalf[:, 0:1],
                                            ALU.pow).then_inc(o_rstd, 1)

            def prob_of(j):
                return prob[:, j // 2, :, j % 2, :]

            def query_rms(h):
                pool.wait_ge(n_sb, h + 1)
                nc.gpsimd.tensor_tensor(small[:, 80:88], small[:, 72:80], mhalf[:], ALU.pow).then_inc(n_r, 1)

            def add_mask(h, j):
                p = prob_of(j)
                m = maskx[:].unsqueeze(1).broadcast_to([P, B, 2, XS])
                pool.wait_ge(p_scaled, h + 1)
                nc.gpsimd.tensor_tensor(p.rearrange("p (b c) k -> p b c k", b=B),
                                        p.rearrange("p (b c) k -> p b c k", b=B), m, ALU.add).then_inc(p_masked, 1)

            def less_max(h, j):
                pool.wait_ge(p_max, h + 1)
                nc.gpsimd.tensor_tensor(prob_of(j), prob_of(j), over(small[:, 88:96], XS),
                                        ALU.subtract).then_inc(p_sub, 1)

            def over_sum(h, j):
                pool.wait_ge(p_rec, h + 1)
                nc.gpsimd.tensor_tensor(prob_of(j), prob_of(j), over(small[:, 104:112], XS),
                                        ALU.mult).then_inc(p_norm, 1)

            def wq_low(h, j):
                pool.wait_ge(wq_hi, h + 1)
                minus(wqs[:, j, 0], wqs[:, j, 1], wqraw[:, j]).then_inc(wq_lo, 1)

            def wx_low(h, j):
                pool.wait_ge(wx_hi, h + 1)
                minus(wxs[:, j, 0], wxs[:, j, 1], wxraw[:, j]).then_inc(wx_lo, 1)

            def project(g):
                h = XR * g
                wx_low(h, 0)
                add_mask(h + 3, 3)
                wx_low(h + 1, 1)
                less_max(h + 3, 3)
                wx_low(h + 2, 2)
                wx_low(h + 3, 3)
                over_sum(h + 3, 3)
                pool.wait_ge(z_hi, g + 1)
                minus(vpad[:, 0, :, XS:2 * XS], vpad[:, 1, :, XS:2 * XS],
                      VTx[:, g, :].rearrange("p (b k) -> p b k", b=B)).then_inc(z_lo, 1)

            def attend(g, more):
                h = XR * g
                if more:
                    wq_low(h + 4, 0)
                    wq_low(h + 5, 1)
                for j in range(3):
                    query_rms(h + j)
                    add_mask(h + j, j)
                    less_max(h + j, j)
                    over_sum(h + j, j)
                    if more and j:
                        wq_low(h + 5 + j, 1 + j)
                query_rms(h + 3)

            pool.wait_ge(qt_ready, NI)
            pool.wait_ge(o_norm, NI)
            nc.gpsimd.memset(vpad[:].bitcast(F32), 0.0).then_inc(z_zero, 1)
            for j in range(XR):
                wq_low(j, j)
            attend(0, True)
            with pool.Fori(1, XG - 1) as g:
                project(g - 1)
                attend(g, True)
            project(XG - 2)
            attend(XG - 1, False)
            project(XG - 1)

            pool.wait_ge(b_hi, 1)
            minus(bases[:, 0], bases[:, 1], baseraw[:]).then_inc(b_lo, 1)
            pool.wait_ge(b_hi, 2)
            minus(gas[:, 0], gas[:, 1], garaw[:]).then_inc(b_lo, 1)
            with pool.Fori(0, NT // 2) as u:
                for s in range(2):
                    pool.wait_ge(f_ve, 2 * u + s + 1)
                    nc.gpsimd.tensor_tensor(small[:, 162 + s:163 + s], small[:, 160 + s:161 + s], mhalf[:, 0:1],
                                            ALU.pow).then_inc(f_rstd, 1)
                    pool.wait_ge(f_x2, 2 * u + s + 1)
                    nc.gpsimd.tensor_tensor(x2b[:, s], x2c[:, s], basebs[:], ALU.add).then_inc(f_bias, 1)
            with pool.Fori(0, NT // 2) as u:
                for s in range(2):
                    pool.wait_ge(h_ve, 2 * u + s + 1)
                    nc.gpsimd.tensor_tensor(small[:, 182 + s:183 + s], small[:, 180 + s:181 + s], mhalf[:, 0:1],
                                            ALU.pow).then_inc(h_rstd, 1)

        @block.scalar
        def _(act):
            def copy(dst, src):
                return nc.scalar.activation(dst, src, ACT.Copy)

            act.sem_inc(q_free, 2)
            act.wait_ge(dve_consts, 3)
            for u in range(4):
                act.wait_ge(k_mm, u + 1)
                for g in range(4):
                    act.wait_ge(k_sq, 4 * u + g)
                    nc.scalar.activation(junk[:], ps[:, u, g * XD:(g + 1) * XD], ACT.Square,
                                         accum_out=small[:, 4 * u + g:4 * u + g + 1]).then_inc(k_sq, 1)
            for u in range(4):
                act.wait_ge(k_tr, u + 1)
                n, t = u // 2, u % 2
                nc.scalar.activation(KTx[:, 4 * n:4 * n + 4, t * P:(t + 1) * P], heads(ps[:, 4 + u % 2, :], 4),
                                     ACT.Copy, scale=wqk[:, 0:1]).then_inc(k_done, 1)

            def q_out(i):
                act.wait_ge(tr_q, i + 1)
                copy(qkt[:, 0].rearrange("p a b -> p (a b)"), ps[:, 0, :]).then_inc(qt_ready, 1)

            def pt_out(i):
                for f in range(4):
                    act.wait_ge(pt_mm, 4 * i + f + 1)
                    act.wait_ge(pts_free, 4 * i + f + 1)
                    copy(pts[:, f % 2], ps[:, pt_bank(f), :]).then_inc(pt_sb, 1)

            def exps(i, par, c):
                act.wait_ge(s_free, 2 * i + c + 3)
                nc.scalar.activation(sb[:, par, c], sb[:, par, c], ACT.Exp, scale=0.25).then_inc(s_exp, 1)

            def ot_out(i, first=False):
                act.wait_ge(pts_free, 4 * i + 6)
                if not first:
                    act.wait_ge(ob_mm, i)
                copy(ot[:], ps[:, 7, 0:SEQ]).then_inc(ot_sb, 1)

            q_out(0)
            q_out(1)
            exps(0, 0, 0)
            exps(0, 0, 1)
            q_out(2)
            pt_out(0)
            exps(1, 1, 0)
            ot_out(0, True)
            exps(1, 1, 1)
            with act.Fori(1, NI // 2 - 1) as u:
                for par in range(2):
                    i = 2 * u + par
                    q_out(i + 1)
                    pt_out(i - 1)
                    exps(i, par, 0)
                    ot_out(i - 1)
                    exps(i, par, 1)
            for i in (NI - 2, NI - 1):
                if i < NI - 1:
                    q_out(i + 1)
                pt_out(i - 1)
                exps(i, i % 2, 0)
                ot_out(i - 1)
                exps(i, i % 2, 1)
            pt_out(NI - 1)
            ot_out(NI - 1)

            def a_parts(u, s):
                t = 2 * u + s
                act.wait_ge(a_tr, t + 1)
                copy(aT[:, s, 0], heads(ps[:, s, :], 4)).then_inc(a_hi, 1)

            def a_copies(u, s):
                copy(heads(attc[:, s], HQ), att[:, bass.ds(u * HQ, HQ), s, :]).then_inc(a_copy, 1)

            def x1_parts(u, s):
                t = 2 * u + s
                act.wait_ge(x1_tr, t + 1)
                copy(x1T[:, 0, :, bass.ds(t * P, P)], heads(ps[:, 4 + s, :], 4)).then_inc(x1_hi, 1)
                copy(yacc[:, t], x1c[:, s]).then_inc(y_init, 1)

            act.sem_inc(y_init, 2)
            act.wait_ge(o_norm, NI)
            a_copies(0, 0)
            a_copies(0, 1)
            a_parts(0, 0)
            act.wait_ge(a_tr, 1)
            a_copies(1, 0)
            a_parts(0, 1)
            with act.Fori(1, NT // 2 - 1) as u:
                act.wait_ge(a_tr, 2 * u)
                a_copies(u, 1)
                a_parts(u, 0)
                x1_parts(u - 1, 0)
                act.wait_ge(a_tr, 2 * u + 1)
                a_copies(u + 1, 0)
                a_parts(u, 1)
                x1_parts(u - 1, 1)
            act.wait_ge(a_tr, NT - 2)
            a_copies(NT // 2 - 1, 1)
            for u in range(NT // 2 - 2, NT // 2):
                for s in range(2):
                    if u == NT // 2 - 2:
                        a_parts(u + 1, s)
                    x1_parts(u, s)

            def q_parts(g, j, nh):
                act.wait_ge(q_mm, 8 * g + 2 * j + nh + 1)
                sl = slice(nh * 512, nh * 512 + 512)
                nc.scalar.activation(sq[:, j % 2, sl], ps[:, nh, :], ACT.Square)
                copy(qT[:, j % 2, sl], ps[:, nh, :]).then_inc(q_free, 1)

            def xt_high(g, k):
                act.wait_ge(xt_mm, 4 * g + k + 1)
                copy(pT[:, 0, k // 2, 4 * (k % 2):4 * (k % 2) + 4, :], heads(ps[:, 4, :], 4)).then_inc(xt_hi, 1)

            def vw_high(g, b, p):
                act.wait_ge(vw_mm, 8 * g + 2 * b + p + 2)
                copy(vws[:, b % 2, 0, p], ps[:, 5 + p, :]).then_inc(vw_hi, 1)

            def exp_of(g, j):
                act.wait_ge(p_sub, XR * g + j + 1)
                p = prob[:, j // 2, :, j % 2, :]
                nc.scalar.activation(p, p, ACT.Exp).then_inc(p_exp, 1)

            def z_high(g):
                act.wait_ge(vw_mm, 8 * g + 1)
                copy(vpad[:, 0, :, XS:2 * XS], VTx[:, g, :].rearrange("p (b k) -> p b k", b=B)).then_inc(z_hi, 1)

            def group(g, one, two):
                if two:
                    z_high(g - 1)
                for n in range(4):
                    if one:
                        q_parts(g, n // 2, n % 2)
                    if two:
                        if n == 2:
                            exp_of(g - 1, 3)
                        xt_high(g - 1, n)
                if two:
                    vw_high(g - 1, 0, 0)
                    vw_high(g - 1, 0, 1)
                if one:
                    exp_of(g, 0)
                    q_parts(g, 2, 0)
                if two:
                    vw_high(g - 1, 1, 0)
                if one:
                    q_parts(g, 2, 1)
                if two:
                    vw_high(g - 1, 1, 1)
                    vw_high(g - 1, 2, 0)
                if one:
                    q_parts(g, 3, 0)
                    exp_of(g, 1)
                if two:
                    vw_high(g - 1, 2, 1)
                if one:
                    q_parts(g, 3, 1)
                if two:
                    vw_high(g - 1, 3, 0)
                    vw_high(g - 1, 3, 1)
                if one:
                    exp_of(g, 2)

            act.wait_ge(z_zero, 1)
            group(0, True, False)
            with act.Fori(1, XG) as g:
                group(g, True, True)
            group(XG, False, True)

            with act.Fori(0, NT // 2) as u:
                for s in range(2):
                    t = 2 * u + s
                    act.wait_ge(f_tr, t + 1)
                    copy(x2T[:, s, 0], heads(ps[:, s, :], 4)).then_inc(f_hi, 1)
                    act.wait_ge(g_mm, t + 1)
                    copy(gl[:, t], ps[:, 2 + s, 0:NE + P]).then_inc(g_sb, 1)
            act.wait_ge(r_step, 8)
            nc.scalar.activation(wts[:, 2], wts[:, 2], ACT.Exp).then_inc(r_exp, 1)
            with act.Fori(0, NT // 2) as u:
                for s in range(2):
                    t = 2 * u + s
                    act.wait_ge(l_tr, t + 1)
                    copy(lowT[:, s], ps[:, s, 0:P]).then_inc(l_sb, 1)

        @block.vector
        def _(dve):
            tt = nc.vector.tensor_tensor

            def high(hi, raw):
                return nc.vector.tensor_copy(hi, raw)

            def stats(src, at6, at2, step, n):
                nc.vector.bn_stats(small[:, at6:at6 + 6], src).then_inc(step, 1)
                dve.wait_ge(step, n + 1)
                dve.sem_inc(dve_passed, 1)
                nc.vector.bn_aggr(small[:, at2:at2 + 2], small[:, at6:at6 + 6]).then_inc(step, 1)
                dve.wait_ge(step, n + 2)

            dve.sem_inc(qkv_free, 6)
            dve.sem_inc(s_free, 2)
            dve.sem_inc(vw_free, 2)
            for started in (rope_done, xt_lo, y_add):
                dve.sem_inc(started, 1)
            dve.wait_ge(d_const, 16 * NCONST)
            nc.vector.tensor_scalar(wqk[:], wqn[:], wkn[:, 0:1], XD ** -0.5, ALU.mult, ALU.mult).then_inc(dve_consts, 1)
            nc.vector.tensor_copy(causb[:], causf[:]).then_inc(dve_consts, 1)
            nc.vector.tensor_scalar(diagb[:], identf[:], MASK_A, None, ALU.mult).then_inc(dve_consts, 1)
            dve.wait_ge(d_ctx, 16)
            high(ctxs[:, 0], ctxraw[:]).then_inc(ctx_hi, 1)

            def kv_high(n):
                dve.wait_ge(d_kv[n], 16)
                high(kvs[:, n % 2, 0], kvraw[:, n]).then_inc(kv_hi, 1)

            def key_ms(u):
                dve.wait_ge(k_sq, 4 * u + 4)
                nc.vector.tensor_scalar(small[:, 16 + 4 * u:20 + 4 * u], small[:, 4 * u:4 * u + 4], 1.0 / XD, EPS,
                                        ALU.mult, ALU.add).then_inc(k_ms, 1)

            def key_scale(u):
                dve.wait_ge(k_r, u + 1)
                if u >= 2:
                    dve.wait_ge(k_tr, u - 1)
                tt(heads(knat[:, u % 2], 4), heads(ps[:, u, :], 4), over(small[:, 32 + 4 * u:36 + 4 * u], XD),
                   ALU.mult).then_inc(k_nat, 1)

            kv_high(0)
            kv_high(1)
            dve.wait_ge(k_mm, 2)
            kv_high(2)
            dve.wait_ge(k_mm, 4)
            kv_high(3)

            def w_high(n):
                dve.wait_ge(d_w[n], 16)
                high(ws[:, 0, n], wraw[:, n]).then_inc(w_hi, 1)

            def x_high(u, s):
                dve.wait_ge(d_x[s], 16 * u + 16)
                high(xs[:, s, 0], xraw[:, s]).then_inc(x_hi, 1)

            w_high(0)
            x_high(0, 0)
            x_high(0, 1)
            w_high(1)
            w_high(2)
            for u in range(4):
                key_ms(u)
            for v in range(4):
                dve.wait_ge(v_mm, v + 1)
                nc.vector.tensor_copy(VTx[:, 2 * v:2 * v + 2], heads(ps[:, 6 + v % 2, :], 2)).then_inc(v_done, 1)
            for u in range(4):
                key_scale(u)

            dve.wait_ge(kv_lo, 4)
            def project(u, s, more):
                t = 2 * u + s
                dve.wait_ge(rope_done, 2 * t + 1)
                for n in range(2):
                    dve.wait_ge(qkv_mm, 3 * t + n + 1)
                    tt(qraw[:, n], ps[:, 3 * s + n, :], qkvbs[:, n], ALU.add).then_inc(qkv_free, 1)
                dve.wait_ge(qkv_mm, 3 * t + 3)
                tt(vx[:, bass.ds(u * HQ, HQ), s, :, 0:D],
                   ps[:, 3 * s + 2, :].rearrange("p (a j d) -> p a j d", a=HQ, j=4),
                   qkvbs[:, 2].rearrange("p (a j d) -> p a j d", a=HQ, j=4), ALU.add).then_inc(qkv_free, 1)
                dve.wait_ge(qkv_free, 3 * t + 8)
                raw = qraw[:].rearrange("p n (h d) -> p (n h) d", d=D)
                rot = qrot[:].rearrange("p n (h d) -> p (n h) d", d=D)
                for a in range(2):
                    half = slice((1 - a) * D // 2, (2 - a) * D // 2)
                    own = slice(a * D // 2, (a + 1) * D // 2)
                    sin = ropes[:, s, 1, own].unsqueeze(1).broadcast_to([P, 2 * H, D // 2])
                    tt(rot[:, :, own], raw[:, :, half], sin, ALU.mult).then_inc(rope_step, 1)
                dve.wait_ge(rope_step, 4 * t + 2)
                for n in range(2):
                    cos = ropes[:, s, 0, :].unsqueeze(1).broadcast_to([P, H, D])
                    tt(qraw[:, n].rearrange("p (h d) -> p h d", d=D),
                       qraw[:, n].rearrange("p (h d) -> p h d", d=D), cos, ALU.mult).then_inc(rope_step, 1)
                dve.wait_ge(rope_step, 4 * t + 4)
                for n in range(2):
                    tt(qk[:, bass.ds(u * HQ, HQ), s, n, :], heads(qraw[:, n], HQ), heads(qrot[:, n], HQ),
                       ALU.add).then_inc(rope_done, 1)
                if more:
                    x_high(u + 1, s)

            with dve.Fori(0, NT // 2 - 1) as u:
                for s in range(2):
                    dve.wait_ge(x_lo, 2 * u + s + 1)
                    project(u, s, True)
            for s in range(2):
                project(NT // 2 - 1, s, False)

            def k_out(i):
                dve.wait_ge(tr_k, i + 2)
                nc.vector.tensor_copy(qkt[:, 1].rearrange("p a b -> p (a b)"), ps[:, 1, :]).then_inc(kt_ready, 1)

            def less_max(i, par, c):
                s4 = ps[:, 2 + 2 * c:4 + 2 * c, :].rearrange("p r (j k) -> p r j k", j=2)
                top = heads(small[:, 112 + 4 * c:116 + 4 * c], 2)
                dve.wait_ge(s_mm, 2 * i + c + 1)
                nc.vector.tensor_reduce(top, s4, AX.X, ALU.max).then_inc(s_max, 1)
                dve.wait_ge(s_max, 2 * i + c + 1)
                tt(sb[:, par, c].rearrange("p (j r) k -> p r j k", r=2), s4, over(top, SEQ), ALU.subtract
                   ).then_inc(s_free, 1)

            def norm_out(i):
                o = ps[:, 7, SEQ:].rearrange("p (h d) -> p h d", d=2 * D)
                dve.wait_ge(ob_mm, i + 1)
                nc.vector.reciprocal(small[:, 120:128], o[:, :, D]).then_inc(o_rec, 1)
                dve.wait_ge(o_rec, i + 1)
                tt(att[:, i].rearrange("p c (j d) -> p (c j) d", d=D), o[:, :, 0:D], over(small[:, 120:128], D),
                   ALU.mult).then_inc(o_norm, 1)

            k_out(0)
            less_max(0, 0, 0)
            k_out(1)
            less_max(0, 0, 1)
            less_max(1, 1, 0)
            k_out(2)
            less_max(1, 1, 1)
            with dve.Fori(1, NI // 2 - 1) as u:
                for par in range(2):
                    i = 2 * u + par
                    less_max(i, par, 0)
                    norm_out(i - 2)
                    k_out(i + 1)
                    less_max(i, par, 1)
            less_max(NI - 2, 0, 0)
            norm_out(NI - 4)
            k_out(NI - 1)
            less_max(NI - 2, 0, 1)
            less_max(NI - 1, 1, 0)
            norm_out(NI - 3)
            less_max(NI - 1, 1, 1)
            norm_out(NI - 2)
            dve.wait_ge(d_wo, 16)
            high(wos[:, 0], woraw[:]).then_inc(wo_hi, 1)
            norm_out(NI - 1)

            dve.sem_inc(x1_free, 2)

            def a_low(t, s):
                dve.wait_ge(a_hi, t + 1)
                tt(aT[:, s, 1], heads(ps[:, s, :], 4), aT[:, s, 0].bitcast(F32), ALU.subtract).then_inc(a_lo, 1)

            def x1_low(t, s):
                dve.wait_ge(x1_hi, t + 1)
                own = bass.ds(t * P, P)
                tt(x1T[:, 1, :, own], heads(ps[:, 4 + s, :], 4), x1T[:, 0, :, own].bitcast(F32),
                   ALU.subtract).then_inc(x1_free, 1)

            def layer1(t, s):
                dve.wait_ge(o_mm, t + 1)
                dve.wait_ge(o_res, t + 1)
                tt(ro[:, s], ps[:, 2 + s, :], xres[:, s], ALU.add).then_inc(o_sum, 1)
                dve.wait_ge(o_sum, t + 1)
                stats(ro[:, s], 128 + 6 * s, 140 + 2 * s, o_stat, 2 * t)
                nc.vector.tensor_scalar(small[:, 62 + s:63 + s], small[:, 141 + 2 * s:142 + 2 * s], EPS, None,
                                        ALU.add).then_inc(o_ve, 1)
                dve.wait_ge(o_rstd, t + 1)
                dve.wait_ge(y_init, t + 1)
                nc.vector.tensor_scalar(x1c[:, s], ro[:, s], small[:, 140 + 2 * s:141 + 2 * s],
                                        small[:, 64 + s:65 + s], ALU.subtract, ALU.mult).then_inc(x1_done, 1)

            a_low(0, 0)
            a_low(1, 1)
            layer1(0, 0)
            with dve.Fori(1, NT // 2) as u:
                a_low(2 * u, 0)
                layer1(2 * u - 1, 1)
                x1_low(2 * u - 2, 0)
                a_low(2 * u + 1, 1)
                layer1(2 * u, 0)
                x1_low(2 * u - 1, 1)
            layer1(NT - 1, 1)
            x1_low(NT - 2, 0)
            x1_low(NT - 1, 1)

            def wq_high(g, j):
                dve.wait_ge(d_wq[j], 16 * g + 16)
                high(wqs[:, j, 0], wqraw[:, j]).then_inc(wq_hi, 1)

            def wx_high(g, j):
                dve.wait_ge(d_wx[j], 16 * g + 16)
                high(wxs[:, j, 0], wxraw[:, j]).then_inc(wx_hi, 1)

            def mean_square(g, j):
                dve.wait_ge(n_mm, XR * g + j + 1)
                nc.vector.tensor_scalar(small[:, 72:80], ps[:, 3, 0:8], 1.0 / XD, EPS, ALU.mult, ALU.add
                                        ).then_inc(n_sb, 1)

            def scores_out(g, j):
                dve.wait_ge(sx_mm, XR * g + j + 1)
                dve.wait_ge(n_r, XR * g + j + 1)
                tt(prob[:, j // 2, :, j % 2, :], heads(ps[:, 2, :], 8), over(small[:, 80:88], XS), ALU.mult
                   ).then_inc(p_scaled, 1)

            def row_max(g, j):
                dve.wait_ge(p_masked, XR * g + j + 1)
                nc.vector.tensor_reduce(small[:, 88:96], prob[:, j // 2, :, j % 2, :], AX.X, ALU.max
                                        ).then_inc(p_max, 1)

            def row_sum(g, j):
                dve.wait_ge(p_exp, XR * g + j + 1)
                nc.vector.tensor_reduce(small[:, 96:104], prob[:, j // 2, :, j % 2, :], AX.X, ALU.add
                                        ).then_inc(p_sum, 1)
                dve.wait_ge(p_sum, XR * g + j + 1)
                nc.vector.reciprocal(small[:, 104:112], small[:, 96:104]).then_inc(p_rec, 1)

            def xt_low(g, k):
                dve.wait_ge(xt_hi, 4 * g + k + 1)
                own = slice(4 * (k % 2), 4 * (k % 2) + 4)
                tt(pT[:, 1, k // 2, own, :], heads(ps[:, 4, :], 4), pT[:, 0, k // 2, own, :].bitcast(F32),
                   ALU.subtract).then_inc(xt_lo, 1)

            def vw_low(g, b, p):
                dve.wait_ge(vw_hi, 8 * g + 2 * b + p + 1)
                tt(vws[:, b % 2, 1, p], ps[:, 5 + p, :], vws[:, b % 2, 0, p].bitcast(F32), ALU.subtract
                   ).then_inc(vw_free, 1)

            def y_sum(g, b, c):
                dve.wait_ge(y_mm, 8 * g + 2 * b + c + 1)
                tt(yacc[:, 2 * b + c], ps[:, 7, :], yacc[:, 2 * b + c], ALU.add).then_inc(y_add, 1)

            def group(g, one, two, more):
                if two:
                    dve.wait_ge(vw_mm, 8 * g - 7)
                    wx_high(g - 1, 0)
                    wx_high(g - 1, 1)
                    scores_out(g - 1, 3)
                    wx_high(g - 1, 2)
                    wx_high(g - 1, 3)
                    row_max(g - 1, 3)
                    xt_low(g - 1, 0)
                    xt_low(g - 1, 1)
                    row_sum(g - 1, 3)
                if more:
                    dve.wait_ge(q_mm, 8 * g + 2)
                    wq_high(g + 1, 0)
                if two:
                    xt_low(g - 1, 2)
                    xt_low(g - 1, 3)
                if more:
                    dve.wait_ge(q_mm, 8 * g + 4)
                    wq_high(g + 1, 1)
                if one:
                    mean_square(g, 0)
                if two:
                    vw_low(g - 1, 0, 0)
                if one:
                    scores_out(g, 0)
                if two:
                    vw_low(g - 1, 0, 1)
                if one:
                    row_max(g, 0)
                if two:
                    vw_low(g - 1, 1, 0)
                    y_sum(g - 1, 0, 0)
                if one:
                    row_sum(g, 0)
                if two:
                    vw_low(g - 1, 1, 1)
                    y_sum(g - 1, 0, 1)
                if more:
                    dve.wait_ge(q_mm, 8 * g + 6)
                    wq_high(g + 1, 2)
                if one:
                    mean_square(g, 1)
                if two:
                    vw_low(g - 1, 2, 0)
                if one:
                    scores_out(g, 1)
                if two:
                    y_sum(g - 1, 1, 0)
                if one:
                    row_max(g, 1)
                if two:
                    vw_low(g - 1, 2, 1)
                    y_sum(g - 1, 1, 1)
                if one:
                    row_sum(g, 1)
                if more:
                    dve.wait_ge(q_mm, 8 * g + 8)
                    wq_high(g + 1, 3)
                if two:
                    vw_low(g - 1, 3, 0)
                    y_sum(g - 1, 2, 0)
                if one:
                    mean_square(g, 2)
                if two:
                    vw_low(g - 1, 3, 1)
                if one:
                    scores_out(g, 2)
                if two:
                    y_sum(g - 1, 2, 1)
                if one:
                    row_max(g, 2)
                if two:
                    y_sum(g - 1, 3, 0)
                if one:
                    row_sum(g, 2)
                if two:
                    y_sum(g - 1, 3, 1)
                if one:
                    mean_square(g, 3)

            for j in range(XR):
                wq_high(0, j)
            dve.wait_ge(y_init, NT + 2)
            group(0, True, False, True)
            with dve.Fori(1, XG - 1) as g:
                group(g, True, True, True)
            group(XG - 1, True, True, False)
            dve.wait_ge(q_mm, 8 * XG)
            dve.wait_ge(d_f, 64)
            high(bases[:, 0], baseraw[:]).then_inc(b_hi, 1)
            high(gas[:, 0], garaw[:]).then_inc(b_hi, 1)
            group(XG, False, True, False)

            def layer2(t, s):
                stats(yacc[:, t], 144 + 6 * s, 156 + 2 * s, f_stat, 2 * t)
                nc.vector.tensor_scalar(small[:, 160 + s:161 + s], small[:, 157 + 2 * s:158 + 2 * s], EPS, None,
                                        ALU.add).then_inc(f_ve, 1)
                dve.wait_ge(f_rstd, t + 1)
                nc.vector.tensor_scalar(x2c[:, s], yacc[:, t], small[:, 156 + 2 * s:157 + 2 * s],
                                        small[:, 162 + s:163 + s], ALU.subtract, ALU.mult).then_inc(f_x2, 1)

            def x2_low(t, s):
                dve.wait_ge(f_hi, t + 1)
                tt(x2T[:, s, 1], heads(ps[:, s, :], 4), x2T[:, s, 0].bitcast(F32), ALU.subtract).then_inc(f_lo, 1)

            def base_sum(t, s):
                dve.wait_ge(f_mm, t + 1)
                dve.wait_ge(f_bias, t + 1)
                tt(yacc[:, t], ps[:, 4 + s, :], x2b[:, s], ALU.add).then_inc(z_sum, 1)

            dve.wait_ge(y_add, 8 * XG + 1)
            layer2(0, 0)
            x2_low(0, 0)
            layer2(1, 1)
            base_sum(0, 0)
            with dve.Fori(1, NT // 2) as u:
                x2_low(2 * u - 1, 1)
                layer2(2 * u, 0)
                base_sum(2 * u - 1, 1)
                x2_low(2 * u, 0)
                layer2(2 * u + 1, 1)
                base_sum(2 * u, 0)
            x2_low(NT - 1, 1)
            base_sum(NT - 1, 1)

            logits = gl[:, :, 0:NE]
            rank = orders[:].unsqueeze(1).broadcast_to([P, NT, NE])
            one, two = route[:, 1], route[:, 4]
            steps = [0]

            def then(ins):
                ins.then_inc(r_step, 1)
                steps[0] += 1
                dve.wait_ge(r_step, steps[0])

            dve.wait_ge(g_sb, NT)
            then(nc.vector.tensor_reduce(wts[:, 0], logits, AX.X, ALU.max))
            then(tt(route[:, 0], logits, over(wts[:, 0], NE), ALU.is_equal))
            then(tt(route[:, 0], route[:, 0], rank, ALU.mult))
            then(nc.vector.tensor_reduce(wts[:, 1], route[:, 0], AX.X, ALU.max))
            then(tt(one, route[:, 0], over(wts[:, 1], NE), ALU.is_equal))
            then(nc.vector.scalar_tensor_tensor(out=route[:, 2], in0=one, scalar=-3e38, in1=logits,
                                                op0=ALU.mult, op1=ALU.add))
            then(nc.vector.tensor_reduce(wts[:, 3], route[:, 2], AX.X, ALU.max))
            then(tt(wts[:, 2], wts[:, 3], wts[:, 0], ALU.subtract))
            then(tt(route[:, 3], route[:, 2], over(wts[:, 3], NE), ALU.is_equal))
            then(tt(route[:, 3], route[:, 3], rank, ALU.mult))
            then(nc.vector.tensor_reduce(wts[:, 1], route[:, 3], AX.X, ALU.max))
            then(tt(two, route[:, 3], over(wts[:, 1], NE), ALU.is_equal))
            dve.wait_ge(r_exp, 1)
            then(nc.vector.tensor_scalar(wts[:, 4], wts[:, 2], 1.0, None, ALU.add))
            then(nc.vector.reciprocal(wts[:, 5], wts[:, 4]))
            then(nc.vector.tensor_scalar(wts[:, 6], wts[:, 5], 2.0, None, ALU.mult))
            then(tt(wts[:, 7], wts[:, 6], wts[:, 2], ALU.mult))
            then(tt(one, one, over(wts[:, 6], NE), ALU.mult))
            then(tt(two, two, over(wts[:, 7], NE), ALU.mult))
            then(tt(route[:, 5], one, two, ALU.add))

            def weigh(t, s):
                tt(heads(lowm[:, s], NE), heads(gl[:, t, NE:], NE), over(route[:, 5, t, :], R), ALU.mult
                   ).then_inc(l_low, 1)

            def layer3(u, s):
                t = 2 * u + s
                dve.wait_ge(l_mm, t + 1)
                tt(fo[:, s], ps[:, 2 + s, :], yacc[:, t], ALU.add).then_inc(h_sum, 1)
                dve.wait_ge(h_sum, t + 1)
                stats(fo[:, s], 168 + 6 * s, 184 + 2 * s, h_stat, 2 * t)
                nc.vector.tensor_scalar(small[:, 180 + s:181 + s], small[:, 185 + 2 * s:186 + 2 * s], EPS, None,
                                        ALU.add).then_inc(h_ve, 1)
                dve.wait_ge(h_rstd, t + 1)
                dve.wait_ge(d_out[s], 16 * u)
                nc.vector.tensor_scalar(fout[:, s], fo[:, s], small[:, 184 + 2 * s:185 + 2 * s],
                                        small[:, 182 + s:183 + s], ALU.subtract, ALU.mult).then_inc(h_out, 1)

            weigh(0, 0)
            weigh(1, 1)
            layer3(0, 0)
            weigh(2, 0)
            layer3(0, 1)
            with dve.Fori(1, NT // 2 - 1) as u:
                weigh(2 * u + 1, 1)
                layer3(u, 0)
                weigh(2 * u + 2, 0)
                layer3(u, 1)
            weigh(NT - 1, 1)
            layer3(NT // 2 - 1, 0)
            layer3(NT // 2 - 1, 1)

        @block.tensor
        def _(pe):
            mm = nc.tensor.matmul

            def product(dst, left, right):
                n = [(k, a, b) for k in range(KC) for a, b in PASSES]
                for at_, (k, a, b) in enumerate(n):
                    last = mm(dst, left(a, k), right(b, k), start=at_ == 0, stop=at_ == len(n) - 1)
                return last

            def turn(dst, src):
                return nc.tensor.transpose(dst, src, identf[:])

            pe.sem_inc(pts_free, 2)
            pe.sem_inc(tr_k, 1)
            pe.sem_inc(vw_mm, 1)
            pe.wait_ge(ctx_lo, 1)
            for n in range(2):
                pe.wait_ge(kv_lo, n + 1)
                for t in range(2):
                    product(ps[:, 2 * n + t, :], lambda a, k: ctxs[:, a, k, t * P:(t + 1) * P],
                            lambda b, k: kvs[:, n, b, k, :]).then_inc(k_mm, 1)
            for v in range(4):
                pe.wait_ge(kv_lo, 3 + v // 2)
                if v >= 2:
                    pe.wait_ge(v_done, v - 1)
                for g in range(2):
                    own = slice((2 * (v % 2) + g) * XD, (2 * (v % 2) + g + 1) * XD)
                    last = product(ps[:, 6 + v % 2, g * B * XS:(g + 1) * B * XS],
                                   lambda a, k: kvs[:, v // 2, a, k, own], lambda b, k: ctxs[:, b, k, :])
                last.then_inc(v_mm, 1)
            pe.wait_ge(d_const, 16 * NCONST)
            for u in range(4):
                pe.wait_ge(k_nat, u + 1)
                if u >= 2:
                    pe.wait_ge(k_done, u - 1)
                for g in range(4):
                    last = turn(ps[:, 4 + u % 2, g * P:(g + 1) * P], knat[:, u % 2, g * XD:(g + 1) * XD])
                last.then_inc(k_tr, 1)

            pe.wait_ge(k_done, 4)
            with pe.Fori(0, NT // 2) as u:
                for s in range(2):
                    t = 2 * u + s
                    pe.wait_ge(x_lo, t + 1)
                    for n in range(3):
                        pe.wait_ge(w_lo, n + 1)
                        pe.wait_ge(qkv_free, 3 * t + n + 1)
                        product(ps[:, 3 * s + n, :], lambda a, k: xs[:, s, a, k, :],
                                lambda b, k: ws[:, b, n, k, :]).then_inc(qkv_mm, 1)

            def turn_qk(i):
                pe.wait_ge(packed, 2 * i + 2)
                for a, done in ((0, tr_q), (1, tr_k)):
                    for p in range(2):
                        for c in range(2):
                            last = turn(ps[:, a, (2 * p + c) * P:(2 * p + c + 1) * P],
                                        pack[:, a, c, 2 * p:2 * p + 2, :].rearrange("p j d -> p (j d)"))
                    last.then_inc(done, 1)

            def scores(i):
                pe.wait_ge(qt_ready, i + 1)
                pe.wait_ge(kt_ready, i + 1)
                for c in range(2):
                    pe.wait_ge(s_free, 2 * i + c + 1)
                    for r in range(2):
                        mm(heads(ps[:, 2 + 2 * c + r, :], 2), diagb[:],
                           causb[:, c, :].unsqueeze(1).broadcast_to([P, 2, SEQ]), start=True, stop=False)
                    for j in range(4):
                        own = slice(64 * (j % 2), 64 * (j % 2) + 3 * D)
                        last = mm(ps[:, 2 + 2 * c + j % 2, (j // 2) * SEQ:(j // 2 + 1) * SEQ],
                                  qkt[own, 0, j // 2, c * P:(c + 1) * P], qkt[own, 1, j // 2, :],
                                  start=False, stop=j >= 2)
                    last.then_inc(s_mm, 1)

            def values(i, par, first=False, last_two=False):
                def pv(j):
                    pe.wait_ge(pt_sb, 4 * i + j + 1)
                    for kc in range(2):
                        last = mm(ps[32 * j:32 * j + 2 * D, 7, 0:SEQ], vst[:, par, kc, j, :],
                                  pts[:, j % 2, kc * SEQ:(kc + 1) * SEQ], start=kc == 0, stop=kc == 1)
                    last.then_inc(pts_free, 1)

                pe.wait_ge(s_exp, 2 * i + 2)
                for j in range(4):
                    if j == 1:
                        pe.wait_ge(qt_ready, NI if last_two else i + 3)
                    elif j:
                        pe.wait_ge(pt_sb, 4 * i + j - 1)
                    for kc in range(2):
                        for c in range(2):
                            last = turn(ps[:, pt_bank(j), (2 * kc + c) * P:(2 * kc + c + 1) * P],
                                        sb[:, par, c, j, kc * P:(kc + 1) * P])
                    last.then_inc(pt_mm, 1)
                    if j == 1:
                        pe.wait_ge(v_ready, i + 2)
                        if not first:
                            pe.wait_ge(o_norm, i)
                    if j:
                        pv(j - 1)
                pv(3)

            def turn_out(i):
                pe.wait_ge(ot_sb, i + 1)
                for c in range(2):
                    last = turn(ps[:, 7, SEQ + c * P:SEQ + (c + 1) * P], ot[:, c * P:(c + 1) * P])
                last.then_inc(ob_mm, 1)

            turn_qk(0)
            scores(0)
            turn_qk(1)
            scores(1)
            turn_qk(2)
            values(0, 0, True)
            with pe.Fori(1, NI // 2 - 1) as u:
                for par in range(2):
                    i = 2 * u + par
                    scores(i)
                    turn_out(i - 2)
                    turn_qk(i + 1)
                    values(i - 1, 1 - par)
            scores(NI - 2)
            turn_out(NI - 4)
            turn_qk(NI - 1)
            values(NI - 3, 1)
            scores(NI - 1)
            turn_out(NI - 3)
            values(NI - 2, 0, last_two=True)
            turn_out(NI - 2)
            values(NI - 1, 1, last_two=True)
            turn_out(NI - 1)

            def turn_att(t, s):
                pe.wait_ge(a_copy, t + 1)
                for k in range(KC):
                    last = turn(ps[:, s, k * P:(k + 1) * P], attc[:, s, k * P:(k + 1) * P])
                last.then_inc(a_tr, 1)

            def out_product(t, s):
                pe.wait_ge(a_lo, t + 1)
                product(ps[:, 2 + s, :], lambda a, k: aT[:, s, a, k, :], lambda b, k: wos[:, b, k, :]
                        ).then_inc(o_mm, 1)

            def turn_x1(t, s):
                pe.wait_ge(x1_done, t + 1)
                pe.wait_ge(x1_free, t + 1)
                for k in range(KC):
                    last = turn(ps[:, 4 + s, k * P:(k + 1) * P], x1c[:, s, k * P:(k + 1) * P])
                last.then_inc(x1_tr, 1)

            turn_att(0, 0)
            pe.wait_ge(wo_lo, 1)
            turn_att(1, 1)
            out_product(0, 0)
            with pe.Fori(1, NT // 2) as u:
                turn_att(2 * u, 0)
                out_product(2 * u - 1, 1)
                turn_x1(2 * u - 2, 0)
                turn_att(2 * u + 1, 1)
                out_product(2 * u, 0)
                turn_x1(2 * u - 1, 1)
            out_product(NT - 1, 1)
            turn_x1(NT - 2, 0)
            turn_x1(NT - 1, 1)

            def queries(g, j, nh):
                pe.wait_ge(wq_lo, XR * g + j + 1)
                pe.wait_ge(q_free, 8 * g + 2 * j + nh + 1)
                product(ps[:, nh, :], lambda a, k: wqs[:, j, a, k, :],
                        lambda b, k: x1T[:, b, k, nh * 512:(nh + 1) * 512]).then_inc(q_mm, 1)

            def norms_scores(g, j):
                h = XR * g + j
                pe.wait_ge(q_free, 8 * g + 2 * j + 4)
                pe.wait_ge(p_scaled, h)
                for t in range(NT):
                    last = mm(ps[:, 3, t:t + 1], sq[:, j % 2, t * P:(t + 1) * P], ones[:], start=True, stop=True)
                last.then_inc(n_mm, 1)
                for t in range(NT):
                    last = mm(ps[:, 2, t * XS:(t + 1) * XS], qT[:, j % 2, t * P:(t + 1) * P],
                              KTx[:, g, t // 2 * XS:(t // 2 + 1) * XS], start=True, stop=True)
                last.then_inc(sx_mm, 1)

            def turn_probs(g, k):
                pe.wait_ge(p_norm, XR * g + 2 * (k // 2) + 2)
                pe.wait_ge(xt_lo, 4 * g + k + 1)
                for q in range(4):
                    t = 4 * (k % 2) + q
                    last = turn(ps[:, 4, q * P:(q + 1) * P],
                                prob[:, k // 2, t].rearrange("p h k -> p (h k)"))
                last.then_inc(xt_mm, 1)

            def values_out(g, b, p):
                pe.wait_ge(z_lo, g + 1)
                pe.wait_ge(wx_lo, XR * g + 2 * p + 2)
                pe.wait_ge(vw_free, 8 * g + 2 * b + p + 1)
                n = [(h, a, w) for h in range(2) for a, w in PASSES]
                for i, (h, a, w) in enumerate(n):
                    last = mm(ps[:, 5 + p, :], vpad[:, a, b, XS - h * XS:3 * XS - h * XS], wxs[:, 2 * p + h, w, :],
                              start=i == 0, stop=i == 5)
                last.then_inc(vw_mm, 1)

            def outputs(g, b, c):
                pe.wait_ge(xt_lo, 4 * g + 5)
                pe.wait_ge(vw_free, 8 * g + 2 * b + 4)
                pe.wait_ge(y_add, 8 * g + 2 * b + c + 1)
                n = [(p, a, w) for p in range(2) for a, w in PASSES]
                for i, (p, a, w) in enumerate(n):
                    last = mm(ps[:, 7, :], pT[:, a, p, 2 * b + c, :], vws[:, b % 2, w, p, :],
                              start=i == 0, stop=i == 5)
                last.then_inc(y_mm, 1)

            def group(g, one, two):
                for n in range(4):
                    if one:
                        queries(g, n // 2, n % 2)
                    if two:
                        turn_probs(g - 1, n)
                if one:
                    norms_scores(g, 0)
                if two:
                    values_out(g - 1, 0, 0)
                    values_out(g - 1, 0, 1)
                if one:
                    queries(g, 2, 0)
                if two:
                    values_out(g - 1, 1, 0)
                    outputs(g - 1, 0, 0)
                if one:
                    queries(g, 2, 1)
                if two:
                    values_out(g - 1, 1, 1)
                    outputs(g - 1, 0, 1)
                if one:
                    norms_scores(g, 1)
                if two:
                    values_out(g - 1, 2, 0)
                    outputs(g - 1, 1, 0)
                if one:
                    queries(g, 3, 0)
                if two:
                    values_out(g - 1, 2, 1)
                    outputs(g - 1, 1, 1)
                if one:
                    queries(g, 3, 1)
                if two:
                    values_out(g - 1, 3, 0)
                    outputs(g - 1, 2, 0)
                if one:
                    norms_scores(g, 2)
                if two:
                    values_out(g - 1, 3, 1)
                    outputs(g - 1, 2, 1)
                    outputs(g - 1, 3, 0)
                    outputs(g - 1, 3, 1)
                if one:
                    norms_scores(g, 3)

            pe.wait_ge(x1_free, NT + 2)
            pe.wait_ge(consts_ready, 2)
            group(0, True, False)
            with pe.Fori(1, XG) as g:
                group(g, True, True)
            group(XG, False, True)

            def turn_x2(t, s):
                pe.wait_ge(f_x2, t + 1)
                for k in range(KC):
                    last = turn(ps[:, s, k * P:(k + 1) * P], x2c[:, s, k * P:(k + 1) * P])
                last.then_inc(f_tr, 1)

            def forward(t, s):
                pe.wait_ge(f_lo, t + 1)
                product(ps[:, 2 + s, 0:NE + P], lambda a, k: x2T[:, s, a, k, :], lambda b, k: gas[:, b, k, :]
                        ).then_inc(g_mm, 1)
                product(ps[:, 4 + s, :], lambda a, k: x2T[:, s, a, k, :], lambda b, k: bases[:, b, k, :]
                        ).then_inc(f_mm, 1)

            turn_x2(0, 0)
            pe.wait_ge(b_lo, 2)
            with pe.Fori(0, NT // 2 - 1) as u:
                forward(2 * u, 0)
                turn_x2(2 * u + 1, 1)
                forward(2 * u + 1, 1)
                turn_x2(2 * u + 2, 0)
            forward(NT - 2, 0)
            turn_x2(NT - 1, 1)
            forward(NT - 1, 1)
            pe.wait_ge(d_f, 64)
            with pe.Fori(0, NT // 2) as u:
                for s in range(2):
                    t = 2 * u + s
                    pe.wait_ge(l_low, t + 1)
                    turn(ps[:, s, 0:P], lowm[:, s]).then_inc(l_tr, 1)
                    pe.wait_ge(l_sb, t + 1)
                    mm(ps[:, 2 + s, :], lowT[:, s], lbs[:], start=True, stop=True).then_inc(l_mm, 1)


def tables(np):
    half = D // 2
    freq = (1.0 / np.float32(10000.0) ** (np.arange(half, dtype=np.float32) / np.float32(half))).astype(np.float32)
    ang = np.arange(SEQ, dtype=np.float32)[:, None] * freq[None, :]
    cos, sin = np.cos(ang), np.sin(ang)
    rope = np.stack([np.concatenate([cos, cos], -1), np.concatenate([-sin, sin], -1)], 1)
    rope = rope.reshape(2, P, 2, D).transpose(1, 0, 2, 3)
    query = np.arange(SEQ).reshape(2, P).T[:, :, None]
    causal = MASK_B * (np.arange(SEQ)[None, None, :] > query)
    return {"rope": rope, "ident": np.eye(P), "causal": causal, "order": np.arange(NE, 0, -1)}


def kernel(x, ctx_4096, mask_1x1xSxS2_ff0, L0_attn_qkv_w, L0_attn_qkv_b, L0_attn_out_w, L0_attn_out_b,
           L0_xattn_q_proj_w, L0_xattn_k_proj_w, L0_xattn_v_proj_w, L0_xattn_o_proj_w, L0_xattn_q_norm_w,
           L0_xattn_k_norm_w, L0_ffn_gate_w, L0_ffn_base_w, L0_ffn_base_b, L0_ffn_lora_A, L0_ffn_lora_B):
    import numpy as np
    import concourse.bacc as bacc
    from concourse.bass_utils import run_bass_kernel_spmd

    def chunks(w):
        return np.asarray(w).reshape(w.shape[0], -1, P).transpose(2, 1, 0)

    kw = np.asarray(L0_xattn_k_proj_w).reshape(2, 512, KC, P).transpose(0, 3, 2, 1)
    vw = np.asarray(L0_xattn_v_proj_w).reshape(2, 512, KC, P).transpose(0, 3, 2, 1)
    a = {
        "xT": np.asarray(x).reshape(NT, P, KC, P).transpose(0, 3, 2, 1),
        "x": np.asarray(x).reshape(NT, P, E),
        "ctxT": chunks(np.asarray(ctx_4096).reshape(B * XS, E)),
        "mask": np.asarray(mask_1x1xSxS2_ff0).reshape(SEQ, XS),
        "wqkv": L0_attn_qkv_w, "qkvb": L0_attn_qkv_b, "wout": L0_attn_out_w, "outb": L0_attn_out_b,
        "wqT": np.asarray(L0_xattn_q_proj_w).reshape(XH, XD, KC, P).transpose(0, 3, 2, 1),
        "wkT": kw, "wvT": vw,
        "woT": np.asarray(L0_xattn_o_proj_w).reshape(E, XH, XD).transpose(1, 2, 0),
        "qn": np.asarray(L0_xattn_q_norm_w).reshape(P, 1), "kn": np.asarray(L0_xattn_k_norm_w).reshape(P, 1),
        "gateT": chunks(L0_ffn_gate_w), "baseT": chunks(L0_ffn_base_w), "baseb": L0_ffn_base_b,
        "loraAT": chunks(np.asarray(L0_ffn_lora_A).reshape(NE * R, E)),
        "loraB": np.asarray(L0_ffn_lora_B).transpose(0, 2, 1).reshape(NE * R, E),
    }
    for name, table in tables(np).items():
        a[name] = np.asarray(table, np.float32)
    nc = bacc.Bacc("TRN2", target_bir_lowering=False, num_devices=1)
    arrays, aps = {}, {}
    for name, v in a.items():
        v = np.ascontiguousarray(v)
        arrays[f"in_{name}"] = v
        aps[name] = nc.dram_tensor(f"in_{name}", v.shape, mybir.dt.from_np(v.dtype), kind="ExternalInput").ap()
    aps["out"] = nc.dram_tensor("out_y", (NT, P, E), F32, kind="ExternalOutput").ap()
    decoder_layer(nc, **aps)
    r = run_bass_kernel_spmd(nc, [arrays], core_ids=[0])
    return r.results[0]["out_y"].reshape(B, SEQ, E)
```

```python
from contextlib import ExitStack

import concourse.bass as bass
from concourse import mybir

ALU = mybir.AluOpType
ACT = mybir.ActivationFunctionType
AX = mybir.AxisListType
F32 = mybir.dt.float32
F32R = mybir.dt.float32r
BF16 = mybir.dt.bfloat16

P = 128
B, SEQ, E = 4, 256, 512
NT = B * SEQ // P
KC = E // P
H, D = 32, 16
HQ = H // 4
NI = B * HQ
XH, XG, XD, XS = 32, 8, 128, 64
XR = XH // XG
NE, R = 8, 16
EPS = 1e-5
MASK_VAL = -66504.0
MASK_A, MASK_B = -1632.0, 163.0
KB = 1024
PASSES = ((0, 0), (0, 1), (1, 0))
assert MASK_A * MASK_B == 4 * MASK_VAL


def decoder_layer(nc, xT, x, ctxT, mask, wqkv, qkvb, wout, outb, wqT, wkT, wvT, woT, qn, kn,
                  gateT, baseT, baseb, loraAT, loraB, rope, ident, causal, order, out):
    with ExitStack() as ctx:
        base_at = 16512

        def at(name, kb, shape, dt):
            return nc.alloc_sbuf_tensor_at(name, shape, dt, offset=base_at + int(kb * KB))

        def sem(name):
            return ctx.enter_context(nc.semaphore(name))

        ps = ctx.enter_context(nc.psum_tensor("ps", [P, 8, 512], F32))

        KTx = at("KTx", 0, [P, XG, B * XS], F32)
        VTx = at("VTx", 8, [P, XG, B * XS], F32)
        c0 = 16
        identf = at("identf", c0, [P, P], F32)
        maskx = at("maskx", c0 + 0.5, [P, 2, XS], F32)
        outbs = at("outbs", c0 + 1, [P, E], F32)
        basebs = at("basebs", c0 + 3, [P, E], F32)
        causb = at("causb", c0 + 5, [P, 2, SEQ], BF16)
        diagb = at("diagb", c0 + 6, [P, P], BF16)
        ropes = at("ropes", c0 + 6.25, [P, 2, 2, D], F32)
        mhalf = at("mhalf", c0 + 6.5625, [P, 8], F32)
        wqn = at("wqn", c0 + 6.625, [P, 1], F32)
        wkn = at("wkn", c0 + 6.6875, [P, 1], F32)
        wqk = at("wqk", c0 + 6.75, [P, 1], F32)
        orders = at("orders", c0 + 6.8125, [P, NE], F32)
        small = at("small", c0 + 7, [P, 256], F32)
        junk = at("junk", 207, [P, P], F32)
        ones = at("ones", 207.5, [P, 32], F32)
        kvraw = at("kvraw", 142, [P, 4, KC, 512], F32)
        kvs = at("kvs", 174, [P, 2, 2, KC, 512], F32R)
        ctxs = at("ctxs", 110, [P, 2, KC, B * XS], F32R)
        ctxraw = at("ctxraw", 124, [P, KC, B * XS], F32)
        knat = at("knat", 128, [P, 2, 512], F32)
        wraw = at("wraw", 72, [P, 3, KC, 512], F32)
        ws = at("ws", 24, [P, 2, 3, KC, 512], F32R)
        xraw = at("xraw", 120, [P, 2, KC, P], F32)
        xs = at("xs", 132, [P, 2, 2, KC, P], F32R)
        qraw = at("qraw", 96, [P, 2, 512], F32)
        qrot = at("qrot", 100, [P, 2, 512], F32)
        qkvbs = at("qkvbs", 104, [P, 3, 512], F32)
        causf = at("causf", 118, [P, 2, SEQ], F32)
        qk = at("qk", 142, [P, NI, 2, 2, 64], F32)
        vx = at("vx", 174, [P, NI, 2, 4, D], F32)
        att = at("att", 191, [P, NI, 2, 64], F32)
        sb = at("sb", 104, [P, 2, 2, 4, SEQ], F32)
        pts = at("pts", 120, [P, 2, 512], F32)
        pack = at("pack", 84, [P, 2, 2, 4, 64], F32)
        qkt = at("qkt", 128, [P, 2, 2, SEQ], F32R)
        vst = at("vst", 140, [P, 2, 2, 4, 2 * D], F32)
        ot = at("ot", 138, [P, SEQ], F32)
        woraw = at("woraw", 72, [P, KC, 512], F32)
        wos = at("wos", 88, [P, 2, KC, 512], F32R)
        aT = at("aT", 80, [P, 2, 2, KC, P], F32R)
        attc = at("attc", 124, [P, 2, E], F32)
        x1c = at("x1c", 108, [P, 2, E], F32)
        ro = at("ro", 112, [P, 2, E], F32)
        xres = at("xres", 132, [P, 2, E], F32)
        yacc = at("yacc", 24, [P, NT, E], F32)
        x1T = at("x1T", 40, [P, 2, KC, B * SEQ], F32R)
        wqs = at("wqs", 72, [P, XR, 2, KC, P], F32R)
        wxs = at("wxs", 88, [P, XR, 2, E], F32R)
        vwa = at("vwa", 104, [P, 2, 2, 2, E], F32R)
        vwb = at("vwb", 191, [P, 2, 2, 2, E], F32R)
        pT = at("pT", 120, [P, 2, 2, 8, P], F32R)
        vsp = at("vsp", 136, [P, 2, B * XS], F32R)
        nrow = at("nrow", 138, [P, SEQ], F32)
        qT = at("qT", 142, [P, 2, B * SEQ], F32)
        sq = at("sq", 150, [P, 2, B * SEQ], F32)
        wqraw = at("wqraw", 158, [P, XR, KC, P], F32)
        wxraw = at("wxraw", 166, [P, XR, E], F32)
        prob = at("prob", 174, [P, 2, 8, 2, XS], F32)
        lbs = at("lbs", 182, [P, E], F32)
        baseraw = at("baseraw", 158, [P, KC, E], F32)
        garaw = at("garaw", 184, [P, KC, NE + P], F32)
        gas = at("gas", 186.5, [P, 2, KC, NE + P], F32R)
        bases = at("bases", 72, [P, 2, KC, E], F32R)
        x2c = at("x2c", 142, [P, 2, E], F32)
        x2T = at("x2T", 146, [P, 2, 2, KC, P], F32R)
        x2b = at("x2b", 154, [P, 2, E], F32)
        lowm = at("lowm", 191, [P, NT, P], F32)
        lowT = at("lowT", 195, [P, NT, P], F32)
        fo = at("fo", 160, [P, 2, E], F32)
        fout = at("fout", 164, [P, 2, E], F32)
        gl = at("gl", 168, [P, NT, NE + P], F32)
        route = at("route", 173, [P, 8, NT, NE], F32)
        wts = at("wts", 175, [P, 8, NT], F32)

        d_const, d_ctx, d_wo, d_f = map(sem, ("d_const", "d_ctx", "d_wo", "d_f"))
        d_out = [sem(f"d_out{n}") for n in range(2)]
        d_kv = [sem(f"d_kv{n}") for n in range(4)]
        d_w = [sem(f"d_w{n}") for n in range(3)]
        d_x = [sem(f"d_x{n}") for n in range(2)]
        d_xres = [sem(f"d_xres{n}") for n in range(2)]
        d_wq = [sem(f"d_wq{n}") for n in range(XR)]
        d_wx = [sem(f"d_wx{n}") for n in range(XR)]
        consts_ready, dve_consts = sem("consts_ready"), sem("dve_consts")
        ctx_hi, ctx_lo, kv_hi, kv_lo = map(sem, ("ctx_hi", "ctx_lo", "kv_hi", "kv_lo"))
        k_mm, k_sq, k_ms, k_r, k_nat, k_tr, k_done = map(
            sem, ("k_mm", "k_sq", "k_ms", "k_r", "k_nat", "k_tr", "k_done"))
        v_mm, v_done = sem("v_mm"), sem("v_done")
        w_hi, w_lo, x_hi, x_lo = map(sem, ("w_hi", "w_lo", "x_hi", "x_lo"))
        qkv_mm, qkv_free, rope_step, rope_done = map(sem, ("qkv_mm", "qkv_free", "rope_step", "rope_done"))
        pack_hi, packed, tr_q, tr_k, qt_ready, kt_ready = map(
            sem, ("pack_hi", "packed", "tr_q", "tr_k", "qt_ready", "kt_ready"))
        s_mm, s_max, s_free, s_exp = map(sem, ("s_mm", "s_max", "s_free", "s_exp"))
        v_ready, pt_mm, pt_sb, pts_free, ot_sb, ob_mm, o_rec, o_norm = map(
            sem, ("v_ready", "pt_mm", "pt_sb", "pts_free", "ot_sb", "ob_mm", "o_rec", "o_norm"))
        wo_hi, wo_lo, a_copy, a_tr, a_hi, a_lo, o_mm, o_res, o_sum = map(
            sem, ("wo_hi", "wo_lo", "a_copy", "a_tr", "a_hi", "a_lo", "o_mm", "o_res", "o_sum"))
        o_stat, o_ve, o_rstd, x1_done, x1_tr, x1_hi, x1_free, y_init = map(
            sem, ("o_stat", "o_ve", "o_rstd", "x1_done", "x1_tr", "x1_hi", "x1_free", "y_init"))
        wq_hi, wq_lo, wx_hi, wx_lo = map(sem, ("wq_hi", "wq_lo", "wx_hi", "wx_lo"))
        q_mm, q_free, n_mm, n_row, n_tr, sx_mm = map(sem, ("q_mm", "q_free", "n_mm", "n_row", "n_tr", "sx_mm"))
        n_sb, n_r, p_scaled, p_masked, p_max, p_sub, p_exp, p_sum, p_rec, p_norm = map(
            sem, ("n_sb", "n_r", "p_scaled", "p_masked", "p_max", "p_sub", "p_exp", "p_sum", "p_rec", "p_norm"))
        xt_mm, xt_hi, xt_lo, z_hi, z_lo = map(sem, ("xt_mm", "xt_hi", "xt_lo", "z_hi", "z_lo"))
        vw_mm, vw_hi, vw_free, y_mm, y_add = map(sem, ("vw_mm", "vw_hi", "vw_free", "y_mm", "y_add"))
        b_hi, b_lo, f_stat, f_ve, f_rstd, f_x2, f_tr, f_hi, f_lo, f_bias = map(
            sem, ("b_hi", "b_lo", "f_stat", "f_ve", "f_rstd", "f_x2", "f_tr", "f_hi", "f_lo", "f_bias"))
        f_mm, g_mm, g_sb, z_sum, r_step, r_exp = map(sem, ("f_mm", "g_mm", "g_sb", "z_sum", "r_step", "r_exp"))
        l_low, l_tr, l_sb, l_mm, h_sum, h_stat, h_ve, h_rstd, h_out = map(
            sem, ("l_low", "l_tr", "l_sb", "l_mm", "h_sum", "h_stat", "h_ve", "h_rstd", "h_out"))
        dve_passed, pool_passed = sem("dve_passed"), sem("pool_passed")
        NCONST = 10

        def over(ap, n):
            return ap.unsqueeze(len(ap.shape)).broadcast_to([*ap.shape, n])

        def heads(ap, n):
            return ap.rearrange("p (a b) -> p a b", a=n)

        def pt_bank(j):
            return (6, 0)[j % 2]

        def vws(b):
            return (vwa, vwb)[b // 2][:, b % 2]

        def y_bank(c):
            return (7, 4)[c]

        block = ctx.enter_context(nc.Block())

        @block.sync
        def _(sp):
            sp.dma_start(ctxraw[:], ctxT).then_inc(d_ctx, 16)
            for n in range(4):
                sp.dma_start(kvraw[:, n], (wkT, wvT)[n // 2][n % 2]).then_inc(d_kv[n], 16)
                if n == 0:
                    for dst, src in ((identf[:], ident), (maskx[:], mask.rearrange("(c p) k -> p c k", p=P)),
                                     (outbs[:], outb.partition_broadcast(P)),
                                     (basebs[:], baseb.partition_broadcast(P)),
                                     (qkvbs[:].rearrange("p a b -> p (a b)"), qkvb.partition_broadcast(P)),
                                     (ropes[:], rope), (wqn[:], qn), (wkn[:], kn),
                                     (orders[:], order.partition_broadcast(P)), (causf[:], causal)):
                        sp.dma_start(dst, src).then_inc(d_const, 16)
            for n in range(3):
                sp.dma_start(wraw[:, n], wqkv.rearrange("(k p) n -> p k n", p=P)[:, :, n * 512:(n + 1) * 512]
                             ).then_inc(d_w[n], 16)
                if n == 0:
                    for s in range(2):
                        sp.dma_start(xraw[:, s], xT[s]).then_inc(d_x[s], 16)
            with sp.Fori(1, NT // 2) as u:
                for s in range(2):
                    sp.wait_ge(x_lo, 2 * u + s - 1)
                    sp.wait_ge(x_hi, 2 * u + s - 1)
                    sp.dma_start(xraw[:, s], xT[2 * u + s]).then_inc(d_x[s], 16)
            sp.wait_ge(w_lo, 3)
            sp.wait_ge(w_hi, 3)
            sp.dma_start(woraw[:], wout.rearrange("(k p) n -> p k n", p=P)).then_inc(d_wo, 16)
            sp.wait_ge(qkv_mm, 3 * NT)
            for s in range(2):
                sp.dma_start(xres[:, s], x[s]).then_inc(d_xres[s], 16)
            sp.wait_ge(packed, 2 * NI)
            for j in range(XR):
                sp.dma_start(wqraw[:, j], wqT[j]).then_inc(d_wq[j], 16)
            for j in range(XR):
                sp.dma_start(wxraw[:, j], woT[j]).then_inc(d_wx[j], 16)
            with sp.Fori(1, NT // 2) as u:
                for s in range(2):
                    sp.wait_ge(o_sum, 2 * u + s - 1)
                    sp.dma_start(xres[:, s], x[2 * u + s]).then_inc(d_xres[s], 16)
            sp.wait_ge(a_copy, NT)
            sp.dma_start(garaw[:, :, 0:NE], gateT).then_inc(d_f, 16)
            sp.dma_start(garaw[:, :, NE:], loraAT).then_inc(d_f, 16)
            sp.dma_start(lbs[:], loraB).then_inc(d_f, 16)

            def wq_load(g, j):
                sp.wait_ge(wq_lo, XR * g + j - (XR - 1))
                sp.wait_ge(wq_hi, XR * g + j - (XR - 1))
                sp.dma_start(wqraw[:, j], wqT[XR * g + j]).then_inc(d_wq[j], 16)

            def wx_load(g, j):
                sp.wait_ge(wx_lo, XR * g + j - (XR - 1))
                sp.wait_ge(wx_hi, XR * g + j - (XR - 1))
                sp.dma_start(wxraw[:, j], woT[XR * g + j]).then_inc(d_wx[j], 16)

            for j in range(XR):
                wq_load(1, j)
            with sp.Fori(2, XG) as g:
                for j in range(3):
                    wq_load(g, j)
                for j in range(XR):
                    wx_load(g - 1, j)
                wq_load(g, 3)
            sp.wait_ge(wq_lo, XR * XG)
            sp.wait_ge(wq_hi, XR * XG)
            sp.dma_start(baseraw[:], baseT).then_inc(d_f, 16)
            for j in range(XR):
                wx_load(XG - 1, j)
            with sp.Fori(0, NT // 2) as u:
                for s in range(2):
                    sp.wait_ge(h_out, 2 * u + s + 3)
                    sp.dma_start(out[2 * u + s], fout[:, s]).then_inc(d_out[s], 16)
            for s in range(2):
                sp.wait_ge(d_out[s], 16 * NT // 2)

        @block.gpsimd
        def _(pool):
            def minus(hi, lo, raw):
                return nc.gpsimd.tensor_tensor(lo, raw, hi.bitcast(F32), ALU.subtract)

            nc.gpsimd.memset(ones[:], 1.0).then_inc(consts_ready, 1)
            nc.gpsimd.memset(mhalf[:], -0.5).then_inc(consts_ready, 1)
            pool.wait_ge(consts_ready, 2)
            pool.wait_ge(d_ctx, 16)
            pool.wait_ge(ctx_hi, 1)
            minus(ctxs[:, 0], ctxs[:, 1], ctxraw[:]).then_inc(ctx_lo, 1)
            for n in range(1, 4):
                pool.wait_ge(kv_lo, n)
                pool.wait_ge(d_kv[n], 16)
                pool.wait_ge(kv_hi, n + 1)
                minus(kvs[:, n % 2, 0], kvs[:, n % 2, 1], kvraw[:, n]).then_inc(kv_lo, 1)
                if n == 3:
                    for u in range(4):
                        pool.wait_ge(k_ms, u + 1)
                        nc.gpsimd.tensor_tensor(small[:, 32 + 4 * u:36 + 4 * u], small[:, 16 + 4 * u:20 + 4 * u],
                                                mhalf[:, 0:4], ALU.pow).then_inc(k_r, 1)
            for n in range(3):
                pool.wait_ge(d_w[n], 16)
                pool.wait_ge(w_hi, n + 1)
                minus(ws[:, 0, n], ws[:, 1, n], wraw[:, n]).then_inc(w_lo, 1)
                if n == 0:
                    for s in range(2):
                        pool.wait_ge(d_x[s], 16)
                        pool.wait_ge(x_hi, s + 1)
                        minus(xs[:, s, 0], xs[:, s, 1], xraw[:, s]).then_inc(x_lo, 1)
            with pool.Fori(1, NT // 2) as u:
                for s in range(2):
                    pool.wait_ge(d_x[s], 16 * u + 16)
                    pool.wait_ge(x_hi, 2 * u + s + 1)
                    minus(xs[:, s, 0], xs[:, s, 1], xraw[:, s]).then_inc(x_lo, 1)

            nc.gpsimd.memset(pack[:], 0.0).then_inc(pack_hi, 1)
            nc.gpsimd.memset(vst[:], 1.0).then_inc(v_ready, 1)
            pool.wait_ge(pack_hi, 1)
            pool.wait_ge(v_ready, 1)

            def pack_qk(i):
                pool.wait_ge(tr_k, i + 1)
                for a in range(2):
                    nat = qk[:, i, :, a, :].rearrange("p c (j d) -> p c j d", j=4)
                    hi = pack[:, a, :, :, 0:D]
                    hi2 = pack[:, a, :, :, (1 + a) * D:(2 + a) * D]
                    lo = pack[:, a, :, :, (2 - a) * D:(3 - a) * D]
                    nc.gpsimd.tensor_copy(hi.bitcast(F32R), nat).then_inc(pack_hi, 1)
                    nc.gpsimd.tensor_copy(hi2.bitcast(F32R), nat).then_inc(pack_hi, 1)
                    pool.wait_ge(pack_hi, 4 * i + 2 * a + 3)
                    pool.sem_inc(pool_passed, 1)
                    nc.gpsimd.tensor_tensor(lo, nat, hi, ALU.subtract).then_inc(packed, 1)

            def v_copy(i, par):
                nc.gpsimd.tensor_copy(vst[:, par, :, :, 0:D], vx[:, i]).then_inc(v_ready, 1)

            pool.wait_ge(rope_done, 2 * 2 + 1)
            pack_qk(0)
            v_copy(0, 0)
            pack_qk(1)
            pool.wait_ge(rope_done, 2 * NT + 1)
            with pool.Fori(1, NI // 2) as u:
                for par in range(2):
                    i = 2 * u + par
                    pack_qk(i)
                    pool.wait_ge(pts_free, 4 * i - 6)
                    v_copy(i - 1, 1 - par)
            pool.wait_ge(pts_free, 4 * NI - 6)
            v_copy(NI - 1, 1)

            pool.wait_ge(wo_hi, 1)
            minus(wos[:, 0], wos[:, 1], woraw[:]).then_inc(wo_lo, 1)
            with pool.Fori(0, NT // 2) as u:
                for s in range(2):
                    pool.wait_ge(d_xres[s], 16 * u + 16)
                    nc.gpsimd.tensor_tensor(xres[:, s], xres[:, s], outbs[:], ALU.add).then_inc(o_res, 1)
                    pool.wait_ge(o_ve, 2 * u + s + 1)
                    nc.gpsimd.tensor_tensor(small[:, 64 + s:65 + s], small[:, 62 + s:63 + s], mhalf[:, 0:1],
                                            ALU.pow).then_inc(o_rstd, 1)

            def prob_of(j):
                return prob[:, j // 2, :, j % 2, :]

            def query_rms(h):
                pool.wait_ge(n_sb, h + 1)
                nc.gpsimd.tensor_tensor(small[:, 80:88], small[:, 72:80], mhalf[:], ALU.pow).then_inc(n_r, 1)

            def add_mask(h, j):
                p = prob_of(j)
                m = maskx[:].unsqueeze(1).broadcast_to([P, B, 2, XS])
                pool.wait_ge(p_scaled, h + 1)
                nc.gpsimd.tensor_tensor(p.rearrange("p (b c) k -> p b c k", b=B),
                                        p.rearrange("p (b c) k -> p b c k", b=B), m, ALU.add).then_inc(p_masked, 1)

            def less_max(h, j):
                pool.wait_ge(p_max, h + 1)
                nc.gpsimd.tensor_tensor(prob_of(j), prob_of(j), over(small[:, 88:96], XS),
                                        ALU.subtract).then_inc(p_sub, 1)

            def over_sum(h, j):
                pool.wait_ge(p_rec, h + 1)
                nc.gpsimd.tensor_tensor(prob_of(j), prob_of(j), over(small[:, 104:112], XS),
                                        ALU.mult).then_inc(p_norm, 1)

            def wq_low(h, j):
                pool.wait_ge(wq_hi, h + 1)
                minus(wqs[:, j, 0], wqs[:, j, 1], wqraw[:, j]).then_inc(wq_lo, 1)

            def wx_low(h, j):
                pool.wait_ge(wx_hi, h + 1)
                minus(wxs[:, j, 0], wxs[:, j, 1], wxraw[:, j]).then_inc(wx_lo, 1)

            def finish(g, more):
                h = XR * g + 3
                less_max(h, 3)
                wx_low(h, 3)
                over_sum(h, 3)
                pool.wait_ge(z_hi, g + 1)
                minus(vsp[:, 0], vsp[:, 1], VTx[:, g]).then_inc(z_lo, 1)
                if more:
                    wq_low(h + 4, 3)

            def attend(g, more):
                h = XR * g
                if more:
                    wq_low(h + 4, 0)
                query_rms(h)
                add_mask(h, 0)
                less_max(h, 0)
                if more:
                    wq_low(h + 5, 1)
                over_sum(h, 0)
                query_rms(h + 1)
                add_mask(h + 1, 1)
                less_max(h + 1, 1)
                over_sum(h + 1, 1)
                if more:
                    wq_low(h + 6, 2)
                query_rms(h + 2)
                add_mask(h + 2, 2)
                wx_low(h, 0)
                less_max(h + 2, 2)
                wx_low(h + 1, 1)
                over_sum(h + 2, 2)
                query_rms(h + 3)
                wx_low(h + 2, 2)
                add_mask(h + 3, 3)

            for j in range(XR):
                wq_low(j, j)
            attend(0, True)
            with pool.Fori(1, XG - 1) as g:
                finish(g - 1, True)
                attend(g, True)
            finish(XG - 2, True)
            attend(XG - 1, False)
            finish(XG - 1, False)

            pool.wait_ge(b_hi, 1)
            minus(bases[:, 0], bases[:, 1], baseraw[:]).then_inc(b_lo, 1)
            pool.wait_ge(b_hi, 2)
            minus(gas[:, 0], gas[:, 1], garaw[:]).then_inc(b_lo, 1)
            with pool.Fori(0, NT // 2) as u:
                for s in range(2):
                    pool.wait_ge(f_ve, 2 * u + s + 1)
                    nc.gpsimd.tensor_tensor(small[:, 162 + s:163 + s], small[:, 160 + s:161 + s], mhalf[:, 0:1],
                                            ALU.pow).then_inc(f_rstd, 1)
                    pool.wait_ge(f_x2, 2 * u + s + 1)
                    pool.wait_ge(z_sum, 2 * u + s + 1)
                    nc.gpsimd.tensor_tensor(x2b[:, s], x2c[:, s], basebs[:], ALU.add).then_inc(f_bias, 1)
            with pool.Fori(0, NT // 2) as u:
                for s in range(2):
                    pool.wait_ge(h_ve, 2 * u + s + 1)
                    nc.gpsimd.tensor_tensor(small[:, 182 + s:183 + s], small[:, 180 + s:181 + s], mhalf[:, 0:1],
                                            ALU.pow).then_inc(h_rstd, 1)

        @block.scalar
        def _(act):
            def copy(dst, src):
                return nc.scalar.activation(dst, src, ACT.Copy)

            act.sem_inc(q_free, 2)
            act.sem_inc(g_sb, 2)
            for u in range(4):
                act.wait_ge(k_mm, u + 1)
                for g in range(4):
                    act.wait_ge(k_sq, 4 * u + g)
                    nc.scalar.activation(junk[:], ps[:, u, g * XD:(g + 1) * XD], ACT.Square,
                                         accum_out=small[:, 4 * u + g:4 * u + g + 1]).then_inc(k_sq, 1)
            act.wait_ge(dve_consts, 3)
            for u in range(4):
                act.wait_ge(k_tr, u + 1)
                n, t = u // 2, u % 2
                nc.scalar.activation(KTx[:, 4 * n:4 * n + 4, t * P:(t + 1) * P], heads(ps[:, 4 + u % 2, :], 4),
                                     ACT.Copy, scale=wqk[:, 0:1]).then_inc(k_done, 1)

            def q_out(i):
                act.wait_ge(tr_q, i + 1)
                copy(qkt[:, 0].rearrange("p a b -> p (a b)"), ps[:, 0, :]).then_inc(qt_ready, 1)

            def pt_out(i):
                for f in range(4):
                    act.wait_ge(pt_mm, 4 * i + f + 1)
                    act.wait_ge(pts_free, 4 * i + f + 1)
                    copy(pts[:, f % 2], ps[:, pt_bank(f), :]).then_inc(pt_sb, 1)

            def exps(i, par, c):
                act.wait_ge(s_free, 2 * i + c + 3)
                nc.scalar.activation(sb[:, par, c], sb[:, par, c], ACT.Exp, scale=0.25).then_inc(s_exp, 1)

            def ot_out(i, first=False):
                act.wait_ge(pts_free, 4 * i + 6)
                if not first:
                    act.wait_ge(ob_mm, i)
                copy(ot[:], ps[:, 7, 0:SEQ]).then_inc(ot_sb, 1)

            def a_copies(u, s):
                act.wait_ge(o_norm, HQ * (u + 1))
                copy(heads(attc[:, s], HQ), att[:, bass.ds(u * HQ, HQ), s, :]).then_inc(a_copy, 1)

            def a_parts(u, s):
                t = 2 * u + s
                act.wait_ge(a_tr, t + 1)
                copy(aT[:, s, 0], heads(ps[:, 2 + s, :], 4)).then_inc(a_hi, 1)

            def x1_parts(u, s):
                t = 2 * u + s
                act.wait_ge(x1_tr, t + 1)
                copy(x1T[:, 0, :, bass.ds(t * P, P)], heads(ps[:, s, :], 4)).then_inc(x1_hi, 1)
                copy(yacc[:, t], x1c[:, s]).then_inc(y_init, 1)

            act.sem_inc(y_init, 2)
            q_out(0)
            act.wait_ge(tr_k, 2)
            copy(qkt[:, 1].rearrange("p a b -> p (a b)"), ps[:, 1, :]).then_inc(kt_ready, 1)
            q_out(1)
            exps(0, 0, 0)
            exps(0, 0, 1)
            q_out(2)
            pt_out(0)
            exps(1, 1, 0)
            ot_out(0, True)
            exps(1, 1, 1)
            with act.Fori(1, NI // 2 - 1) as u:
                for par in range(2):
                    i = 2 * u + par
                    q_out(i + 1)
                    pt_out(i - 1)
                    exps(i, par, 0)
                    ot_out(i - 1)
                    exps(i, par, 1)
            for i in (NI - 2, NI - 1):
                if i < NI - 1:
                    q_out(i + 1)
                pt_out(i - 1)
                exps(i, i % 2, 0)
                ot_out(i - 1)
                exps(i, i % 2, 1)
                a_copies(0, i % 2)
            pt_out(NI - 1)
            a_parts(0, 0)
            ot_out(NI - 1)

            act.wait_ge(a_tr, 1)
            a_copies(1, 0)
            a_parts(0, 1)
            with act.Fori(1, NT // 2 - 1) as u:
                act.wait_ge(a_tr, 2 * u)
                a_copies(u, 1)
                a_parts(u, 0)
                x1_parts(u - 1, 0)
                act.wait_ge(a_tr, 2 * u + 1)
                a_copies(u + 1, 0)
                a_parts(u, 1)
                x1_parts(u - 1, 1)
            act.wait_ge(a_tr, NT - 2)
            a_copies(NT // 2 - 1, 1)
            for u in range(NT // 2 - 2, NT // 2):
                for s in range(2):
                    if u == NT // 2 - 2:
                        a_parts(u + 1, s)
                    x1_parts(u, s)

            def q_parts(g, j, nh):
                act.wait_ge(q_mm, 8 * g + 2 * j + nh + 1)
                sl = slice(nh * 512, nh * 512 + 512)
                nc.scalar.activation(sq[:, j % 2, sl], ps[:, nh, :], ACT.Square)
                copy(qT[:, j % 2, sl], ps[:, nh, :]).then_inc(q_free, 1)

            def xt_high(g, k):
                act.wait_ge(xt_mm, 4 * g + k + 1)
                copy(pT[:, 0, k // 2, 4 * (k % 2):4 * (k % 2) + 4, :], heads(ps[:, 4, :], 4)).then_inc(xt_hi, 1)

            def norm_row(g, j):
                act.wait_ge(n_mm, XR * g + j + 1)
                copy(nrow[:], ps[:, 3, 0:SEQ]).then_inc(n_row, 1)

            def vw_high(g, n):
                act.wait_ge(vw_mm, 8 * g + n + 2)
                pair, head = n // 4, n % 4
                for d in range(2):
                    last = copy(vws(2 * pair + d)[XS * (head % 2):XS * (head % 2 + 1), 0, head // 2, :],
                                ps[XS * d:XS * (d + 1), 5 + n % 2, :])
                last.then_inc(vw_hi, 1)

            def exp_of(g, j):
                act.wait_ge(p_sub, XR * g + j + 1)
                p = prob[:, j // 2, :, j % 2, :]
                nc.scalar.activation(p, p, ACT.Exp).then_inc(p_exp, 1)

            def z_high(g):
                act.wait_ge(vw_mm, 8 * g + 1)
                copy(vsp[:, 0], VTx[:, g, :]).then_inc(z_hi, 1)

            def group(g, one, two):
                if two:
                    z_high(g - 1)
                for n in range(2):
                    if one:
                        q_parts(g, 0, n)
                    if two:
                        xt_high(g - 1, n)
                        if n == 0:
                            exp_of(g - 1, 3)
                if one:
                    q_parts(g, 1, 0)
                    norm_row(g, 0)
                if two:
                    vw_high(g - 1, 0)
                    vw_high(g - 1, 1)
                    xt_high(g - 1, 2)
                if one:
                    q_parts(g, 1, 1)
                if two:
                    xt_high(g - 1, 3)
                if one:
                    exp_of(g, 0)
                if two:
                    vw_high(g - 1, 2)
                    vw_high(g - 1, 3)
                if one:
                    q_parts(g, 2, 0)
                    norm_row(g, 1)
                    q_parts(g, 2, 1)
                if two:
                    vw_high(g - 1, 4)
                    vw_high(g - 1, 5)
                if one:
                    exp_of(g, 1)
                    q_parts(g, 3, 0)
                    norm_row(g, 2)
                if two:
                    vw_high(g - 1, 6)
                    vw_high(g - 1, 7)
                if one:
                    q_parts(g, 3, 1)
                    norm_row(g, 3)
                    exp_of(g, 2)

            def last_projection(g):
                z_high(g)
                exp_of(g, 3)
                xt_high(g, 0)
                xt_high(g, 1)
                for n in range(4):
                    vw_high(g, n)
                act.wait_ge(q_mm, 8 * XG)
                act.wait_ge(d_f, 64)
                copy(bases[:, 0], baseraw[:]).then_inc(b_hi, 1)
                copy(gas[:, 0], garaw[:]).then_inc(b_hi, 1)
                xt_high(g, 2)
                xt_high(g, 3)
                for n in range(4, 8):
                    vw_high(g, n)

            group(0, True, False)
            with act.Fori(1, XG) as g:
                group(g, True, True)
            last_projection(XG - 1)

            def x2_parts(t, s):
                act.wait_ge(f_tr, t + 1)
                copy(x2T[:, s, 0], heads(ps[:, s, :], 4)).then_inc(f_hi, 1)

            def gates_out(t, s):
                act.wait_ge(g_mm, t + 1)
                copy(gl[:, t], ps[:, 2 + s, 0:NE + P]).then_inc(g_sb, 1)

            x2_parts(0, 0)
            x2_parts(1, 1)
            with act.Fori(1, NT // 2) as u:
                for s in range(2):
                    gates_out(2 * u + s - 2, s)
                    x2_parts(2 * u + s, s)
            gates_out(NT - 2, 0)
            gates_out(NT - 1, 1)
            act.wait_ge(r_step, 8)
            nc.scalar.activation(wts[:, 2], wts[:, 2], ACT.Exp).then_inc(r_exp, 1)
            for n in range(2):
                act.wait_ge(l_tr, n + 1)
                copy(lowT[:, 4 * n:4 * n + 4], heads(ps[:, n, :], 4)).then_inc(l_sb, 1)
            with act.Fori(0, NT // 2) as u:
                for s in range(2):
                    act.wait_ge(l_mm, 2 * u + s + 1)
                    act.wait_ge(h_out, 2 * u + s + 1)
                    copy(fo[:, s], ps[:, 2 + s, :]).then_inc(h_sum, 1)

        @block.vector
        def _(dve):
            tt = nc.vector.tensor_tensor

            def high(hi, raw):
                return nc.vector.tensor_copy(hi, raw)

            def stats(src, at6, at2, step, n):
                nc.vector.bn_stats(small[:, at6:at6 + 6], src).then_inc(step, 1)
                dve.wait_ge(step, n + 1)
                dve.sem_inc(dve_passed, 1)
                nc.vector.bn_aggr(small[:, at2:at2 + 2], small[:, at6:at6 + 6]).then_inc(step, 1)
                dve.wait_ge(step, n + 2)

            dve.sem_inc(qkv_free, 6)
            dve.sem_inc(s_free, 2)
            dve.sem_inc(vw_free, 2)
            for started in (rope_done, xt_lo):
                dve.sem_inc(started, 1)
            dve.sem_inc(y_add, 2)
            dve.sem_inc(z_sum, 2)
            dve.sem_inc(h_out, 2)
            dve.wait_ge(d_ctx, 16)
            high(ctxs[:, 0], ctxraw[:]).then_inc(ctx_hi, 1)

            def kv_high(n):
                dve.wait_ge(d_kv[n], 16)
                high(kvs[:, n % 2, 0], kvraw[:, n]).then_inc(kv_hi, 1)

            def key_ms(u):
                dve.wait_ge(k_sq, 4 * u + 4)
                nc.vector.tensor_scalar(small[:, 16 + 4 * u:20 + 4 * u], small[:, 4 * u:4 * u + 4], 1.0 / XD, EPS,
                                        ALU.mult, ALU.add).then_inc(k_ms, 1)

            def key_scale(u):
                dve.wait_ge(k_r, u + 1)
                if u >= 2:
                    dve.wait_ge(k_tr, u - 1)
                tt(heads(knat[:, u % 2], 4), heads(ps[:, u, :], 4), over(small[:, 32 + 4 * u:36 + 4 * u], XD),
                   ALU.mult).then_inc(k_nat, 1)

            kv_high(0)
            dve.wait_ge(kv_hi, 1)
            tt(kvs[:, 0, 1], kvraw[:, 0], kvs[:, 0, 0].bitcast(F32), ALU.subtract).then_inc(kv_lo, 1)
            kv_high(1)
            dve.wait_ge(d_const, 16 * NCONST)
            nc.vector.tensor_scalar(wqk[:], wqn[:], wkn[:, 0:1], XD ** -0.5, ALU.mult, ALU.mult).then_inc(dve_consts, 1)
            nc.vector.tensor_copy(causb[:], causf[:]).then_inc(dve_consts, 1)
            nc.vector.tensor_scalar(diagb[:], identf[:], MASK_A, None, ALU.mult).then_inc(dve_consts, 1)
            dve.wait_ge(k_mm, 2)
            kv_high(2)
            dve.wait_ge(k_mm, 4)
            kv_high(3)

            def w_high(n):
                dve.wait_ge(d_w[n], 16)
                high(ws[:, 0, n], wraw[:, n]).then_inc(w_hi, 1)

            def x_high(u, s):
                dve.wait_ge(d_x[s], 16 * u + 16)
                high(xs[:, s, 0], xraw[:, s]).then_inc(x_hi, 1)

            w_high(0)
            x_high(0, 0)
            x_high(0, 1)
            w_high(1)
            w_high(2)
            for u in range(4):
                key_ms(u)
            for v in range(4):
                dve.wait_ge(v_mm, v + 1)
                nc.vector.tensor_copy(VTx[:, 2 * v:2 * v + 2], heads(ps[:, 6 + v % 2, :], 2)).then_inc(v_done, 1)
            for u in range(4):
                key_scale(u)

            dve.wait_ge(kv_lo, 4)
            def project(u, s, more):
                t = 2 * u + s
                dve.wait_ge(rope_done, 2 * t + 1)
                for n in range(2):
                    dve.wait_ge(qkv_mm, 3 * t + n + 1)
                    tt(qraw[:, n], ps[:, 3 * s + n, :], qkvbs[:, n], ALU.add).then_inc(qkv_free, 1)
                dve.wait_ge(qkv_mm, 3 * t + 3)
                tt(vx[:, bass.ds(u * HQ, HQ), s, :, 0:D],
                   ps[:, 3 * s + 2, :].rearrange("p (a j d) -> p a j d", a=HQ, j=4),
                   qkvbs[:, 2].rearrange("p (a j d) -> p a j d", a=HQ, j=4), ALU.add).then_inc(qkv_free, 1)
                dve.wait_ge(qkv_free, 3 * t + 8)
                raw = qraw[:].rearrange("p n (h d) -> p (n h) d", d=D)
                rot = qrot[:].rearrange("p n (h d) -> p (n h) d", d=D)
                for a in range(2):
                    half = slice((1 - a) * D // 2, (2 - a) * D // 2)
                    own = slice(a * D // 2, (a + 1) * D // 2)
                    sin = ropes[:, s, 1, own].unsqueeze(1).broadcast_to([P, 2 * H, D // 2])
                    tt(rot[:, :, own], raw[:, :, half], sin, ALU.mult).then_inc(rope_step, 1)
                dve.wait_ge(rope_step, 4 * t + 2)
                for n in range(2):
                    cos = ropes[:, s, 0, :].unsqueeze(1).broadcast_to([P, H, D])
                    tt(qraw[:, n].rearrange("p (h d) -> p h d", d=D),
                       qraw[:, n].rearrange("p (h d) -> p h d", d=D), cos, ALU.mult).then_inc(rope_step, 1)
                dve.wait_ge(rope_step, 4 * t + 4)
                for n in range(2):
                    tt(qk[:, bass.ds(u * HQ, HQ), s, n, :], heads(qraw[:, n], HQ), heads(qrot[:, n], HQ),
                       ALU.add).then_inc(rope_done, 1)
                if more:
                    x_high(u + 1, s)

            with dve.Fori(0, NT // 2 - 1) as u:
                for s in range(2):
                    dve.wait_ge(x_lo, 2 * u + s + 1)
                    project(u, s, True)
            for s in range(2):
                project(NT // 2 - 1, s, False)

            def k_out(i):
                dve.wait_ge(tr_k, i + 2)
                nc.vector.tensor_copy(qkt[:, 1].rearrange("p a b -> p (a b)"), ps[:, 1, :]).then_inc(kt_ready, 1)

            def less_max(i, par, c):
                s4 = ps[:, 2 + 2 * c:4 + 2 * c, :].rearrange("p r (j k) -> p r j k", j=2)
                top = heads(small[:, 112 + 4 * c:116 + 4 * c], 2)
                dve.wait_ge(s_mm, 2 * i + c + 1)
                nc.vector.tensor_reduce(top, s4, AX.X, ALU.max).then_inc(s_max, 1)
                dve.wait_ge(s_max, 2 * i + c + 1)
                tt(sb[:, par, c].rearrange("p (j r) k -> p r j k", r=2), s4, over(top, SEQ), ALU.subtract
                   ).then_inc(s_free, 1)

            def norm_out(i):
                o = ps[:, 7, SEQ:].rearrange("p (h d) -> p h d", d=2 * D)
                dve.wait_ge(ob_mm, i + 1)
                nc.vector.reciprocal(small[:, 120:128], o[:, :, D]).then_inc(o_rec, 1)
                dve.wait_ge(o_rec, i + 1)
                tt(att[:, i].rearrange("p c (j d) -> p (c j) d", d=D), o[:, :, 0:D], over(small[:, 120:128], D),
                   ALU.mult).then_inc(o_norm, 1)

            less_max(0, 0, 0)
            k_out(1)
            less_max(0, 0, 1)
            less_max(1, 1, 0)
            k_out(2)
            less_max(1, 1, 1)
            with dve.Fori(1, NI // 2 - 1) as u:
                for par in range(2):
                    i = 2 * u + par
                    less_max(i, par, 0)
                    norm_out(i - 2)
                    k_out(i + 1)
                    less_max(i, par, 1)
            dve.wait_ge(d_wo, 16)
            high(wos[:, 0], woraw[:]).then_inc(wo_hi, 1)
            less_max(NI - 2, 0, 0)
            norm_out(NI - 4)
            k_out(NI - 1)
            less_max(NI - 2, 0, 1)
            less_max(NI - 1, 1, 0)
            norm_out(NI - 3)
            less_max(NI - 1, 1, 1)
            norm_out(NI - 2)

            dve.sem_inc(x1_free, 2)

            def a_low(t, s):
                dve.wait_ge(a_hi, t + 1)
                tt(aT[:, s, 1], heads(ps[:, 2 + s, :], 4), aT[:, s, 0].bitcast(F32), ALU.subtract).then_inc(a_lo, 1)

            def x1_low(t, s):
                dve.wait_ge(x1_hi, t + 1)
                own = bass.ds(t * P, P)
                tt(x1T[:, 1, :, own], heads(ps[:, s, :], 4), x1T[:, 0, :, own].bitcast(F32),
                   ALU.subtract).then_inc(x1_free, 1)

            def layer1(t, s):
                dve.wait_ge(o_mm, t + 1)
                dve.wait_ge(o_res, t + 1)
                tt(ro[:, s], ps[:, 4 + s, :], xres[:, s], ALU.add).then_inc(o_sum, 1)
                dve.wait_ge(o_sum, t + 1)
                stats(ro[:, s], 128 + 6 * s, 140 + 2 * s, o_stat, 2 * t)
                nc.vector.tensor_scalar(small[:, 62 + s:63 + s], small[:, 141 + 2 * s:142 + 2 * s], EPS, None,
                                        ALU.add).then_inc(o_ve, 1)
                dve.wait_ge(o_rstd, t + 1)
                dve.wait_ge(y_init, t + 1)
                nc.vector.tensor_scalar(x1c[:, s], ro[:, s], small[:, 140 + 2 * s:141 + 2 * s],
                                        small[:, 64 + s:65 + s], ALU.subtract, ALU.mult).then_inc(x1_done, 1)

            a_low(0, 0)
            norm_out(NI - 1)
            a_low(1, 1)
            layer1(0, 0)
            with dve.Fori(1, NT // 2) as u:
                a_low(2 * u, 0)
                layer1(2 * u - 1, 1)
                x1_low(2 * u - 2, 0)
                a_low(2 * u + 1, 1)
                layer1(2 * u, 0)
                x1_low(2 * u - 1, 1)
            layer1(NT - 1, 1)
            x1_low(NT - 2, 0)
            x1_low(NT - 1, 1)

            def wq_high(g, j):
                dve.wait_ge(d_wq[j], 16 * g + 16)
                high(wqs[:, j, 0], wqraw[:, j]).then_inc(wq_hi, 1)

            def wx_high(g, j):
                dve.wait_ge(d_wx[j], 16 * g + 16)
                high(wxs[:, j, 0], wxraw[:, j]).then_inc(wx_hi, 1)

            def mean_square(g, j):
                dve.wait_ge(n_tr, XR * g + j + 1)
                sums = ps[:, 3, SEQ:].rearrange("p (c b e) -> p b c e", c=2, b=B)[:, :, :, 0]
                nc.vector.tensor_scalar(small[:, 72:80].rearrange("p (b c) -> p b c", b=B), sums, 1.0 / XD, EPS,
                                        ALU.mult, ALU.add).then_inc(n_sb, 1)

            def scores_out(g, j):
                dve.wait_ge(sx_mm, XR * g + j + 1)
                dve.wait_ge(n_r, XR * g + j + 1)
                tt(prob[:, j // 2, :, j % 2, :], heads(ps[:, 2, :], 8), over(small[:, 80:88], XS), ALU.mult
                   ).then_inc(p_scaled, 1)

            def row_max(g, j):
                dve.wait_ge(p_masked, XR * g + j + 1)
                nc.vector.tensor_reduce(small[:, 88:96], prob[:, j // 2, :, j % 2, :], AX.X, ALU.max
                                        ).then_inc(p_max, 1)

            def row_sum(g, j):
                dve.wait_ge(p_exp, XR * g + j + 1)
                nc.vector.tensor_reduce(small[:, 96:104], prob[:, j // 2, :, j % 2, :], AX.X, ALU.add
                                        ).then_inc(p_sum, 1)
                dve.wait_ge(p_sum, XR * g + j + 1)
                nc.vector.reciprocal(small[:, 104:112], small[:, 96:104]).then_inc(p_rec, 1)

            def xt_low(g, k):
                dve.wait_ge(xt_hi, 4 * g + k + 1)
                own = slice(4 * (k % 2), 4 * (k % 2) + 4)
                tt(pT[:, 1, k // 2, own, :], heads(ps[:, 4, :], 4), pT[:, 0, k // 2, own, :].bitcast(F32),
                   ALU.subtract).then_inc(xt_lo, 1)

            def vw_low(g, n):
                dve.wait_ge(vw_hi, 8 * g + n + 1)
                pair, head = n // 4, n % 4
                for d in range(2):
                    own = slice(XS * (head % 2), XS * (head % 2 + 1))
                    last = tt(vws(2 * pair + d)[own, 1, head // 2, :], ps[XS * d:XS * (d + 1), 5 + n % 2, :],
                              vws(2 * pair + d)[own, 0, head // 2, :].bitcast(F32), ALU.subtract)
                last.then_inc(vw_free, 1)

            def y_sum(g, b, c):
                dve.wait_ge(y_mm, 8 * g + 2 * b + c + 1)
                tt(yacc[:, 2 * b + c], ps[:, y_bank(c), :], yacc[:, 2 * b + c], ALU.add).then_inc(y_add, 1)

            def next_wq(g, j):
                dve.wait_ge(q_mm, 8 * g + 2 * j + 2)
                wq_high(g + 1, j)

            def group(g, one, two, more):
                if two:
                    xt_low(g - 1, 0)
                    row_sum(g - 1, 3)
                    xt_low(g - 1, 1)
                if more:
                    next_wq(g, 0)
                if one:
                    mean_square(g, 0)
                if two:
                    vw_low(g - 1, 0)
                    vw_low(g - 1, 1)
                if one:
                    scores_out(g, 0)
                if two:
                    xt_low(g - 1, 2)
                if one:
                    row_max(g, 0)
                if two:
                    xt_low(g - 1, 3)
                if more:
                    next_wq(g, 1)
                if one:
                    row_sum(g, 0)
                if two:
                    vw_low(g - 1, 2)
                    vw_low(g - 1, 3)
                if one:
                    mean_square(g, 1)
                if two:
                    y_sum(g - 1, 0, 0)
                if one:
                    scores_out(g, 1)
                if two:
                    y_sum(g - 1, 0, 1)
                if one:
                    row_max(g, 1)
                if two:
                    vw_low(g - 1, 4)
                    vw_low(g - 1, 5)
                if more:
                    next_wq(g, 2)
                if one:
                    row_sum(g, 1)
                if two:
                    y_sum(g - 1, 1, 0)
                if one:
                    mean_square(g, 2)
                if two:
                    vw_low(g - 1, 6)
                    vw_low(g - 1, 7)
                if one:
                    scores_out(g, 2)
                    dve.wait_ge(vw_mm, 8 * g + 1)
                    wx_high(g, 0)
                    wx_high(g, 1)
                    row_max(g, 2)
                    wx_high(g, 2)
                    wx_high(g, 3)
                if two:
                    y_sum(g - 1, 1, 1)
                if more:
                    next_wq(g, 3)
                if one:
                    row_sum(g, 2)
                if two:
                    y_sum(g - 1, 2, 0)
                if one:
                    mean_square(g, 3)
                if two:
                    y_sum(g - 1, 2, 1)
                if one:
                    scores_out(g, 3)
                if two:
                    y_sum(g - 1, 3, 0)
                if one:
                    row_max(g, 3)
                if two:
                    y_sum(g - 1, 3, 1)

            for j in range(XR):
                wq_high(0, j)
            dve.wait_ge(y_init, NT + 2)
            group(0, True, False, True)
            with dve.Fori(1, XG - 1) as g:
                group(g, True, True, True)
            group(XG - 1, True, True, False)

            def layer2a(t, s):
                dve.wait_ge(y_add, 8 * (XG - 1) + t + 3)
                stats(yacc[:, t], 144 + 6 * s, 156 + 2 * s, f_stat, 2 * t)
                nc.vector.tensor_scalar(small[:, 160 + s:161 + s], small[:, 157 + 2 * s:158 + 2 * s], EPS, None,
                                        ALU.add).then_inc(f_ve, 1)

            def layer2b(t, s, first=False):
                dve.wait_ge(f_rstd, t + 1)
                if not first:
                    dve.wait_ge(f_bias, t - 1)
                nc.vector.tensor_scalar(x2c[:, s], yacc[:, t], small[:, 156 + 2 * s:157 + 2 * s],
                                        small[:, 162 + s:163 + s], ALU.subtract, ALU.mult).then_inc(f_x2, 1)

            def x2_low(t, s):
                dve.wait_ge(f_hi, t + 1)
                tt(x2T[:, s, 1], heads(ps[:, s, :], 4), x2T[:, s, 0].bitcast(F32), ALU.subtract).then_inc(f_lo, 1)

            def base_sum(t, s):
                dve.wait_ge(f_mm, t + 1)
                dve.wait_ge(f_bias, t + 1)
                tt(yacc[:, t], ps[:, 4 + s, :], x2b[:, s], ALU.add).then_inc(z_sum, 1)

            g = XG - 1
            row_sum(g, 3)
            xt_low(g, 0)
            xt_low(g, 1)
            for n in range(4):
                vw_low(g, n)
            xt_low(g, 2)
            xt_low(g, 3)
            vw_low(g, 4)
            vw_low(g, 5)
            y_sum(g, 0, 0)
            vw_low(g, 6)
            vw_low(g, 7)
            y_sum(g, 0, 1)
            layer2a(0, 0)
            y_sum(g, 1, 0)
            layer2a(1, 1)
            y_sum(g, 1, 1)
            layer2b(0, 0, True)
            y_sum(g, 2, 0)
            layer2b(1, 1, True)
            for b, c in ((2, 1), (3, 0), (3, 1)):
                y_sum(g, b, c)
            x2_low(0, 0)
            with dve.Fori(0, NT // 2 - 1) as u:
                for s in range(2):
                    t = 2 * u + s
                    layer2a(t + 2, s)
                    x2_low(t + 1, 1 - s)
                    layer2b(t + 2, s)
                    base_sum(t, s)
            x2_low(NT - 1, 1)
            base_sum(NT - 2, 0)
            base_sum(NT - 1, 1)

            logits = gl[:, :, 0:NE]
            rank = orders[:].unsqueeze(1).broadcast_to([P, NT, NE])
            one, two = route[:, 1], route[:, 4]
            steps = [0]

            def then(ins):
                ins.then_inc(r_step, 1)
                steps[0] += 1
                dve.wait_ge(r_step, steps[0])

            dve.wait_ge(g_sb, NT + 2)
            then(nc.vector.tensor_reduce(wts[:, 0], logits, AX.X, ALU.max))
            then(tt(route[:, 0], logits, over(wts[:, 0], NE), ALU.is_equal))
            then(tt(route[:, 0], route[:, 0], rank, ALU.mult))
            then(nc.vector.tensor_reduce(wts[:, 1], route[:, 0], AX.X, ALU.max))
            then(tt(one, route[:, 0], over(wts[:, 1], NE), ALU.is_equal))
            then(nc.vector.scalar_tensor_tensor(out=route[:, 2], in0=one, scalar=-3e38, in1=logits,
                                                op0=ALU.mult, op1=ALU.add))
            then(nc.vector.tensor_reduce(wts[:, 3], route[:, 2], AX.X, ALU.max))
            then(tt(wts[:, 2], wts[:, 3], wts[:, 0], ALU.subtract))
            then(tt(route[:, 3], route[:, 2], over(wts[:, 3], NE), ALU.is_equal))
            then(tt(route[:, 3], route[:, 3], rank, ALU.mult))
            then(nc.vector.tensor_reduce(wts[:, 1], route[:, 3], AX.X, ALU.max))
            then(tt(two, route[:, 3], over(wts[:, 1], NE), ALU.is_equal))
            dve.wait_ge(r_exp, 1)
            then(nc.vector.tensor_scalar(wts[:, 4], wts[:, 2], 1.0, None, ALU.add))
            then(nc.vector.reciprocal(wts[:, 5], wts[:, 4]))
            then(nc.vector.tensor_scalar(wts[:, 6], wts[:, 5], 2.0, None, ALU.mult))
            then(tt(wts[:, 7], wts[:, 6], wts[:, 2], ALU.mult))
            then(tt(one, one, over(wts[:, 6], NE), ALU.mult))
            then(tt(two, two, over(wts[:, 7], NE), ALU.mult))
            then(tt(route[:, 5], one, two, ALU.add))

            nc.vector.tensor_tensor(lowm[:].rearrange("p t (e r) -> p t e r", r=R),
                                    gl[:, :, NE:].rearrange("p t (e r) -> p t e r", r=R),
                                    over(route[:, 5], R), ALU.mult).then_inc(l_low, 1)

            def layer3a(t, s):
                dve.wait_ge(h_sum, t + 1)
                stats(fo[:, s], 168 + 6 * s, 184 + 2 * s, h_stat, 2 * t)
                nc.vector.tensor_scalar(small[:, 180 + s:181 + s], small[:, 185 + 2 * s:186 + 2 * s], EPS, None,
                                        ALU.add).then_inc(h_ve, 1)

            def layer3b(u, s, first=False):
                dve.wait_ge(h_rstd, 2 * u + s + 1)
                if not first:
                    dve.wait_ge(d_out[s], 16 * u)
                nc.vector.tensor_scalar(fout[:, s], fo[:, s], small[:, 184 + 2 * s:185 + 2 * s],
                                        small[:, 182 + s:183 + s], ALU.subtract, ALU.mult).then_inc(h_out, 1)

            layer3a(0, 0)
            layer3a(1, 1)
            layer3b(0, 0, True)
            layer3a(2, 0)
            layer3b(0, 1, True)
            layer3a(3, 1)
            layer3b(1, 0)
            with dve.Fori(2, NT // 2) as u:
                layer3a(2 * u, 0)
                layer3b(u - 1, 1)
                layer3a(2 * u + 1, 1)
                layer3b(u, 0)
            layer3b(NT // 2 - 1, 1)

        @block.tensor
        def _(pe):
            mm = nc.tensor.matmul

            def product(dst, left, right):
                n = [(k, a, b) for k in range(KC) for a, b in PASSES]
                for at_, (k, a, b) in enumerate(n):
                    last = mm(dst, left(a, k), right(b, k), start=at_ == 0, stop=at_ == len(n) - 1)
                return last

            def turn(dst, src):
                return nc.tensor.transpose(dst, src, identf[:])

            pe.sem_inc(pts_free, 2)
            pe.sem_inc(tr_k, 1)
            pe.sem_inc(vw_mm, 1)
            pe.wait_ge(ctx_lo, 1)
            for n in range(2):
                pe.wait_ge(kv_lo, n + 1)
                for t in range(2):
                    product(ps[:, 2 * n + t, :], lambda a, k: ctxs[:, a, k, t * P:(t + 1) * P],
                            lambda b, k: kvs[:, n, b, k, :]).then_inc(k_mm, 1)
            for v in range(4):
                pe.wait_ge(kv_lo, 3 + v // 2)
                if v >= 2:
                    pe.wait_ge(v_done, v - 1)
                for g in range(2):
                    own = slice((2 * (v % 2) + g) * XD, (2 * (v % 2) + g + 1) * XD)
                    last = product(ps[:, 6 + v % 2, g * B * XS:(g + 1) * B * XS],
                                   lambda a, k: kvs[:, v // 2, a, k, own], lambda b, k: ctxs[:, b, k, :])
                last.then_inc(v_mm, 1)
            pe.wait_ge(d_const, 16 * NCONST)
            for u in range(4):
                pe.wait_ge(k_nat, u + 1)
                if u >= 2:
                    pe.wait_ge(k_done, u - 1)
                for g in range(4):
                    last = turn(ps[:, 4 + u % 2, g * P:(g + 1) * P], knat[:, u % 2, g * XD:(g + 1) * XD])
                last.then_inc(k_tr, 1)

            pe.wait_ge(k_done, 4)
            with pe.Fori(0, NT // 2) as u:
                for s in range(2):
                    t = 2 * u + s
                    pe.wait_ge(x_lo, t + 1)
                    for n in range(3):
                        pe.wait_ge(w_lo, n + 1)
                        pe.wait_ge(qkv_free, 3 * t + n + 1)
                        product(ps[:, 3 * s + n, :], lambda a, k: xs[:, s, a, k, :],
                                lambda b, k: ws[:, b, n, k, :]).then_inc(qkv_mm, 1)

            def turn_att(t, s):
                pe.wait_ge(a_copy, t + 1)
                for k in range(KC):
                    last = turn(ps[:, 2 + s, k * P:(k + 1) * P], attc[:, s, k * P:(k + 1) * P])
                last.then_inc(a_tr, 1)

            def out_product(t, s):
                pe.wait_ge(a_lo, t + 1)
                product(ps[:, 4 + s, :], lambda a, k: aT[:, s, a, k, :], lambda b, k: wos[:, b, k, :]
                        ).then_inc(o_mm, 1)

            def turn_x1(t, s):
                pe.wait_ge(x1_done, t + 1)
                pe.wait_ge(x1_free, t + 1)
                for k in range(KC):
                    last = turn(ps[:, s, k * P:(k + 1) * P], x1c[:, s, k * P:(k + 1) * P])
                last.then_inc(x1_tr, 1)

            def turn_qk(i):
                pe.wait_ge(packed, 2 * i + 2)
                for a, done in ((0, tr_q), (1, tr_k)):
                    for p in range(2):
                        for c in range(2):
                            last = turn(ps[:, a, (2 * p + c) * P:(2 * p + c + 1) * P],
                                        pack[:, a, c, 2 * p:2 * p + 2, :].rearrange("p j d -> p (j d)"))
                    last.then_inc(done, 1)

            def scores(i):
                pe.wait_ge(qt_ready, i + 1)
                pe.wait_ge(kt_ready, i + 1)
                for c in range(2):
                    pe.wait_ge(s_free, 2 * i + c + 1)
                    for r in range(2):
                        mm(heads(ps[:, 2 + 2 * c + r, :], 2), diagb[:],
                           causb[:, c, :].unsqueeze(1).broadcast_to([P, 2, SEQ]), start=True, stop=False)
                    for j in range(4):
                        own = slice(64 * (j % 2), 64 * (j % 2) + 3 * D)
                        last = mm(ps[:, 2 + 2 * c + j % 2, (j // 2) * SEQ:(j // 2 + 1) * SEQ],
                                  qkt[own, 0, j // 2, c * P:(c + 1) * P], qkt[own, 1, j // 2, :],
                                  start=False, stop=j >= 2)
                    last.then_inc(s_mm, 1)

            def values(i, par, first=False, last_two=False):
                def pv(j):
                    pe.wait_ge(pt_sb, 4 * i + j + 1)
                    for kc in range(2):
                        last = mm(ps[32 * j:32 * j + 2 * D, 7, 0:SEQ], vst[:, par, kc, j, :],
                                  pts[:, j % 2, kc * SEQ:(kc + 1) * SEQ], start=kc == 0, stop=kc == 1)
                    last.then_inc(pts_free, 1)

                pe.wait_ge(s_exp, 2 * i + 2)
                for j in range(4):
                    if j == 1:
                        pe.wait_ge(qt_ready, NI if last_two else i + 3)
                    elif j:
                        pe.wait_ge(pt_sb, 4 * i + j - 1)
                    for kc in range(2):
                        for c in range(2):
                            last = turn(ps[:, pt_bank(j), (2 * kc + c) * P:(2 * kc + c + 1) * P],
                                        sb[:, par, c, j, kc * P:(kc + 1) * P])
                    last.then_inc(pt_mm, 1)
                    if j == 1:
                        pe.wait_ge(v_ready, i + 2)
                        if not first:
                            pe.wait_ge(o_norm, i)
                    if j:
                        pv(j - 1)
                pv(3)

            def turn_out(i):
                pe.wait_ge(ot_sb, i + 1)
                for c in range(2):
                    last = turn(ps[:, 7, SEQ + c * P:SEQ + (c + 1) * P], ot[:, c * P:(c + 1) * P])
                last.then_inc(ob_mm, 1)

            pe.wait_ge(qkv_free, 3 * NT + 3)
            turn_qk(0)
            pe.wait_ge(qkv_free, 3 * NT + 6)
            scores(0)
            turn_qk(1)
            scores(1)
            turn_qk(2)
            values(0, 0, True)
            with pe.Fori(1, NI // 2 - 1) as u:
                for par in range(2):
                    i = 2 * u + par
                    scores(i)
                    turn_out(i - 2)
                    turn_qk(i + 1)
                    values(i - 1, 1 - par)
            scores(NI - 2)
            turn_out(NI - 4)
            turn_qk(NI - 1)
            values(NI - 3, 1)
            scores(NI - 1)
            turn_out(NI - 3)
            values(NI - 2, 0, last_two=True)
            turn_out(NI - 2)
            turn_att(0, 0)
            turn_att(1, 1)
            values(NI - 1, 1, last_two=True)

            pe.wait_ge(wo_lo, 1)
            out_product(0, 0)
            turn_out(NI - 1)
            with pe.Fori(1, NT // 2) as u:
                turn_att(2 * u, 0)
                out_product(2 * u - 1, 1)
                turn_x1(2 * u - 2, 0)
                turn_att(2 * u + 1, 1)
                out_product(2 * u, 0)
                turn_x1(2 * u - 1, 1)
            out_product(NT - 1, 1)
            turn_x1(NT - 2, 0)
            turn_x1(NT - 1, 1)

            def queries(g, j, nh):
                pe.wait_ge(wq_lo, XR * g + j + 1)
                pe.wait_ge(q_free, 8 * g + 2 * j + nh + 1)
                product(ps[:, nh, :], lambda a, k: wqs[:, j, a, k, :],
                        lambda b, k: x1T[:, b, k, nh * 512:(nh + 1) * 512]).then_inc(q_mm, 1)

            def norms_scores(g, j):
                h = XR * g + j
                pe.wait_ge(q_free, 8 * g + 2 * j + 4)
                pe.wait_ge(p_scaled, h)
                for b in range(B):
                    last = mm(ps[32 * b:32 * (b + 1), 3, 0:SEQ], ones[:], sq[:, j % 2, b * SEQ:(b + 1) * SEQ],
                              start=True, stop=True)
                last.then_inc(n_mm, 1)
                for t in range(NT):
                    last = mm(ps[:, 2, t * XS:(t + 1) * XS], qT[:, j % 2, t * P:(t + 1) * P],
                              KTx[:, g, t // 2 * XS:(t // 2 + 1) * XS], start=True, stop=True)
                last.then_inc(sx_mm, 1)
                pe.wait_ge(n_row, h + 1)
                for c in range(2):
                    last = turn(ps[:, 3, SEQ + c * P:SEQ + (c + 1) * P], nrow[:, c * P:(c + 1) * P])
                last.then_inc(n_tr, 1)

            def turn_probs(g, k):
                pe.wait_ge(p_norm, XR * g + 2 * (k // 2) + 2)
                pe.wait_ge(xt_lo, 4 * g + k + 1)
                if k == 0:
                    pe.wait_ge(y_add, 8 * g + 2)
                for q in range(4):
                    t = 4 * (k % 2) + q
                    last = turn(ps[:, 4, q * P:(q + 1) * P],
                                prob[:, k // 2, t].rearrange("p h k -> p (h k)"))
                last.then_inc(xt_mm, 1)

            def values_out(g, n):
                pe.wait_ge(z_lo, g + 1)
                pe.wait_ge(wx_lo, XR * g + n % 4 + 1)
                pe.wait_ge(vw_free, 8 * g + n + 1)
                for i, (a, w) in enumerate(PASSES):
                    last = mm(ps[:, 5 + n % 2, :], vsp[:, a, n // 4 * P:(n // 4 + 1) * P], wxs[:, n % 4, w, :],
                              start=i == 0, stop=i == 2)
                last.then_inc(vw_mm, 1)

            def outputs(g, b, c):
                pe.wait_ge(xt_lo, 4 * g + 5)
                pe.wait_ge(vw_free, 8 * g + 4 * (b // 2) + 6)
                pe.wait_ge(y_add, 8 * g + 2 * b + c + 1)
                n = [(p, a, w) for p in range(2) for a, w in PASSES]
                for i, (p, a, w) in enumerate(n):
                    last = mm(ps[:, y_bank(c), :], pT[:, a, p, 2 * b + c, :], vws(b)[:, w, p, :],
                              start=i == 0, stop=i == 5)
                last.then_inc(y_mm, 1)

            def group(g, one, two):
                for n in range(2):
                    if one:
                        queries(g, 0, n)
                    if two:
                        turn_probs(g - 1, n)
                if one:
                    queries(g, 1, 0)
                    norms_scores(g, 0)
                if two:
                    values_out(g - 1, 0)
                    values_out(g - 1, 1)
                    turn_probs(g - 1, 2)
                if one:
                    queries(g, 1, 1)
                if two:
                    turn_probs(g - 1, 3)
                    values_out(g - 1, 2)
                    values_out(g - 1, 3)
                if one:
                    queries(g, 2, 0)
                    norms_scores(g, 1)
                if two:
                    outputs(g - 1, 0, 0)
                if one:
                    queries(g, 2, 1)
                if two:
                    outputs(g - 1, 0, 1)
                    values_out(g - 1, 4)
                    values_out(g - 1, 5)
                if one:
                    queries(g, 3, 0)
                if two:
                    outputs(g - 1, 1, 0)
                if one:
                    norms_scores(g, 2)
                if two:
                    values_out(g - 1, 6)
                    values_out(g - 1, 7)
                if one:
                    queries(g, 3, 1)
                if two:
                    outputs(g - 1, 1, 1)
                    outputs(g - 1, 2, 0)
                if one:
                    norms_scores(g, 3)
                if two:
                    outputs(g - 1, 2, 1)
                    outputs(g - 1, 3, 0)
                    outputs(g - 1, 3, 1)

            pe.wait_ge(x1_free, NT + 2)
            pe.wait_ge(consts_ready, 2)
            group(0, True, False)
            with pe.Fori(1, XG) as g:
                group(g, True, True)
            g = XG - 1
            turn_probs(g, 0)
            turn_probs(g, 1)
            for n in range(4):
                values_out(g, n)
            turn_probs(g, 2)
            turn_probs(g, 3)
            values_out(g, 4)
            values_out(g, 5)
            outputs(g, 0, 0)
            values_out(g, 6)
            values_out(g, 7)
            for t in range(1, NT):
                outputs(g, t // 2, t % 2)

            def turn_x2(t, s):
                pe.wait_ge(f_x2, t + 1)
                for k in range(KC):
                    last = turn(ps[:, s, k * P:(k + 1) * P], x2c[:, s, k * P:(k + 1) * P])
                last.then_inc(f_tr, 1)

            def forward(t, s):
                pe.wait_ge(f_lo, t + 1)
                pe.wait_ge(g_sb, t + 1)
                pe.wait_ge(z_sum, t + 1)
                product(ps[:, 2 + s, 0:NE + P], lambda a, k: x2T[:, s, a, k, :], lambda b, k: gas[:, b, k, :]
                        ).then_inc(g_mm, 1)
                product(ps[:, 4 + s, :], lambda a, k: x2T[:, s, a, k, :], lambda b, k: bases[:, b, k, :]
                        ).then_inc(f_mm, 1)

            turn_x2(0, 0)
            turn_x2(1, 1)
            pe.wait_ge(b_lo, 2)
            with pe.Fori(0, NT // 2 - 1) as u:
                for s in range(2):
                    forward(2 * u + s, s)
                    turn_x2(2 * u + s + 2, s)
            forward(NT - 2, 0)
            forward(NT - 1, 1)
            pe.wait_ge(d_f, 64)

            pe.wait_ge(l_low, 1)
            for n in range(2):
                for t in range(4):
                    last = turn(ps[:, n, t * P:(t + 1) * P], lowm[:, 4 * n + t])
                last.then_inc(l_tr, 1)
            for t in range(NT):
                if t % 4 == 0:
                    pe.wait_ge(l_sb, t // 4 + 1)
                if t >= 2:
                    pe.wait_ge(h_sum, t - 1)
                mm(ps[:, 2 + t % 2, :], lowT[:, t], lbs[:], start=True, stop=False)
                mm(ps[:, 2 + t % 2, :], identf[:], yacc[:, t], start=False, stop=True).then_inc(l_mm, 1)


def tables(np):
    half = D // 2
    freq = (1.0 / np.float32(10000.0) ** (np.arange(half, dtype=np.float32) / np.float32(half))).astype(np.float32)
    ang = np.arange(SEQ, dtype=np.float32)[:, None] * freq[None, :]
    cos, sin = np.cos(ang), np.sin(ang)
    rope = np.stack([np.concatenate([cos, cos], -1), np.concatenate([-sin, sin], -1)], 1)
    rope = rope.reshape(2, P, 2, D).transpose(1, 0, 2, 3)
    query = np.arange(SEQ).reshape(2, P).T[:, :, None]
    causal = MASK_B * (np.arange(SEQ)[None, None, :] > query)
    return {"rope": rope, "ident": np.eye(P), "causal": causal, "order": np.arange(NE, 0, -1)}


def kernel(x, ctx_4096, mask_1x1xSxS2_ff0, L0_attn_qkv_w, L0_attn_qkv_b, L0_attn_out_w, L0_attn_out_b,
           L0_xattn_q_proj_w, L0_xattn_k_proj_w, L0_xattn_v_proj_w, L0_xattn_o_proj_w, L0_xattn_q_norm_w,
           L0_xattn_k_norm_w, L0_ffn_gate_w, L0_ffn_base_w, L0_ffn_base_b, L0_ffn_lora_A, L0_ffn_lora_B):
    import numpy as np
    import concourse.bacc as bacc
    from concourse.bass_utils import run_bass_kernel_spmd

    def chunks(w):
        return np.asarray(w).reshape(w.shape[0], -1, P).transpose(2, 1, 0)

    kw = np.asarray(L0_xattn_k_proj_w).reshape(2, 512, KC, P).transpose(0, 3, 2, 1)
    vw = np.asarray(L0_xattn_v_proj_w).reshape(2, 512, KC, P).transpose(0, 3, 2, 1)
    a = {
        "xT": np.asarray(x).reshape(NT, P, KC, P).transpose(0, 3, 2, 1),
        "x": np.asarray(x).reshape(NT, P, E),
        "ctxT": chunks(np.asarray(ctx_4096).reshape(B * XS, E)),
        "mask": np.asarray(mask_1x1xSxS2_ff0).reshape(SEQ, XS),
        "wqkv": L0_attn_qkv_w, "qkvb": L0_attn_qkv_b, "wout": L0_attn_out_w, "outb": L0_attn_out_b,
        "wqT": np.asarray(L0_xattn_q_proj_w).reshape(XH, XD, KC, P).transpose(0, 3, 2, 1),
        "wkT": kw, "wvT": vw,
        "woT": np.asarray(L0_xattn_o_proj_w).reshape(E, XH, XD).transpose(1, 2, 0),
        "qn": np.asarray(L0_xattn_q_norm_w).reshape(P, 1), "kn": np.asarray(L0_xattn_k_norm_w).reshape(P, 1),
        "gateT": chunks(L0_ffn_gate_w), "baseT": chunks(L0_ffn_base_w), "baseb": L0_ffn_base_b,
        "loraAT": chunks(np.asarray(L0_ffn_lora_A).reshape(NE * R, E)),
        "loraB": np.asarray(L0_ffn_lora_B).transpose(0, 2, 1).reshape(NE * R, E),
    }
    for name, table in tables(np).items():
        a[name] = np.asarray(table, np.float32)
    nc = bacc.Bacc("TRN2", target_bir_lowering=False, num_devices=1)
    arrays, aps = {}, {}
    for name, v in a.items():
        v = np.ascontiguousarray(v)
        arrays[f"in_{name}"] = v
        aps[name] = nc.dram_tensor(f"in_{name}", v.shape, mybir.dt.from_np(v.dtype), kind="ExternalInput").ap()
    aps["out"] = nc.dram_tensor("out_y", (NT, P, E), F32, kind="ExternalOutput").ap()
    decoder_layer(nc, **aps)
    r = run_bass_kernel_spmd(nc, [arrays], core_ids=[0])
    return r.results[0]["out_y"].reshape(B, SEQ, E)
```

```python
from contextlib import ExitStack

import concourse.bass as bass
from concourse import mybir

ALU = mybir.AluOpType
ACT = mybir.ActivationFunctionType
AX = mybir.AxisListType
F32 = mybir.dt.float32
F32R = mybir.dt.float32r
BF16 = mybir.dt.bfloat16

P = 128
B, SEQ, E = 4, 256, 512
NT = B * SEQ // P
KC = E // P
H, D = 32, 16
HQ = H // 4
NI = B * HQ
XH, XG, XD, XS = 32, 8, 128, 64
XR = XH // XG
NE, R = 8, 16
EPS = 1e-5
MASK_VAL = -66504.0
MASK_A, MASK_B = -1632.0, 163.0
KB = 1024
PASSES = ((0, 0), (0, 1), (1, 0))
assert MASK_A * MASK_B == 4 * MASK_VAL


def decoder_layer(nc, xT, x, ctxT, mask, wqkv, qkvb, wout, outb, wqT, wkT, wvT, woT, qn, kn,
                  gateT, baseT, baseb, loraAT, loraB, rope, ident, causal, order, out):
    with ExitStack() as ctx:
        base_at = 16512

        def at(name, kb, shape, dt):
            return nc.alloc_sbuf_tensor_at(name, shape, dt, offset=base_at + int(kb * KB))

        def sem(name):
            return ctx.enter_context(nc.semaphore(name))

        ps = ctx.enter_context(nc.psum_tensor("ps", [P, 8, 512], F32))

        KTx = at("KTx", 0, [P, XG, B * XS], F32)
        VTx = at("VTx", 8, [P, XG, B * XS], F32)
        c0 = 16
        identf = at("identf", c0, [P, P], F32)
        maskx = at("maskx", c0 + 0.5, [P, 2, XS], F32)
        outbs = at("outbs", c0 + 1, [P, E], F32)
        basebs = at("basebs", c0 + 3, [P, E], F32)
        causb = at("causb", c0 + 5, [P, P], BF16)
        diagb = at("diagb", c0 + 6, [P, P], BF16)
        ropes = at("ropes", c0 + 6.25, [P, 2, 2, D], F32)
        mhalf = at("mhalf", c0 + 6.5625, [P, 8], F32)
        wqn = at("wqn", c0 + 6.625, [P, 1], F32)
        wkn = at("wkn", c0 + 6.6875, [P, 1], F32)
        wqk = at("wqk", c0 + 6.75, [P, 1], F32)
        orders = at("orders", c0 + 6.8125, [P, NE], F32)
        small = at("small", c0 + 7, [P, 256], F32)
        junk = at("junk", 207, [P, P], F32)
        ones = at("ones", 207.5, [P, 32], F32)
        kvraw = at("kvraw", 142, [P, 4, KC, 512], F32)
        kvs = at("kvs", 174, [P, 2, 2, KC, 512], F32R)
        ctxs = at("ctxs", 110, [P, 2, KC, B * XS], F32R)
        ctxraw = at("ctxraw", 124, [P, KC, B * XS], F32)
        knat = at("knat", 96, [P, 4, 512], F32)
        wraw = at("wraw", 72, [P, 3, KC, 512], F32)
        ws = at("ws", 24, [P, 2, 3, KC, 512], F32R)
        xraw = at("xraw", 120, [P, 2, KC, P], F32)
        xs = at("xs", 132, [P, 2, 2, KC, P], F32R)
        qraw = at("qraw", 96, [P, 2, 512], F32)
        qrot = at("qrot", 100, [P, 2, 512], F32)
        qkvbs = at("qkvbs", 104, [P, 3, 512], F32)
        causf = at("causf", 118, [P, P], F32)
        qk = at("qk", 142, [P, NI, 2, 2, 64], F32)
        vx = at("vx", 174, [P, NI, 2, 4, D], F32)
        att = at("att", 191, [P, NI, 2, 64], F32)
        sb = at("sb", 104, [P, 2, 2, 4, SEQ], F32)
        pts = at("pts", 120, [P, 4, 512], F32)
        pack = at("pack", 84, [P, 2, 2, 4, 64], F32)
        qkt = at("qkt", 128, [P, 2, 2, 2, SEQ], F32R)
        vst = at("vst", 140, [P, 2, 2, 4, 2 * D], F32)
        ot = at("ot", 138, [P, SEQ], F32)
        woraw = at("woraw", 72, [P, KC, 512], F32)
        wos = at("wos", 88, [P, 2, KC, 512], F32R)
        aT = at("aT", 80, [P, 2, 2, KC, P], F32R)
        attc = at("attc", 36, [P, 2, E], F32)
        x1c = at("x1c", 108, [P, 2, E], F32)
        ro = at("ro", 112, [P, 2, E], F32)
        xres = at("xres", 154, [P, 2, E], F32)
        yacc = at("yacc", 24, [P, NT, E], F32)
        x1T = at("x1T", 40, [P, 2, KC, B * SEQ], F32R)
        wqs = at("wqs", 72, [P, XR, 2, KC, P], F32R)
        wxs = at("wxs", 88, [P, XR, 2, E], F32R)
        vwa = at("vwa", 104, [P, 2, 2, 2, E], F32R)
        vwb = at("vwb", 191, [P, 2, 2, 2, E], F32R)
        pT = at("pT", 120, [P, 2, 2, 8, P], F32R)
        vsp = at("vsp", 136, [P, 2, B * XS], F32R)
        nrow = at("nrow", 138, [P, SEQ], F32)
        qT = at("qT", 142, [P, 2, B * SEQ], F32)
        sq = at("sq", 150, [P, 2, B * SEQ], F32)
        wqraw = at("wqraw", 158, [P, XR, KC, P], F32)
        wxraw = at("wxraw", 166, [P, XR, E], F32)
        prob = at("prob", 174, [P, 2, 8, 2, XS], F32)
        lbs = at("lbs", 182, [P, E], F32)
        baseraw = at("baseraw", 158, [P, KC, E], F32)
        garaw = at("garaw", 184, [P, KC, NE + P], F32)
        gas = at("gas", 186.5, [P, 2, KC, NE + P], F32R)
        bases = at("bases", 72, [P, 2, KC, E], F32R)
        x2c = at("x2c", 142, [P, 2, E], F32)
        x2T = at("x2T", 40, [P, 2, KC, B * SEQ], F32R)
        lowm = at("lowm", 191, [P, NT, P], F32)
        lowT = at("lowT", 195, [P, NT, P], F32)
        fo = at("fo", 160, [P, 2, E], F32)
        fout = at("fout", 164, [P, 2, E], F32)
        gl = at("gl", 168, [P, NT, NE + P], F32)
        route = at("route", 173, [P, 8, NT, NE], F32)
        wts = at("wts", 175, [P, 8, NT], F32)

        d_const, d_ctx, d_wo, d_f = map(sem, ("d_const", "d_ctx", "d_wo", "d_f"))
        d_out = [sem(f"d_out{n}") for n in range(2)]
        d_kv = [sem(f"d_kv{n}") for n in range(4)]
        d_w = [sem(f"d_w{n}") for n in range(3)]
        d_x = [sem(f"d_x{n}") for n in range(2)]
        d_xres = [sem(f"d_xres{n}") for n in range(2)]
        d_wq = [sem(f"d_wq{n}") for n in range(XR)]
        d_wx = [sem(f"d_wx{n}") for n in range(XR)]
        consts_ready, dve_consts = sem("consts_ready"), sem("dve_consts")
        ctx_hi, ctx_lo, kv_hi, kv_lo = map(sem, ("ctx_hi", "ctx_lo", "kv_hi", "kv_lo"))
        k_mm, k_sq, k_ms, k_r, k_nat, k_tr, k_done = map(
            sem, ("k_mm", "k_sq", "k_ms", "k_r", "k_nat", "k_tr", "k_done"))
        v_mm, v_done = sem("v_mm"), sem("v_done")
        w_hi, w_lo, x_hi, x_lo = map(sem, ("w_hi", "w_lo", "x_hi", "x_lo"))
        qkv_mm, qkv_free, rope_step, rope_done = map(sem, ("qkv_mm", "qkv_free", "rope_step", "rope_done"))
        pack_hi, packed, tr_q, tr_k, qt_ready, kt_ready = map(
            sem, ("pack_hi", "packed", "tr_q", "tr_k", "qt_ready", "kt_ready"))
        s_mm, s_max, s_free, s_exp = map(sem, ("s_mm", "s_max", "s_free", "s_exp"))
        v_ready, pt_mm, pt_sb, pts_free, ot_sb, ob_mm, o_rec, o_norm = map(
            sem, ("v_ready", "pt_mm", "pt_sb", "pts_free", "ot_sb", "ob_mm", "o_rec", "o_norm"))
        wo_hi, wo_lo, a_copy, a_tr, a_hi, a_lo, o_mm, o_res, o_sum = map(
            sem, ("wo_hi", "wo_lo", "a_copy", "a_tr", "a_hi", "a_lo", "o_mm", "o_res", "o_sum"))
        o_stat, o_ve, o_rstd, x1_done, x1_tr, x1_hi, x1_free, y_init = map(
            sem, ("o_stat", "o_ve", "o_rstd", "x1_done", "x1_tr", "x1_hi", "x1_free", "y_init"))
        wq_hi, wq_lo, wx_hi, wx_lo = map(sem, ("wq_hi", "wq_lo", "wx_hi", "wx_lo"))
        q_mm, q_free, n_mm, n_row, n_tr, sx_mm = map(sem, ("q_mm", "q_free", "n_mm", "n_row", "n_tr", "sx_mm"))
        n_sb, n_r, p_scaled, p_masked, p_max, p_sub, p_exp, p_sum, p_rec, p_norm = map(
            sem, ("n_sb", "n_r", "p_scaled", "p_masked", "p_max", "p_sub", "p_exp", "p_sum", "p_rec", "p_norm"))
        xt_mm, xt_hi, xt_lo, z_hi, z_lo = map(sem, ("xt_mm", "xt_hi", "xt_lo", "z_hi", "z_lo"))
        vw_mm, vw_hi, vw_free, y_mm, y_add = map(sem, ("vw_mm", "vw_hi", "vw_free", "y_mm", "y_add"))
        b_hi, b_lo, f_stat, f_ve, f_rstd, f_x2, f_tr, f_hi, f_lo, f_bias = map(
            sem, ("b_hi", "b_lo", "f_stat", "f_ve", "f_rstd", "f_x2", "f_tr", "f_hi", "f_lo", "f_bias"))
        g_mm, g_sb, r_step, r_exp = map(sem, ("g_mm", "g_sb", "r_step", "r_exp"))
        l_low, l_tr, l_sb, l_mm, h_sum, h_stat, h_ve, h_rstd, h_out = map(
            sem, ("l_low", "l_tr", "l_sb", "l_mm", "h_sum", "h_stat", "h_ve", "h_rstd", "h_out"))
        dve_passed, pool_passed = sem("dve_passed"), sem("pool_passed")
        NCONST = 10

        def over(ap, n):
            return ap.unsqueeze(len(ap.shape)).broadcast_to([*ap.shape, n])

        def heads(ap, n):
            return ap.rearrange("p (a b) -> p a b", a=n)

        def pt_bank(j):
            return (6, 0)[j % 2]

        def vws(b):
            return (vwa, vwb)[b // 2][:, b % 2]

        def f_bank(t):
            return (t + NT // 2) % NT if isinstance(t, int) else t - NT // 2

        def y_bank(c):
            return (7, 4)[c]

        block = ctx.enter_context(nc.Block())

        @block.sync
        def _(sp):
            sp.dma_start(ctxraw[:], ctxT).then_inc(d_ctx, 16)
            for n in range(4):
                sp.dma_start(kvraw[:, n], (wkT, wvT)[n // 2][n % 2]).then_inc(d_kv[n], 16)
                if n == 3:
                    for dst, src in ((identf[:], ident), (maskx[:], mask.rearrange("(c p) k -> p c k", p=P)),
                                     (outbs[:], outb.partition_broadcast(P)),
                                     (basebs[:], baseb.partition_broadcast(P)),
                                     (qkvbs[:].rearrange("p a b -> p (a b)"), qkvb.partition_broadcast(P)),
                                     (ropes[:], rope), (wqn[:], qn), (wkn[:], kn),
                                     (orders[:], order.partition_broadcast(P)), (causf[:], causal)):
                        sp.dma_start(dst, src).then_inc(d_const, 16)
            for n in range(3):
                sp.dma_start(wraw[:, n], wqkv.rearrange("(k p) n -> p k n", p=P)[:, :, n * 512:(n + 1) * 512]
                             ).then_inc(d_w[n], 16)
                if n == 0:
                    for s in range(2):
                        sp.dma_start(xraw[:, s], xT[s]).then_inc(d_x[s], 16)
            with sp.Fori(1, NT // 2) as u:
                for s in range(2):
                    sp.wait_ge(x_lo, 2 * u + s - 1)
                    sp.wait_ge(x_hi, 2 * u + s - 1)
                    sp.dma_start(xraw[:, s], xT[2 * u + s]).then_inc(d_x[s], 16)
            sp.wait_ge(w_lo, 3)
            sp.wait_ge(w_hi, 3)
            sp.dma_start(woraw[:], wout.rearrange("(k p) n -> p k n", p=P)).then_inc(d_wo, 16)
            sp.wait_ge(packed, 2 * NI)
            for s in range(2):
                sp.dma_start(xres[:, s], x[s]).then_inc(d_xres[s], 16)
            for j in range(XR):
                sp.dma_start(wqraw[:, j], wqT[j]).then_inc(d_wq[j], 16)
            for j in range(XR):
                sp.dma_start(wxraw[:, j], woT[j]).then_inc(d_wx[j], 16)
            with sp.Fori(1, NT // 2) as u:
                for s in range(2):
                    sp.wait_ge(o_sum, 2 * u + s - 1)
                    sp.dma_start(xres[:, s], x[2 * u + s]).then_inc(d_xres[s], 16)
            sp.wait_ge(a_copy, NT)
            sp.dma_start(garaw[:, :, 0:NE], gateT).then_inc(d_f, 16)
            sp.dma_start(garaw[:, :, NE:], loraAT).then_inc(d_f, 16)
            sp.dma_start(lbs[:], loraB).then_inc(d_f, 16)

            def wq_load(g, j):
                sp.wait_ge(wq_lo, XR * g + j - (XR - 1))
                sp.wait_ge(wq_hi, XR * g + j - (XR - 1))
                sp.dma_start(wqraw[:, j], wqT[XR * g + j]).then_inc(d_wq[j], 16)

            def wx_load(g, j):
                sp.wait_ge(wx_lo, XR * g + j - (XR - 1))
                sp.wait_ge(wx_hi, XR * g + j - (XR - 1))
                sp.dma_start(wxraw[:, j], woT[XR * g + j]).then_inc(d_wx[j], 16)

            for j in range(XR):
                wq_load(1, j)
            with sp.Fori(2, XG) as g:
                for j in range(3):
                    wq_load(g, j)
                for j in range(XR):
                    wx_load(g - 1, j)
                wq_load(g, 3)
            sp.wait_ge(wq_lo, XR * XG)
            sp.wait_ge(wq_hi, XR * XG)
            sp.dma_start(baseraw[:], baseT).then_inc(d_f, 16)
            for j in range(XR):
                wx_load(XG - 1, j)
            with sp.Fori(0, NT // 2) as u:
                for s in range(2):
                    sp.wait_ge(h_out, 2 * u + s + 3)
                    sp.dma_start(out[2 * u + s], fout[:, s]).then_inc(d_out[s], 16)
            for s in range(2):
                sp.wait_ge(d_out[s], 16 * NT // 2)

        @block.gpsimd
        def _(pool):
            def minus(hi, lo, raw):
                return nc.gpsimd.tensor_tensor(lo, raw, hi.bitcast(F32), ALU.subtract)

            nc.gpsimd.memset(ones[:], 1.0).then_inc(consts_ready, 1)
            nc.gpsimd.memset(mhalf[:], -0.5).then_inc(consts_ready, 1)
            pool.wait_ge(consts_ready, 2)
            pool.wait_ge(d_ctx, 16)
            pool.wait_ge(ctx_hi, 1)
            minus(ctxs[:, 0], ctxs[:, 1], ctxraw[:]).then_inc(ctx_lo, 1)
            pool.wait_ge(d_kv[1], 16)
            pool.wait_ge(kv_hi, 2)
            pool.wait_ge(kv_lo, 1)
            minus(kvs[:, 1, 0], kvs[:, 1, 1], kvraw[:, 1]).then_inc(kv_lo, 1)
            for u in range(4):
                pool.wait_ge(k_ms, u + 1)
                nc.gpsimd.tensor_tensor(small[:, 32 + 4 * u:36 + 4 * u], small[:, 16 + 4 * u:20 + 4 * u],
                                        mhalf[:, 0:4], ALU.pow).then_inc(k_r, 1)

            def w_low(n):
                pool.wait_ge(d_w[n], 16)
                pool.wait_ge(w_hi, n + 1)
                minus(ws[:, 0, n], ws[:, 1, n], wraw[:, n]).then_inc(w_lo, 1)

            w_low(0)
            for s in range(2):
                pool.wait_ge(d_x[s], 16)
                pool.wait_ge(x_hi, s + 1)
                minus(xs[:, s, 0], xs[:, s, 1], xraw[:, s]).then_inc(x_lo, 1)
            pool.wait_ge(w_lo, 2)
            w_low(2)
            with pool.Fori(1, NT // 2) as u:
                for s in range(2):
                    pool.wait_ge(d_x[s], 16 * u + 16)
                    pool.wait_ge(x_hi, 2 * u + s + 1)
                    minus(xs[:, s, 0], xs[:, s, 1], xraw[:, s]).then_inc(x_lo, 1)

            nc.gpsimd.memset(pack[:], 0.0).then_inc(consts_ready, 1)
            pool.wait_ge(consts_ready, 3)
            nc.gpsimd.memset(pack[:, 0, 0, :, 3 * D], MASK_A).then_inc(consts_ready, 1)
            nc.gpsimd.memset(pack[:, 1, 1, :, 3 * D], MASK_B).then_inc(pack_hi, 1)
            nc.gpsimd.memset(vst[:], 1.0).then_inc(v_ready, 1)
            pool.wait_ge(consts_ready, 4)
            pool.wait_ge(pack_hi, 1)
            pool.wait_ge(v_ready, 1)

            def pack_qk(i):
                pool.wait_ge(tr_k, i + 1)
                for a in range(2):
                    nat = qk[:, i, :, a, :].rearrange("p c (j d) -> p c j d", j=4)
                    hi = pack[:, a, :, :, 0:D]
                    hi2 = pack[:, a, :, :, (1 + a) * D:(2 + a) * D]
                    lo = pack[:, a, :, :, (2 - a) * D:(3 - a) * D]
                    nc.gpsimd.tensor_copy(hi.bitcast(F32R), nat).then_inc(pack_hi, 1)
                    nc.gpsimd.tensor_copy(hi2.bitcast(F32R), nat).then_inc(pack_hi, 1)
                    pool.wait_ge(pack_hi, 4 * i + 2 * a + 3)
                    pool.sem_inc(pool_passed, 1)
                    nc.gpsimd.tensor_tensor(lo, nat, hi, ALU.subtract).then_inc(packed, 1)

            def v_copy(i, par):
                nc.gpsimd.tensor_copy(vst[:, par, :, :, 0:D], vx[:, i]).then_inc(v_ready, 1)

            pool.wait_ge(rope_done, 2 * 2 + 1)
            pack_qk(0)
            v_copy(0, 0)
            pack_qk(1)
            pool.wait_ge(rope_done, 2 * NT + 1)
            with pool.Fori(1, NI // 2) as u:
                for par in range(2):
                    i = 2 * u + par
                    pack_qk(i)
                    pool.wait_ge(pts_free, 4 * i - 4)
                    v_copy(i - 1, 1 - par)
            pool.wait_ge(pts_free, 4 * NI - 4)
            v_copy(NI - 1, 1)

            def wq_low(h, j):
                pool.wait_ge(wq_hi, h + 1)
                minus(wqs[:, j, 0], wqs[:, j, 1], wqraw[:, j]).then_inc(wq_lo, 1)

            pool.wait_ge(wo_hi, 1)
            minus(wos[:, 0], wos[:, 1], woraw[:]).then_inc(wo_lo, 1)
            wq_low(0, 0)
            wq_low(1, 1)
            with pool.Fori(0, NT // 2) as u:
                for s in range(2):
                    pool.wait_ge(d_xres[s], 16 * u + 16)
                    nc.gpsimd.tensor_tensor(xres[:, s], xres[:, s], outbs[:], ALU.add).then_inc(o_res, 1)
                    pool.wait_ge(o_ve, 2 * u + s + 1)
                    nc.gpsimd.tensor_tensor(small[:, 64 + s:65 + s], small[:, 62 + s:63 + s], mhalf[:, 0:1],
                                            ALU.pow).then_inc(o_rstd, 1)

            def prob_of(j):
                return prob[:, j // 2, :, j % 2, :]

            def query_rms(h):
                pool.wait_ge(n_sb, h + 1)
                nc.gpsimd.tensor_tensor(small[:, 80:88], small[:, 72:80], mhalf[:], ALU.pow).then_inc(n_r, 1)

            def add_mask(h, j):
                p = prob_of(j)
                m = maskx[:].unsqueeze(1).broadcast_to([P, B, 2, XS])
                pool.wait_ge(p_scaled, h + 1)
                nc.gpsimd.tensor_tensor(p.rearrange("p (b c) k -> p b c k", b=B),
                                        p.rearrange("p (b c) k -> p b c k", b=B), m, ALU.add).then_inc(p_masked, 1)

            def less_max(h, j):
                pool.wait_ge(p_max, h + 1)
                nc.gpsimd.tensor_tensor(prob_of(j), prob_of(j), over(small[:, 88:96], XS),
                                        ALU.subtract).then_inc(p_sub, 1)

            def over_sum(h, j):
                pool.wait_ge(p_rec, h + 1)
                nc.gpsimd.tensor_tensor(prob_of(j), prob_of(j), over(small[:, 104:112], XS),
                                        ALU.mult).then_inc(p_norm, 1)

            def wx_low(h, j):
                pool.wait_ge(wx_hi, h + 1)
                minus(wxs[:, j, 0], wxs[:, j, 1], wxraw[:, j]).then_inc(wx_lo, 1)

            def finish(g, more):
                h = XR * g + 3
                less_max(h, 3)
                wx_low(h, 3)
                over_sum(h, 3)
                if more:
                    wq_low(h + 4, 3)

            def attend(g, more):
                h = XR * g
                if more:
                    wq_low(h + 4, 0)
                query_rms(h)
                add_mask(h, 0)
                less_max(h, 0)
                if more:
                    wq_low(h + 5, 1)
                over_sum(h, 0)
                query_rms(h + 1)
                add_mask(h + 1, 1)
                less_max(h + 1, 1)
                over_sum(h + 1, 1)
                if more:
                    wq_low(h + 6, 2)
                query_rms(h + 2)
                add_mask(h + 2, 2)
                wx_low(h, 0)
                less_max(h + 2, 2)
                wx_low(h + 1, 1)
                over_sum(h + 2, 2)
                query_rms(h + 3)
                wx_low(h + 2, 2)
                pool.wait_ge(z_hi, g + 1)
                minus(vsp[:, 0], vsp[:, 1], VTx[:, g]).then_inc(z_lo, 1)
                add_mask(h + 3, 3)

            wq_low(2, 2)
            wq_low(3, 3)
            attend(0, True)
            with pool.Fori(1, XG - 1) as g:
                finish(g - 1, True)
                attend(g, True)
            finish(XG - 2, True)
            attend(XG - 1, False)
            finish(XG - 1, False)

            pool.wait_ge(b_hi, 1)
            minus(gas[:, 0], gas[:, 1], garaw[:]).then_inc(b_lo, 1)

            def layer2(t, s):
                pool.wait_ge(f_ve, t + 1)
                nc.gpsimd.tensor_tensor(small[:, 162 + s:163 + s], small[:, 160 + s:161 + s], mhalf[:, 0:1],
                                        ALU.pow).then_inc(f_rstd, 1)
                pool.wait_ge(f_x2, t + 1)
                nc.gpsimd.tensor_tensor(yacc[:, t], x2c[:, s], basebs[:], ALU.add).then_inc(f_bias, 1)

            layer2(0, 0)
            layer2(1, 1)
            pool.wait_ge(b_hi, 2)
            minus(bases[:, 0], bases[:, 1], baseraw[:]).then_inc(b_lo, 1)
            with pool.Fori(1, NT // 2) as u:
                for s in range(2):
                    layer2(2 * u + s, s)
            with pool.Fori(0, NT // 2) as u:
                for s in range(2):
                    pool.wait_ge(h_ve, 2 * u + s + 1)
                    nc.gpsimd.tensor_tensor(small[:, 182 + s:183 + s], small[:, 180 + s:181 + s], mhalf[:, 0:1],
                                            ALU.pow).then_inc(h_rstd, 1)

        @block.scalar
        def _(act):
            def copy(dst, src):
                return nc.scalar.activation(dst, src, ACT.Copy)

            act.sem_inc(q_free, 2)
            act.sem_inc(g_sb, 2)
            for u in range(4):
                act.wait_ge(k_mm, u + 1)
                for g in range(4):
                    act.wait_ge(k_sq, 4 * u + g)
                    nc.scalar.activation(junk[:], ps[:, u, g * XD:(g + 1) * XD], ACT.Square,
                                         accum_out=small[:, 4 * u + g:4 * u + g + 1]).then_inc(k_sq, 1)
            act.wait_ge(dve_consts, 1)
            for u in range(4):
                act.wait_ge(k_tr, u + 1)
                n, t = u // 2, u % 2
                nc.scalar.activation(KTx[:, 4 * n:4 * n + 4, t * P:(t + 1) * P], heads(ps[:, 4 + u % 2, :], 4),
                                     ACT.Copy, scale=wqk[:, 0:1]).then_inc(k_done, 1)

            def q_out(i, par):
                act.wait_ge(tr_q, i + 1)
                copy(qkt[:, par, 0].rearrange("p a b -> p (a b)"), ps[:, 0, :]).then_inc(qt_ready, 1)

            def k_out(i, par):
                act.wait_ge(tr_k, i + 2)
                copy(qkt[:, par, 1].rearrange("p a b -> p (a b)"), ps[:, 1, :]).then_inc(kt_ready, 1)

            def exps(i, par, c):
                act.wait_ge(s_free, 2 * i + c + 3)
                nc.scalar.activation(sb[:, par, c], sb[:, par, c], ACT.Exp, scale=0.25).then_inc(s_exp, 1)

            def pt_out(i, exp_next, k_next):
                for f in range(4):
                    act.wait_ge(pt_mm, 4 * i + f + 1)
                    act.wait_ge(pts_free, 4 * i + f + 1)
                    copy(pts[:, f], ps[:, pt_bank(f), :]).then_inc(pt_sb, 1)
                    if f == 1 and k_next:
                        k_out(i + 2, 1 - exp_next)
                    if f == 1 and exp_next is not None:
                        exps(i + 1, exp_next, 0)

            def ot_out(i, first=False):
                act.wait_ge(pts_free, 4 * i + 8)
                if not first:
                    act.wait_ge(ob_mm, i)
                copy(ot[:], ps[:, 7, 0:SEQ]).then_inc(ot_sb, 1)

            def a_copies(u, s):
                act.wait_ge(o_norm, HQ * (u + 1))
                copy(heads(attc[:, s], HQ), att[:, bass.ds(u * HQ, HQ), s, :]).then_inc(a_copy, 1)

            def a_parts(u, s):
                t = 2 * u + s
                act.wait_ge(a_tr, t + 1)
                copy(aT[:, s, 0], heads(ps[:, 2 + s, :], 4)).then_inc(a_hi, 1)

            def x1_parts(u, s):
                t = 2 * u + s
                act.wait_ge(x1_tr, t + 1)
                copy(x1T[:, 0, :, bass.ds(t * P, P)], heads(ps[:, 6 + s, :], 4)).then_inc(x1_hi, 1)
                copy(yacc[:, t], x1c[:, s]).then_inc(y_init, 1)

            act.sem_inc(y_init, 2)
            q_out(0, 0)
            k_out(0, 0)
            q_out(1, 1)
            k_out(1, 1)
            exps(0, 0, 0)
            exps(0, 0, 1)
            q_out(2, 0)
            pt_out(0, 1, True)
            exps(1, 1, 1)
            ot_out(0, True)
            with act.Fori(1, NI // 2 - 1) as u:
                for par in range(2):
                    i = 2 * u + par
                    q_out(i + 1, 1 - par)
                    pt_out(i - 1, par, True)
                    exps(i, par, 1)
                    ot_out(i - 1)
            for i in (NI - 2, NI - 1):
                if i < NI - 1:
                    q_out(i + 1, 1)
                pt_out(i - 1, i % 2, i < NI - 1)
                exps(i, i % 2, 1)
                ot_out(i - 1)
                a_copies(0, i % 2)
            pt_out(NI - 1, None, False)
            a_parts(0, 0)
            ot_out(NI - 1)

            act.wait_ge(a_tr, 1)
            a_copies(1, 0)
            a_parts(0, 1)
            with act.Fori(1, NT // 2 - 1) as u:
                act.wait_ge(a_tr, 2 * u)
                a_copies(u, 1)
                a_parts(u, 0)
                x1_parts(u - 1, 0)
                act.wait_ge(a_tr, 2 * u + 1)
                a_copies(u + 1, 0)
                a_parts(u, 1)
                x1_parts(u - 1, 1)
            act.wait_ge(a_tr, NT - 2)
            a_copies(NT // 2 - 1, 1)
            for u in range(NT // 2 - 2, NT // 2):
                for s in range(2):
                    if u == NT // 2 - 2:
                        a_parts(u + 1, s)
                    x1_parts(u, s)

            def q_parts(g, j, nh):
                act.wait_ge(q_mm, 8 * g + 2 * j + nh + 1)
                sl = slice(nh * 512, nh * 512 + 512)
                nc.scalar.activation(sq[:, j % 2, sl], ps[:, nh, :], ACT.Square)
                copy(qT[:, j % 2, sl], ps[:, nh, :]).then_inc(q_free, 1)

            def xt_high(g, k):
                act.wait_ge(xt_mm, 4 * g + k + 1)
                copy(pT[:, 0, k // 2, 4 * (k % 2):4 * (k % 2) + 4, :], heads(ps[:, 4, :], 4)).then_inc(xt_hi, 1)

            def norm_row(g, j):
                act.wait_ge(n_mm, XR * g + j + 1)
                copy(nrow[:], ps[:, 3, 0:SEQ]).then_inc(n_row, 1)

            def vw_high(g, n):
                act.wait_ge(vw_mm, 8 * g + n + 2)
                pair, head = n // 4, n % 4
                for d in range(2):
                    last = copy(vws(2 * pair + d)[XS * (head % 2):XS * (head % 2 + 1), 0, head // 2, :],
                                ps[XS * d:XS * (d + 1), 5 + n % 2, :])
                last.then_inc(vw_hi, 1)

            def exp_of(g, j):
                act.wait_ge(p_sub, XR * g + j + 1)
                p = prob[:, j // 2, :, j % 2, :]
                nc.scalar.activation(p, p, ACT.Exp).then_inc(p_exp, 1)

            def z_high(g):
                act.wait_ge(vw_mm, 8 * g + 1)
                copy(vsp[:, 0], VTx[:, g, :]).then_inc(z_hi, 1)

            def group(g, one, two):
                for n in range(2):
                    if one:
                        q_parts(g, 0, n)
                    if two:
                        xt_high(g - 1, n)
                        if n == 0:
                            exp_of(g - 1, 3)
                if one:
                    q_parts(g, 1, 0)
                    norm_row(g, 0)
                if two:
                    vw_high(g - 1, 0)
                    vw_high(g - 1, 1)
                    xt_high(g - 1, 2)
                if one:
                    q_parts(g, 1, 1)
                if two:
                    vw_high(g - 1, 2)
                    vw_high(g - 1, 3)
                    xt_high(g - 1, 3)
                if one:
                    exp_of(g, 0)
                if one:
                    q_parts(g, 2, 0)
                    norm_row(g, 1)
                    q_parts(g, 2, 1)
                if two:
                    vw_high(g - 1, 4)
                    vw_high(g - 1, 5)
                if one:
                    exp_of(g, 1)
                    q_parts(g, 3, 0)
                    norm_row(g, 2)
                if two:
                    vw_high(g - 1, 6)
                    vw_high(g - 1, 7)
                if one:
                    q_parts(g, 3, 1)
                    norm_row(g, 3)
                    z_high(g)
                    exp_of(g, 2)

            def last_projection(g):
                xt_high(g, 0)
                vw_high(g, 0)
                xt_high(g, 1)
                vw_high(g, 1)
                exp_of(g, 3)
                vw_high(g, 2)
                vw_high(g, 3)
                xt_high(g, 2)
                xt_high(g, 3)
                act.wait_ge(d_f, 64)
                copy(gas[:, 0], garaw[:]).then_inc(b_hi, 1)
                for n in range(4, 8):
                    vw_high(g, n)
                act.wait_ge(q_mm, 8 * XG)
                copy(bases[:, 0], baseraw[:]).then_inc(b_hi, 1)

            group(0, True, False)
            with act.Fori(1, XG) as g:
                group(g, True, True)
            last_projection(XG - 1)

            def x2_parts(t, s):
                act.wait_ge(f_tr, t + 1)
                copy(x2T[:, 0, :, bass.ds(t * P, P)], heads(ps[:, s, :], 4)).then_inc(f_hi, 1)

            def gates_out(t, s):
                act.wait_ge(g_mm, t + 1)
                copy(gl[:, t], ps[:, 2 + s, 0:NE + P]).then_inc(g_sb, 1)

            x2_parts(0, 0)
            x2_parts(1, 1)
            with act.Fori(1, NT // 2) as u:
                for s in range(2):
                    gates_out(2 * u + s - 2, s)
                    x2_parts(2 * u + s, s)
            gates_out(NT - 2, 0)
            gates_out(NT - 1, 1)
            act.wait_ge(r_step, 8)
            nc.scalar.activation(wts[:, 2], wts[:, 2], ACT.Exp).then_inc(r_exp, 1)
            for n in range(2):
                act.wait_ge(l_tr, n + 1)
                copy(lowT[:, 4 * n:4 * n + 4], heads(ps[:, 2 + n, :], 4)).then_inc(l_sb, 1)

            def sum_out(t, s):
                act.wait_ge(l_mm, t + 1)
                act.wait_ge(h_out, t + 1)
                copy(fo[:, s], ps[:, f_bank(t), :]).then_inc(h_sum, 1)

            for t in range(NT // 2):
                sum_out(t, t % 2)
            with act.Fori(NT // 4, NT // 2) as u:
                for s in range(2):
                    sum_out(2 * u + s, s)

        @block.vector
        def _(dve):
            tt = nc.vector.tensor_tensor

            def high(hi, raw):
                return nc.vector.tensor_copy(hi, raw)

            def stats(src, at6, at2, step, n):
                nc.vector.bn_stats(small[:, at6:at6 + 6], src).then_inc(step, 1)
                dve.wait_ge(step, n + 1)
                dve.sem_inc(dve_passed, 1)
                nc.vector.bn_aggr(small[:, at2:at2 + 2], small[:, at6:at6 + 6]).then_inc(step, 1)
                dve.wait_ge(step, n + 2)

            dve.sem_inc(qkv_free, 6)
            dve.sem_inc(s_free, 2)
            dve.sem_inc(vw_free, 2)
            for started in (rope_done, xt_lo):
                dve.sem_inc(started, 1)
            dve.sem_inc(y_add, 2)
            dve.sem_inc(h_out, 2)
            dve.wait_ge(d_ctx, 16)
            high(ctxs[:, 0], ctxraw[:]).then_inc(ctx_hi, 1)

            def kv_high(n):
                dve.wait_ge(d_kv[n], 16)
                high(kvs[:, n % 2, 0], kvraw[:, n]).then_inc(kv_hi, 1)

            def key_ms(u):
                dve.wait_ge(k_sq, 4 * u + 4)
                nc.vector.tensor_scalar(small[:, 16 + 4 * u:20 + 4 * u], small[:, 4 * u:4 * u + 4], 1.0 / XD, EPS,
                                        ALU.mult, ALU.add).then_inc(k_ms, 1)

            def key_scale(u):
                dve.wait_ge(k_r, u + 1)
                tt(heads(knat[:, u], 4), heads(ps[:, u, :], 4), over(small[:, 32 + 4 * u:36 + 4 * u], XD),
                   ALU.mult).then_inc(k_nat, 1)

            def kv_low(n):
                dve.wait_ge(kv_hi, n + 1)
                dve.wait_ge(kv_lo, n)
                tt(kvs[:, n % 2, 1], kvraw[:, n], kvs[:, n % 2, 0].bitcast(F32), ALU.subtract).then_inc(kv_lo, 1)

            def value_out(v):
                dve.wait_ge(v_mm, v + 1)
                nc.vector.tensor_copy(VTx[:, 2 * v:2 * v + 2], heads(ps[:, 6 + v % 2, :], 2)).then_inc(v_done, 1)

            def w_high(n):
                dve.wait_ge(d_w[n], 16)
                high(ws[:, 0, n], wraw[:, n]).then_inc(w_hi, 1)

            def x_high(u, s):
                dve.wait_ge(d_x[s], 16 * u + 16)
                high(xs[:, s, 0], xraw[:, s]).then_inc(x_hi, 1)

            kv_high(0)
            kv_low(0)
            kv_high(1)
            dve.wait_ge(k_mm, 2)
            kv_high(2)
            kv_low(2)
            key_ms(0)
            key_ms(1)
            dve.wait_ge(k_mm, 4)
            kv_high(3)
            kv_low(3)
            key_ms(2)
            key_ms(3)
            value_out(0)
            w_high(0)
            x_high(0, 0)
            value_out(1)
            x_high(0, 1)
            for u in range(4):
                key_scale(u)
            dve.wait_ge(d_const, 16 * NCONST)
            nc.vector.tensor_scalar(wqk[:], wqn[:], wkn[:, 0:1], XD ** -0.5, ALU.mult, ALU.mult).then_inc(dve_consts, 1)
            w_high(1)
            dve.wait_ge(w_hi, 2)
            dve.wait_ge(w_lo, 1)
            tt(ws[:, 1, 1], wraw[:, 1], ws[:, 0, 1].bitcast(F32), ALU.subtract).then_inc(w_lo, 1)
            w_high(2)
            value_out(2)
            value_out(3)
            nc.vector.tensor_copy(causb[:], causf[:]).then_inc(dve_consts, 1)
            nc.vector.tensor_scalar(diagb[:], identf[:], MASK_A, None, ALU.mult).then_inc(dve_consts, 1)

            dve.wait_ge(kv_lo, 4)
            def project(u, s, more):
                t = 2 * u + s
                dve.wait_ge(rope_done, 2 * t + 1)
                for n in range(2):
                    dve.wait_ge(qkv_mm, 3 * t + n + 1)
                    tt(qraw[:, n], ps[:, 3 * s + n, :], qkvbs[:, n], ALU.add).then_inc(qkv_free, 1)
                dve.wait_ge(qkv_mm, 3 * t + 3)
                tt(vx[:, bass.ds(u * HQ, HQ), s, :, 0:D],
                   ps[:, 3 * s + 2, :].rearrange("p (a j d) -> p a j d", a=HQ, j=4),
                   qkvbs[:, 2].rearrange("p (a j d) -> p a j d", a=HQ, j=4), ALU.add).then_inc(qkv_free, 1)
                dve.wait_ge(qkv_free, 3 * t + 8)
                raw = qraw[:].rearrange("p n (h d) -> p (n h) d", d=D)
                rot = qrot[:].rearrange("p n (h d) -> p (n h) d", d=D)
                for a in range(2):
                    half = slice((1 - a) * D // 2, (2 - a) * D // 2)
                    own = slice(a * D // 2, (a + 1) * D // 2)
                    sin = ropes[:, s, 1, own].unsqueeze(1).broadcast_to([P, 2 * H, D // 2])
                    tt(rot[:, :, own], raw[:, :, half], sin, ALU.mult).then_inc(rope_step, 1)
                dve.wait_ge(rope_step, 4 * t + 2)
                for n in range(2):
                    cos = ropes[:, s, 0, :].unsqueeze(1).broadcast_to([P, H, D])
                    tt(qraw[:, n].rearrange("p (h d) -> p h d", d=D),
                       qraw[:, n].rearrange("p (h d) -> p h d", d=D), cos, ALU.mult).then_inc(rope_step, 1)
                dve.wait_ge(rope_step, 4 * t + 4)
                for n in range(2):
                    tt(qk[:, bass.ds(u * HQ, HQ), s, n, :], heads(qraw[:, n], HQ), heads(qrot[:, n], HQ),
                       ALU.add).then_inc(rope_done, 1)
                if more:
                    x_high(u + 1, s)

            with dve.Fori(0, NT // 2 - 1) as u:
                for s in range(2):
                    dve.wait_ge(x_lo, 2 * u + s + 1)
                    project(u, s, True)
            for s in range(2):
                project(NT // 2 - 1, s, False)

            def top_of(c):
                return heads(small[:, 112 + 4 * c:116 + 4 * c], 2)

            def scores_of(c):
                return ps[:, 2 + 2 * c:4 + 2 * c, :].rearrange("p r (j k) -> p r j k", j=2)

            def score_max(i, c):
                dve.wait_ge(s_mm, 2 * i + c + 1)
                nc.vector.tensor_reduce(top_of(c), scores_of(c), AX.X, ALU.max).then_inc(s_max, 1)

            def less_max(i, par, c):
                dve.wait_ge(s_max, 2 * i + c + 1)
                tt(sb[:, par, c].rearrange("p (j r) k -> p r j k", r=2), scores_of(c), over(top_of(c), SEQ),
                   ALU.subtract).then_inc(s_free, 1)

            out_of = ps[:, 7, SEQ:].rearrange("p (h d) -> p h d", d=2 * D)

            def sum_over(i):
                dve.wait_ge(ob_mm, i + 1)
                nc.vector.reciprocal(small[:, 120:128], out_of[:, :, D]).then_inc(o_rec, 1)

            def norm_out(i):
                dve.wait_ge(o_rec, i + 1)
                tt(att[:, i].rearrange("p c (j d) -> p (c j) d", d=D), out_of[:, :, 0:D], over(small[:, 120:128], D),
                   ALU.mult).then_inc(o_norm, 1)

            def quad(i, par, norm=True):
                score_max(i, 0)
                less_max(i, par, 0)
                if norm:
                    sum_over(i - 2)
                    norm_out(i - 2)
                score_max(i, 1)
                less_max(i, par, 1)

            quad(0, 0, False)
            quad(1, 1, False)
            with dve.Fori(1, NI // 2 - 1) as u:
                for par in range(2):
                    quad(2 * u + par, par)
            dve.wait_ge(d_wo, 16)
            high(wos[:, 0], woraw[:]).then_inc(wo_hi, 1)
            quad(NI - 2, 0)
            quad(NI - 1, 1)
            sum_over(NI - 2)
            norm_out(NI - 2)
            def wq_high(g, j):
                dve.wait_ge(d_wq[j], 16 * g + 16)
                high(wqs[:, j, 0], wqraw[:, j]).then_inc(wq_hi, 1)

            dve.wait_ge(wo_lo, 1)
            wq_high(0, 0)
            wq_high(0, 1)

            dve.sem_inc(x1_free, 2)

            def a_low(t, s):
                dve.wait_ge(a_hi, t + 1)
                tt(aT[:, s, 1], heads(ps[:, 2 + s, :], 4), aT[:, s, 0].bitcast(F32), ALU.subtract).then_inc(a_lo, 1)

            def x1_low(t, s):
                dve.wait_ge(x1_hi, t + 1)
                own = bass.ds(t * P, P)
                tt(x1T[:, 1, :, own], heads(ps[:, 6 + s, :], 4), x1T[:, 0, :, own].bitcast(F32),
                   ALU.subtract).then_inc(x1_free, 1)

            def layer1a(t, s):
                dve.wait_ge(o_mm, t + 1)
                dve.wait_ge(o_res, t + 1)
                tt(ro[:, s], ps[:, 4 + s, :], xres[:, s], ALU.add).then_inc(o_sum, 1)
                dve.wait_ge(o_sum, t + 1)
                stats(ro[:, s], 128 + 6 * s, 140 + 2 * s, o_stat, 2 * t)
                nc.vector.tensor_scalar(small[:, 62 + s:63 + s], small[:, 141 + 2 * s:142 + 2 * s], EPS, None,
                                        ALU.add).then_inc(o_ve, 1)

            def layer1b(t, s):
                dve.wait_ge(o_rstd, t + 1)
                dve.wait_ge(y_init, t + 1)
                nc.vector.tensor_scalar(x1c[:, s], ro[:, s], small[:, 140 + 2 * s:141 + 2 * s],
                                        small[:, 64 + s:65 + s], ALU.subtract, ALU.mult).then_inc(x1_done, 1)

            a_low(0, 0)
            sum_over(NI - 1)
            norm_out(NI - 1)
            a_low(1, 1)
            layer1a(0, 0)
            with dve.Fori(1, NT // 2) as u:
                for s in range(2):
                    t = 2 * u + s
                    a_low(t, s)
                    layer1b(t - 2, s)
                    layer1a(t - 1, 1 - s)
                    x1_low(t - 2, s)
            layer1b(NT - 2, 0)
            layer1a(NT - 1, 1)
            x1_low(NT - 2, 0)
            layer1b(NT - 1, 1)
            x1_low(NT - 1, 1)

            def wx_high(g, j):
                dve.wait_ge(d_wx[j], 16 * g + 16)
                high(wxs[:, j, 0], wxraw[:, j]).then_inc(wx_hi, 1)

            def mean_square(g, j):
                dve.wait_ge(n_tr, XR * g + j + 1)
                sums = ps[:, 3, SEQ:].rearrange("p (c b e) -> p b c e", c=2, b=B)[:, :, :, 0]
                nc.vector.tensor_scalar(small[:, 72:80].rearrange("p (b c) -> p b c", b=B), sums, 1.0 / XD, EPS,
                                        ALU.mult, ALU.add).then_inc(n_sb, 1)

            def scores_out(g, j):
                dve.wait_ge(sx_mm, XR * g + j + 1)
                dve.wait_ge(n_r, XR * g + j + 1)
                tt(prob[:, j // 2, :, j % 2, :], heads(ps[:, 2, :], 8), over(small[:, 80:88], XS), ALU.mult
                   ).then_inc(p_scaled, 1)

            def row_max(g, j):
                dve.wait_ge(p_masked, XR * g + j + 1)
                nc.vector.tensor_reduce(small[:, 88:96], prob[:, j // 2, :, j % 2, :], AX.X, ALU.max
                                        ).then_inc(p_max, 1)

            def row_sum(g, j):
                dve.wait_ge(p_exp, XR * g + j + 1)
                nc.vector.tensor_reduce(small[:, 96:104], prob[:, j // 2, :, j % 2, :], AX.X, ALU.add
                                        ).then_inc(p_sum, 1)
                dve.wait_ge(p_sum, XR * g + j + 1)
                nc.vector.reciprocal(small[:, 104:112], small[:, 96:104]).then_inc(p_rec, 1)

            def xt_low(g, k):
                dve.wait_ge(xt_hi, 4 * g + k + 1)
                own = slice(4 * (k % 2), 4 * (k % 2) + 4)
                tt(pT[:, 1, k // 2, own, :], heads(ps[:, 4, :], 4), pT[:, 0, k // 2, own, :].bitcast(F32),
                   ALU.subtract).then_inc(xt_lo, 1)

            def vw_low(g, n):
                dve.wait_ge(vw_hi, 8 * g + n + 1)
                pair, head = n // 4, n % 4
                for d in range(2):
                    own = slice(XS * (head % 2), XS * (head % 2 + 1))
                    last = tt(vws(2 * pair + d)[own, 1, head // 2, :], ps[XS * d:XS * (d + 1), 5 + n % 2, :],
                              vws(2 * pair + d)[own, 0, head // 2, :].bitcast(F32), ALU.subtract)
                last.then_inc(vw_free, 1)

            def y_sum(g, b, c):
                dve.wait_ge(y_mm, 8 * g + 2 * b + c + 1)
                tt(yacc[:, 2 * b + c], ps[:, y_bank(c), :], yacc[:, 2 * b + c], ALU.add).then_inc(y_add, 1)

            def next_wq(g, j):
                dve.wait_ge(q_mm, 8 * g + 2 * j + 2)
                wq_high(g + 1, j)

            def group(g, one, two, more):
                if two:
                    xt_low(g - 1, 0)
                    row_sum(g - 1, 3)
                    xt_low(g - 1, 1)
                if more:
                    next_wq(g, 0)
                if one:
                    mean_square(g, 0)
                if two:
                    vw_low(g - 1, 0)
                    vw_low(g - 1, 1)
                if one:
                    scores_out(g, 0)
                if two:
                    xt_low(g - 1, 2)
                if one:
                    row_max(g, 0)
                if two:
                    vw_low(g - 1, 2)
                    vw_low(g - 1, 3)
                    xt_low(g - 1, 3)
                if more:
                    next_wq(g, 1)
                if one:
                    row_sum(g, 0)
                if one:
                    mean_square(g, 1)
                if two:
                    y_sum(g - 1, 0, 0)
                if one:
                    scores_out(g, 1)
                if two:
                    y_sum(g - 1, 0, 1)
                if one:
                    row_max(g, 1)
                if two:
                    vw_low(g - 1, 4)
                    vw_low(g - 1, 5)
                if more:
                    next_wq(g, 2)
                if one:
                    row_sum(g, 1)
                if two:
                    y_sum(g - 1, 1, 0)
                if one:
                    mean_square(g, 2)
                if two:
                    vw_low(g - 1, 6)
                    vw_low(g - 1, 7)
                if one:
                    scores_out(g, 2)
                    dve.wait_ge(vw_mm, 8 * g + 1)
                    wx_high(g, 0)
                    wx_high(g, 1)
                    row_max(g, 2)
                    wx_high(g, 2)
                    wx_high(g, 3)
                if two:
                    y_sum(g - 1, 1, 1)
                if more:
                    next_wq(g, 3)
                if two:
                    y_sum(g - 1, 2, 0)
                if one:
                    row_sum(g, 2)
                    mean_square(g, 3)
                if two:
                    y_sum(g - 1, 2, 1)
                if one:
                    scores_out(g, 3)
                if two:
                    y_sum(g - 1, 3, 0)
                    y_sum(g - 1, 3, 1)
                if one:
                    row_max(g, 3)

            wq_high(0, 2)
            wq_high(0, 3)
            dve.wait_ge(y_init, NT + 2)
            group(0, True, False, True)
            with dve.Fori(1, XG - 1) as g:
                group(g, True, True, True)
            group(XG - 1, True, True, False)

            def layer2a(t, s):
                dve.wait_ge(y_add, 8 * (XG - 1) + t + 3)
                stats(yacc[:, t], 144 + 6 * s, 156 + 2 * s, f_stat, 2 * t)
                nc.vector.tensor_scalar(small[:, 160 + s:161 + s], small[:, 157 + 2 * s:158 + 2 * s], EPS, None,
                                        ALU.add).then_inc(f_ve, 1)

            def layer2b(t, s, first=False):
                dve.wait_ge(f_rstd, t + 1)
                if not first:
                    dve.wait_ge(f_bias, t - 1)
                nc.vector.tensor_scalar(x2c[:, s], yacc[:, t], small[:, 156 + 2 * s:157 + 2 * s],
                                        small[:, 162 + s:163 + s], ALU.subtract, ALU.mult).then_inc(f_x2, 1)

            def x2_low(t, s):
                dve.wait_ge(f_hi, t + 1)
                own = bass.ds(t * P, P)
                tt(x2T[:, 1, :, own], heads(ps[:, s, :], 4), x2T[:, 0, :, own].bitcast(F32), ALU.subtract
                   ).then_inc(f_lo, 1)

            g = XG - 1
            xt_low(g, 0)
            vw_low(g, 0)
            xt_low(g, 1)
            vw_low(g, 1)
            row_sum(g, 3)
            vw_low(g, 2)
            vw_low(g, 3)
            xt_low(g, 2)
            xt_low(g, 3)
            vw_low(g, 4)
            vw_low(g, 5)
            y_sum(g, 0, 0)
            vw_low(g, 6)
            vw_low(g, 7)
            y_sum(g, 0, 1)
            layer2a(0, 0)
            y_sum(g, 1, 0)
            layer2a(1, 1)
            y_sum(g, 1, 1)
            layer2b(0, 0, True)
            y_sum(g, 2, 0)
            layer2b(1, 1, True)
            for b, c in ((2, 1), (3, 0), (3, 1)):
                y_sum(g, b, c)
            x2_low(0, 0)
            with dve.Fori(0, NT // 2 - 1) as u:
                for s in range(2):
                    t = 2 * u + s
                    layer2a(t + 2, s)
                    x2_low(t + 1, 1 - s)
                    layer2b(t + 2, s)
            x2_low(NT - 1, 1)

            logits = gl[:, :, 0:NE]
            rank = orders[:].unsqueeze(1).broadcast_to([P, NT, NE])
            one, two = route[:, 1], route[:, 4]
            steps = [0]

            def then(ins):
                ins.then_inc(r_step, 1)
                steps[0] += 1
                dve.wait_ge(r_step, steps[0])

            dve.wait_ge(g_sb, NT + 2)
            then(nc.vector.tensor_reduce(wts[:, 0], logits, AX.X, ALU.max))
            then(tt(route[:, 0], logits, over(wts[:, 0], NE), ALU.is_equal))
            then(tt(route[:, 0], route[:, 0], rank, ALU.mult))
            then(nc.vector.tensor_reduce(wts[:, 1], route[:, 0], AX.X, ALU.max))
            then(tt(one, route[:, 0], over(wts[:, 1], NE), ALU.is_equal))
            then(nc.vector.scalar_tensor_tensor(out=route[:, 2], in0=one, scalar=-3e38, in1=logits,
                                                op0=ALU.mult, op1=ALU.add))
            then(nc.vector.tensor_reduce(wts[:, 3], route[:, 2], AX.X, ALU.max))
            then(tt(wts[:, 2], wts[:, 3], wts[:, 0], ALU.subtract))
            then(tt(route[:, 3], route[:, 2], over(wts[:, 3], NE), ALU.is_equal))
            then(tt(route[:, 3], route[:, 3], rank, ALU.mult))
            then(nc.vector.tensor_reduce(wts[:, 1], route[:, 3], AX.X, ALU.max))
            then(tt(two, route[:, 3], over(wts[:, 1], NE), ALU.is_equal))
            dve.wait_ge(r_exp, 1)
            then(nc.vector.tensor_scalar(wts[:, 4], wts[:, 2], 1.0, None, ALU.add))
            then(nc.vector.reciprocal(wts[:, 5], wts[:, 4]))
            then(nc.vector.tensor_scalar(wts[:, 6], wts[:, 5], 2.0, None, ALU.mult))
            then(tt(wts[:, 7], wts[:, 6], wts[:, 2], ALU.mult))
            then(tt(one, one, over(wts[:, 6], NE), ALU.mult))
            then(tt(two, two, over(wts[:, 7], NE), ALU.mult))
            then(tt(route[:, 5], one, two, ALU.add))

            nc.vector.tensor_tensor(lowm[:].rearrange("p t (e r) -> p t e r", r=R),
                                    gl[:, :, NE:].rearrange("p t (e r) -> p t e r", r=R),
                                    over(route[:, 5], R), ALU.mult).then_inc(l_low, 1)

            def layer3a(t, s):
                dve.wait_ge(h_sum, t + 1)
                stats(fo[:, s], 168 + 6 * s, 184 + 2 * s, h_stat, 2 * t)
                nc.vector.tensor_scalar(small[:, 180 + s:181 + s], small[:, 185 + 2 * s:186 + 2 * s], EPS, None,
                                        ALU.add).then_inc(h_ve, 1)

            def layer3b(u, s, first=False):
                dve.wait_ge(h_rstd, 2 * u + s + 1)
                if not first:
                    dve.wait_ge(d_out[s], 16 * u)
                nc.vector.tensor_scalar(fout[:, s], fo[:, s], small[:, 184 + 2 * s:185 + 2 * s],
                                        small[:, 182 + s:183 + s], ALU.subtract, ALU.mult).then_inc(h_out, 1)

            layer3a(0, 0)
            layer3a(1, 1)
            layer3b(0, 0, True)
            layer3a(2, 0)
            layer3b(0, 1, True)
            layer3a(3, 1)
            layer3b(1, 0)
            with dve.Fori(2, NT // 2) as u:
                layer3a(2 * u, 0)
                layer3b(u - 1, 1)
                layer3a(2 * u + 1, 1)
                layer3b(u, 0)
            layer3b(NT // 2 - 1, 1)

        @block.tensor
        def _(pe):
            mm = nc.tensor.matmul

            def product(dst, left, right):
                n = [(k, a, b) for k in range(KC) for a, b in PASSES]
                for at_, (k, a, b) in enumerate(n):
                    last = mm(dst, left(a, k), right(b, k), start=at_ == 0, stop=at_ == len(n) - 1)
                return last

            def turn(dst, src):
                return nc.tensor.transpose(dst, src, identf[:])

            pe.sem_inc(pts_free, 4)
            pe.sem_inc(tr_k, 1)
            pe.sem_inc(vw_mm, 1)
            pe.wait_ge(ctx_hi, 1)
            pe.wait_ge(kv_hi, 1)
            for i, (a, b) in enumerate(((0, 0), (1, 0), (0, 1))):
                if i == 1:
                    pe.wait_ge(ctx_lo, 1)
                elif i == 2:
                    pe.wait_ge(kv_lo, 1)
                for k in range(KC):
                    last = mm(ps[:, 0, :], ctxs[:, a, k, 0:P], kvs[:, 0, b, k, :],
                              start=i == 0 and k == 0, stop=i == 2 and k == KC - 1)
            last.then_inc(k_mm, 1)
            for n in range(2):
                pe.wait_ge(kv_lo, n + 1)
                for t in range(1 - n, 2):
                    product(ps[:, 2 * n + t, :], lambda a, k: ctxs[:, a, k, t * P:(t + 1) * P],
                            lambda b, k: kvs[:, n, b, k, :]).then_inc(k_mm, 1)
            for v in range(4):
                pe.wait_ge(kv_lo, 3 + v // 2)
                if v >= 2:
                    pe.wait_ge(v_done, v - 1)
                for g in range(2):
                    own = slice((2 * (v % 2) + g) * XD, (2 * (v % 2) + g + 1) * XD)
                    last = product(ps[:, 6 + v % 2, g * B * XS:(g + 1) * B * XS],
                                   lambda a, k: kvs[:, v // 2, a, k, own], lambda b, k: ctxs[:, b, k, :])
                last.then_inc(v_mm, 1)
            pe.wait_ge(d_const, 16 * NCONST)
            for u in range(4):
                pe.wait_ge(k_nat, u + 1)
                if u >= 2:
                    pe.wait_ge(k_done, u - 1)
                for g in range(4):
                    last = turn(ps[:, 4 + u % 2, g * P:(g + 1) * P], knat[:, u, g * XD:(g + 1) * XD])
                last.then_inc(k_tr, 1)

            pe.wait_ge(k_done, 4)
            with pe.Fori(0, NT // 2) as u:
                for s in range(2):
                    t = 2 * u + s
                    pe.wait_ge(x_lo, t + 1)
                    for n in range(3):
                        pe.wait_ge(w_lo, n + 1)
                        pe.wait_ge(qkv_free, 3 * t + n + 1)
                        product(ps[:, 3 * s + n, :], lambda a, k: xs[:, s, a, k, :],
                                lambda b, k: ws[:, b, n, k, :]).then_inc(qkv_mm, 1)

            def turn_att(t, s):
                pe.wait_ge(a_copy, t + 1)
                for k in range(KC):
                    last = turn(ps[:, 2 + s, k * P:(k + 1) * P], attc[:, s, k * P:(k + 1) * P])
                last.then_inc(a_tr, 1)

            def out_product(t, s):
                pe.wait_ge(a_lo, t + 1)
                product(ps[:, 4 + s, :], lambda a, k: aT[:, s, a, k, :], lambda b, k: wos[:, b, k, :]
                        ).then_inc(o_mm, 1)

            def turn_x1(t, s):
                pe.wait_ge(x1_done, t + 1)
                pe.wait_ge(x1_free, t + 1)
                for k in range(KC):
                    last = turn(ps[:, 6 + s, k * P:(k + 1) * P], x1c[:, s, k * P:(k + 1) * P])
                last.then_inc(x1_tr, 1)

            def turn_qk(i):
                pe.wait_ge(packed, 2 * i + 2)
                for a, done in ((0, tr_q), (1, tr_k)):
                    for p in range(2):
                        for c in range(2):
                            last = turn(ps[:, a, (2 * p + c) * P:(2 * p + c + 1) * P],
                                        pack[:, a, c, 2 * p:2 * p + 2, :].rearrange("p j d -> p (j d)"))
                    last.then_inc(done, 1)

            def scores(i, par, c):
                pe.wait_ge(qt_ready, i + 1)
                pe.wait_ge(kt_ready, i + 1)
                pe.wait_ge(s_free, 2 * i + c + 1)
                for j in range(4):
                    own = slice(64 * (j % 2), 64 * (j % 2) + 3 * D + 1)
                    mm(ps[:, 2 + 2 * c + j % 2, (j // 2) * SEQ:(j // 2 + 1) * SEQ],
                       qkt[own, par, 0, j // 2, c * P:(c + 1) * P], qkt[own, par, 1, j // 2, :], start=j < 2, stop=False)
                for r in range(2):
                    last = mm(heads(ps[:, 2 + 2 * c + r, :], 2)[:, :, c * P:(c + 1) * P], diagb[:],
                              causb[:].unsqueeze(1).broadcast_to([P, 2, P]), start=False, stop=True)
                last.then_inc(s_mm, 1)

            def turn_probs_pair(i, par, half, last_two=False):
                for j in (2 * half, 2 * half + 1):
                    if j == 0:
                        pe.wait_ge(s_exp, 2 * i + 2)
                    elif j == 1:
                        pe.wait_ge(qt_ready, NI if last_two else i + 3)
                    else:
                        pe.wait_ge(pt_sb, 4 * i + j - 1)
                    for kc in range(2):
                        for c in range(2):
                            last = turn(ps[:, pt_bank(j), (2 * kc + c) * P:(2 * kc + c + 1) * P],
                                        sb[:, par, c, j, kc * P:(kc + 1) * P])
                    last.then_inc(pt_mm, 1)

            def values(i, par, first=False):
                pe.wait_ge(v_ready, i + 2)
                if not first:
                    pe.wait_ge(o_norm, i)
                for j in range(4):
                    pe.wait_ge(pt_sb, 4 * i + j + 1)
                    for kc in range(2):
                        last = mm(ps[32 * j:32 * j + 2 * D, 7, 0:SEQ], vst[:, par, kc, j, :],
                                  pts[:, j, kc * SEQ:(kc + 1) * SEQ], start=kc == 0, stop=kc == 1)
                    last.then_inc(pts_free, 1)

            def turn_out(i):
                pe.wait_ge(ot_sb, i + 1)
                for c in range(2):
                    last = turn(ps[:, 7, SEQ + c * P:SEQ + (c + 1) * P], ot[:, c * P:(c + 1) * P])
                last.then_inc(ob_mm, 1)

            pe.wait_ge(qkv_free, 3 * NT + 3)
            turn_qk(0)
            pe.wait_ge(qkv_free, 3 * NT + 6)
            scores(0, 0, 0)
            scores(0, 0, 1)
            turn_qk(1)
            scores(1, 1, 0)

            def quad(i, par, out=True, more=True):
                if more:
                    turn_qk(i + 1)
                turn_probs_pair(i - 1, 1 - par, 0, not more)
                if out:
                    turn_out(i - 2)
                scores(i, par, 1)
                turn_probs_pair(i - 1, 1 - par, 1)
                if more:
                    scores(i + 1, 1 - par, 0)
                values(i - 1, 1 - par, not out)

            quad(1, 1, out=False)
            with pe.Fori(1, NI // 2 - 1) as u:
                for par in range(2):
                    quad(2 * u + par, par)
            quad(NI - 2, 0)
            quad(NI - 1, 1, more=False)
            turn_out(NI - 2)
            turn_att(0, 0)
            turn_att(1, 1)
            for half in range(2):
                turn_probs_pair(NI - 1, 1, half, True)
            values(NI - 1, 1)

            def queries(g, j, nh):
                pe.wait_ge(wq_lo, XR * g + j + 1)
                pe.wait_ge(q_free, 8 * g + 2 * j + nh + 1)
                product(ps[:, nh, :], lambda a, k: wqs[:, j, a, k, :],
                        lambda b, k: x1T[:, b, k, nh * 512:(nh + 1) * 512]).then_inc(q_mm, 1)

            pe.wait_ge(wo_lo, 1)
            out_product(0, 0)
            turn_out(NI - 1)
            with pe.Fori(1, NT // 2) as u:
                turn_att(2 * u, 0)
                out_product(2 * u - 1, 1)
                turn_x1(2 * u - 2, 0)
                turn_att(2 * u + 1, 1)
                out_product(2 * u, 0)
                turn_x1(2 * u - 1, 1)
            out_product(NT - 1, 1)
            turn_x1(NT - 2, 0)
            pe.wait_ge(x1_free, NT // 2 + 2)
            queries(0, 0, 0)
            turn_x1(NT - 1, 1)

            def norms_scores(g, j):
                h = XR * g + j
                pe.wait_ge(q_free, 8 * g + 2 * j + 4)
                pe.wait_ge(p_scaled, h)
                for b in range(B):
                    last = mm(ps[32 * b:32 * (b + 1), 3, 0:SEQ], ones[:], sq[:, j % 2, b * SEQ:(b + 1) * SEQ],
                              start=True, stop=True)
                last.then_inc(n_mm, 1)
                for t in range(NT):
                    last = mm(ps[:, 2, t * XS:(t + 1) * XS], qT[:, j % 2, t * P:(t + 1) * P],
                              KTx[:, g, t // 2 * XS:(t // 2 + 1) * XS], start=True, stop=True)
                last.then_inc(sx_mm, 1)
                pe.wait_ge(n_row, h + 1)
                for c in range(2):
                    last = turn(ps[:, 3, SEQ + c * P:SEQ + (c + 1) * P], nrow[:, c * P:(c + 1) * P])
                last.then_inc(n_tr, 1)

            def turn_probs(g, k):
                pe.wait_ge(p_norm, XR * g + 2 * (k // 2) + 2)
                pe.wait_ge(xt_lo, 4 * g + k + 1)
                if k == 0:
                    pe.wait_ge(y_add, 8 * g + 2)
                for q in range(4):
                    t = 4 * (k % 2) + q
                    last = turn(ps[:, 4, q * P:(q + 1) * P],
                                prob[:, k // 2, t].rearrange("p h k -> p (h k)"))
                last.then_inc(xt_mm, 1)

            def values_out(g, n):
                pe.wait_ge(z_lo, g + 1)
                pe.wait_ge(wx_lo, XR * g + n % 4 + 1)
                pe.wait_ge(vw_free, 8 * g + n + 1)
                for i, (a, w) in enumerate(PASSES):
                    last = mm(ps[:, 5 + n % 2, :], vsp[:, a, n // 4 * P:(n // 4 + 1) * P], wxs[:, n % 4, w, :],
                              start=i == 0, stop=i == 2)
                last.then_inc(vw_mm, 1)

            def outputs(g, b, c):
                pe.wait_ge(xt_lo, 4 * g + 5)
                pe.wait_ge(vw_free, 8 * g + 4 * (b // 2) + 6)
                pe.wait_ge(y_add, 8 * g + 2 * b + c + 1)
                n = [(p, a, w) for p in range(2) for a, w in PASSES]
                for i, (p, a, w) in enumerate(n):
                    last = mm(ps[:, y_bank(c), :], pT[:, a, p, 2 * b + c, :], vws(b)[:, w, p, :],
                              start=i == 0, stop=i == 5)
                last.then_inc(y_mm, 1)

            def group(g, one, two):
                for n in range(2):
                    if one and (n or two):
                        queries(g, 0, n)
                    if two:
                        turn_probs(g - 1, n)
                if one:
                    queries(g, 1, 0)
                    norms_scores(g, 0)
                if two:
                    values_out(g - 1, 0)
                    values_out(g - 1, 1)
                if one:
                    queries(g, 1, 1)
                if two:
                    turn_probs(g - 1, 2)
                    values_out(g - 1, 2)
                    values_out(g - 1, 3)
                    turn_probs(g - 1, 3)
                if one:
                    queries(g, 2, 0)
                    norms_scores(g, 1)
                if two:
                    outputs(g - 1, 0, 0)
                if one:
                    queries(g, 2, 1)
                if two:
                    outputs(g - 1, 0, 1)
                    values_out(g - 1, 4)
                    values_out(g - 1, 5)
                if one:
                    queries(g, 3, 0)
                if two:
                    outputs(g - 1, 1, 0)
                if one:
                    norms_scores(g, 2)
                if two:
                    values_out(g - 1, 6)
                    values_out(g - 1, 7)
                if one:
                    queries(g, 3, 1)
                if two:
                    outputs(g - 1, 1, 1)
                    outputs(g - 1, 2, 0)
                if one:
                    norms_scores(g, 3)
                if two:
                    outputs(g - 1, 2, 1)
                    outputs(g - 1, 3, 0)
                    outputs(g - 1, 3, 1)

            pe.wait_ge(x1_free, NT + 2)
            pe.wait_ge(consts_ready, 2)
            group(0, True, False)
            with pe.Fori(1, XG) as g:
                group(g, True, True)
            g = XG - 1
            turn_probs(g, 0)
            values_out(g, 0)
            turn_probs(g, 1)
            values_out(g, 1)
            values_out(g, 2)
            values_out(g, 3)
            turn_probs(g, 2)
            turn_probs(g, 3)
            values_out(g, 4)
            values_out(g, 5)
            outputs(g, 0, 0)
            values_out(g, 6)
            values_out(g, 7)
            for t in range(1, NT):
                outputs(g, t // 2, t % 2)

            def turn_x2(t, s):
                pe.wait_ge(f_x2, t + 1)
                for k in range(KC):
                    last = turn(ps[:, s, k * P:(k + 1) * P], x2c[:, s, k * P:(k + 1) * P])
                last.then_inc(f_tr, 1)

            def x2_of(t):
                return lambda a, k: x2T[:, a, k, t * P:(t + 1) * P]

            def gates(t):
                pe.wait_ge(f_lo, t + 1)
                pe.wait_ge(g_sb, t + 1)
                product(ps[:, 2 + t % 2, 0:NE + P], x2_of(t), lambda b, k: gas[:, b, k, :]).then_inc(g_mm, 1)

            def base(t):
                n = [(k, a, b) for k in range(KC) for a, b in PASSES]
                for i, (k, a, b) in enumerate(n):
                    mm(ps[:, f_bank(t), :], x2_of(t)(a, k), bases[:, b, k, :], start=i == 0, stop=False)

            def residual(t):
                pe.wait_ge(f_bias, t + 1)
                mm(ps[:, f_bank(t), :], identf[:], yacc[:, t], start=False, stop=False)

            def lora(t):
                pe.wait_ge(l_sb, t // 4 + 1)
                mm(ps[:, f_bank(t), :], lowT[:, t], lbs[:], start=False, stop=True).then_inc(l_mm, 1)

            turn_x2(0, 0)
            turn_x2(1, 1)
            pe.wait_ge(b_lo, 1)
            for t in range(NT):
                gates(t)
                if t < NT - 2:
                    turn_x2(t + 2, t % 2)
                if t == 1:
                    pe.wait_ge(b_lo, 2)
                if 1 <= t <= 4:
                    base(t - 1)
            for t in (4, 5):
                base(t)
                residual(t)
            for t in range(4):
                residual(t)
            pe.wait_ge(l_low, 1)
            pe.wait_ge(g_sb, NT + 2)
            for n in range(2):
                for t in range(4):
                    last = turn(ps[:, 2 + n, t * P:(t + 1) * P], lowm[:, 4 * n + t])
                last.then_inc(l_tr, 1)
            pe.wait_ge(d_f, 64)
            for t in range(6):
                lora(t)
            for t in range(6, NT):
                base(t)
                residual(t)
                lora(t)


def tables(np):
    half = D // 2
    freq = (1.0 / np.float32(10000.0) ** (np.arange(half, dtype=np.float32) / np.float32(half))).astype(np.float32)
    ang = np.arange(SEQ, dtype=np.float32)[:, None] * freq[None, :]
    cos, sin = np.cos(ang), np.sin(ang)
    rope = np.stack([np.concatenate([cos, cos], -1), np.concatenate([-sin, sin], -1)], 1)
    rope = rope.reshape(2, P, 2, D).transpose(1, 0, 2, 3)
    causal = MASK_B * (np.arange(P)[None, :] > np.arange(P)[:, None])
    return {"rope": rope, "ident": np.eye(P), "causal": causal, "order": np.arange(NE, 0, -1)}


def kernel(x, ctx_4096, mask_1x1xSxS2_ff0, L0_attn_qkv_w, L0_attn_qkv_b, L0_attn_out_w, L0_attn_out_b,
           L0_xattn_q_proj_w, L0_xattn_k_proj_w, L0_xattn_v_proj_w, L0_xattn_o_proj_w, L0_xattn_q_norm_w,
           L0_xattn_k_norm_w, L0_ffn_gate_w, L0_ffn_base_w, L0_ffn_base_b, L0_ffn_lora_A, L0_ffn_lora_B):
    import numpy as np
    import concourse.bacc as bacc
    from concourse.bass_utils import run_bass_kernel_spmd

    def chunks(w):
        return np.asarray(w).reshape(w.shape[0], -1, P).transpose(2, 1, 0)

    kw = np.asarray(L0_xattn_k_proj_w).reshape(2, 512, KC, P).transpose(0, 3, 2, 1)
    vw = np.asarray(L0_xattn_v_proj_w).reshape(2, 512, KC, P).transpose(0, 3, 2, 1)
    a = {
        "xT": np.asarray(x).reshape(NT, P, KC, P).transpose(0, 3, 2, 1),
        "x": np.asarray(x).reshape(NT, P, E),
        "ctxT": chunks(np.asarray(ctx_4096).reshape(B * XS, E)),
        "mask": np.asarray(mask_1x1xSxS2_ff0).reshape(SEQ, XS),
        "wqkv": L0_attn_qkv_w, "qkvb": L0_attn_qkv_b, "wout": L0_attn_out_w, "outb": L0_attn_out_b,
        "wqT": np.asarray(L0_xattn_q_proj_w).reshape(XH, XD, KC, P).transpose(0, 3, 2, 1),
        "wkT": kw, "wvT": vw,
        "woT": np.asarray(L0_xattn_o_proj_w).reshape(E, XH, XD).transpose(1, 2, 0),
        "qn": np.asarray(L0_xattn_q_norm_w).reshape(P, 1), "kn": np.asarray(L0_xattn_k_norm_w).reshape(P, 1),
        "gateT": chunks(L0_ffn_gate_w), "baseT": chunks(L0_ffn_base_w), "baseb": L0_ffn_base_b,
        "loraAT": chunks(np.asarray(L0_ffn_lora_A).reshape(NE * R, E)),
        "loraB": np.asarray(L0_ffn_lora_B).transpose(0, 2, 1).reshape(NE * R, E),
    }
    for name, table in tables(np).items():
        a[name] = np.asarray(table, np.float32)
    nc = bacc.Bacc("TRN2", target_bir_lowering=False, num_devices=1)
    arrays, aps = {}, {}
    for name, v in a.items():
        v = np.ascontiguousarray(v)
        arrays[f"in_{name}"] = v
        aps[name] = nc.dram_tensor(f"in_{name}", v.shape, mybir.dt.from_np(v.dtype), kind="ExternalInput").ap()
    aps["out"] = nc.dram_tensor("out_y", (NT, P, E), F32, kind="ExternalOutput").ap()
    decoder_layer(nc, **aps)
    r = run_bass_kernel_spmd(nc, [arrays], core_ids=[0])
    return r.results[0]["out_y"].reshape(B, SEQ, E)
```
